# Optimizing a Trainium2 kernel written in Bass

```python
import numpy as np
import jax
import jax.numpy as jnp

def _softmax(x, axis=-1):
    return jax.nn.softmax(x, axis=axis)

def _gelu(x):
    return jax.nn.gelu(x, approximate=True)

def _silu(x):
    return jax.nn.silu(x)

def _sigmoid(x):
    return jax.nn.sigmoid(x)

def _layernorm(x, axis=-1, eps=1e-05):
    m = jnp.mean(x, axis=axis, keepdims=True)
    v = jnp.var(x, axis=axis, keepdims=True)
    return (x - m) / jnp.sqrt(v + eps)

def _scatter_add(tgt, idx, src, axis=0):
    return tgt.at[idx].add(src)

def _segment_sum(src, seg, n):
    return jax.ops.segment_sum(src, seg, n)
kernel_name = 'mk_prb_d2_jaxref_r8_d1cbe7'

def setup_inputs(seed: int=0):
    np.random.seed(seed)
    _w = jnp.asarray

    def _L0_attn_setup():
        import jax, jax.numpy as jnp
        import numpy as np
        MAX_LR = 0.01
        NS_A, NS_B, NS_C = (3.4445, -4.775, 2.0315)

        def newtonschulz5(G, steps=5, eps=1e-07):
            transpose = G.shape[-2] > G.shape[-1]
            X = jnp.swapaxes(G, -2, -1) if transpose else G
            X = X / (jnp.linalg.norm(X, axis=(-2, -1), keepdims=True) + eps)
            for _ in range(steps):
                A = X @ jnp.swapaxes(X, -2, -1)
                Bm = NS_B * A + NS_C * (A @ A)
                X = NS_A * X + Bm @ X
            return jnp.swapaxes(X, -2, -1) if transpose else X

        def _reference_tuple_inner(tokens, wq, wk, wv, wo, w_lr, w_target, w_gates, rms_w):
            N = tokens.shape[1]
            scale = wq.shape[-1] ** (-0.5)
            eps = jnp.finfo(tokens.dtype).eps
            t = tokens * jax.lax.rsqrt(jnp.mean(tokens * tokens, -1, keepdims=True) + eps) * rms_w
            gates = jnp.swapaxes(jax.nn.sigmoid(t @ w_gates), -2, -1)[..., None]
            q = jnp.einsum('bnd,hde->bhne', t, wq)
            k = jnp.einsum('bnd,hde->bhne', t, wk)
            v = jnp.einsum('bnd,hde->bhne', t, wv)
            score = jnp.einsum('bhie,bhje->bhij', q, k) * scale
            causal_mask = jnp.triu(jnp.ones((N, N), bool), 1)
            score = jnp.where(causal_mask, -jnp.finfo(score.dtype).max, score)
            attn = jax.nn.softmax(score, axis=-1)
            out = jnp.einsum('bhij,bhje->bhie', attn, v) * gates
            pred_values = jnp.einsum('bhne,hed->bnd', out, wo)
            tv = t[:, 1:] @ w_target
            tv = (tv - tv.mean(-1, keepdims=True)) * jax.lax.rsqrt(tv.var(-1, keepdims=True) + 1e-05)
            ts = t[:, :-1]
            pv = pred_values[:, :-1]
            o = out[:, :, :-1]
            g = gates[:, :, :-1]
            a = attn[:, :, :-1, :-1]
            qs, ks_, vs = (q[:, :, :-1], k[:, :, :-1], v[:, :, :-1])
            lrs = jax.nn.sigmoid(ts @ w_lr) * MAX_LR
            lr, mlr = (lrs[..., 0], lrs[..., 1])
            error = tv - pv
            dout = jnp.einsum('bnd,hed->bhne', error, wo)
            du = dout * g
            delta = jnp.sum(dout * o, -1, keepdims=True)
            dv = jnp.einsum('bhij,bhie->bhje', a, du)
            dattn = jnp.einsum('bhje,bhie->bhij', vs, du)
            dscore = scale * a * (dattn - delta)
            dq = jnp.einsum('bhje,bhij->bhie', ks_, dscore)
            dk = jnp.einsum('bhie,bhij->bhje', qs, dscore)
            t_qk = ts * lr[..., None]
            t_v = ts * mlr[..., None]
            o_wo = o * mlr[:, None, :, None]
            dwq = jnp.einsum('bhie,bid->bhde', dq, t_qk)
            dwk = jnp.einsum('bhje,bjd->bhde', dk, t_qk)
            dwv = jnp.einsum('bhje,bjd->bhde', dv, t_v)
            dwo = jnp.einsum('bnd,bhne->bhed', error, o_wo)
            dwv = newtonschulz5(dwv)
            dwo = newtonschulz5(dwo)
            return (pred_values, dwq, dwk, dwv, dwo)
        key = jax.random.key(seed)
        ks = jax.random.split(key, 9)
        B, N, D, H, DH = (4, 128, 128, 8, 64)
        s = D ** (-0.5)
        return {'tokens': jax.random.normal(ks[0], (B, N, D), jnp.float32), 'wq': jax.random.normal(ks[1], (H, D, DH), jnp.float32) * s, 'wk': jax.random.normal(ks[2], (H, D, DH), jnp.float32) * s, 'wv': jax.random.normal(ks[3], (H, D, DH), jnp.float32) * s, 'wo': jax.random.normal(ks[4], (H, DH, D), jnp.float32) * s, 'w_lr': jax.random.normal(ks[5], (D, 2), jnp.float32) * 0.02, 'w_target': jax.random.normal(ks[6], (D, D), jnp.float32) * 0.02, 'w_gates': jax.random.normal(ks[7], (D, H), jnp.float32) * 0.02, 'rms_w': jnp.ones((D,), jnp.float32)}
    _L0_attn_in = _L0_attn_setup()

    def _L0_ffn_setup():
        import jax, jax.numpy as jnp
        import numpy as np
        DIM = 128
        INTER = 64
        E = 16
        TOPK = 4
        N_GROUPS = 4
        TOPK_GROUPS = 2
        ROUTE_SCALE = 1.0
        INIT_STD = 0.02
        B, S = (2, 128)
        key = jax.random.key(seed)
        ks = jax.random.split(key, 8)
        return {'x': jax.random.normal(ks[0], (B, S, DIM), jnp.float32), 'gate_w': jax.random.normal(ks[1], (E, DIM), jnp.float32) * INIT_STD, 'gate_bias': jnp.zeros((E,), jnp.float32), 'w1': jax.random.normal(ks[2], (E, INTER, DIM), jnp.float32) * INIT_STD, 'w2': jax.random.normal(ks[3], (E, DIM, INTER), jnp.float32) * INIT_STD, 'w3': jax.random.normal(ks[4], (E, INTER, DIM), jnp.float32) * INIT_STD, 'ws1': jax.random.normal(ks[5], (INTER, DIM), jnp.float32) * INIT_STD, 'ws2': jax.random.normal(ks[6], (DIM, INTER), jnp.float32) * INIT_STD, 'ws3': jax.random.normal(ks[7], (INTER, DIM), jnp.float32) * INIT_STD}
    _L0_ffn_in = _L0_ffn_setup()

    def _L1_attn_setup():
        import math
        import jax, jax.numpy as jnp
        import numpy as np
        N_HEADS = 16
        CHUNK = 64

        def _chunked_causal_attention(q, k, v, chunk=CHUNK):
            B, H, S, D = q.shape
            scale = 1.0 / math.sqrt(D)
            nc = S // chunk
            qc = jnp.moveaxis(q.reshape(B, H, nc, chunk, D), 2, 0)
            kpos = jnp.arange(S)

            def body(_, inp):
                qi, ci = inp
                scores = jnp.einsum('bhcd,bhsd->bhcs', qi, k) * scale
                qpos = ci * chunk + jnp.arange(chunk)
                mask = kpos[None, :] <= qpos[:, None]
                scores = jnp.where(mask, scores, jnp.finfo(scores.dtype).min)
                p = jax.nn.softmax(scores, axis=-1)
                return (None, jnp.einsum('bhcs,bhsd->bhcd', p, v))
            _, outs = jax.lax.scan(body, None, (qc, jnp.arange(nc)))
            return jnp.moveaxis(outs, 0, 2).reshape(B, H, S, D)
        key = jax.random.key(seed)
        kx, kq, kk, kv, ko = jax.random.split(key, 5)
        d = 128
        x = jax.random.normal(kx, (1, 512, d), dtype=jnp.float32)
        Wq = jax.random.normal(kq, (d, d), dtype=jnp.float32) * 0.02
        Wk = jax.random.normal(kk, (d, d), dtype=jnp.float32) * 0.02
        Wv = jax.random.normal(kv, (d, d), dtype=jnp.float32) * 0.02
        Wo = jax.random.normal(ko, (d, d), dtype=jnp.float32) * 0.02
        return {'x': x, 'Wq': Wq, 'Wk': Wk, 'Wv': Wv, 'Wo': Wo}
    _L1_attn_in = _L1_attn_setup()

    def _L1_ffn_setup():
        import jax, jax.numpy as jnp
        import numpy as np
        DIM = 128
        DEPTH = 6
        HEADS = 16
        DIM_HEAD = 64
        WINDOW = 32
        INNER = HEADS * DIM_HEAD
        DIM_INNER = int(DIM * 4 * 2 / 3)
        QK_SCALE = 8.0

        def shift_tokens(t):
            a, s = jnp.split(t, 2, -1)
            s = jnp.pad(s, ((0, 0), (1, 0), (0, 0)))[:, :-1]
            return jnp.concatenate([a, s], -1)

        def l2norm(t):
            return t / jnp.maximum(jnp.linalg.norm(t, axis=-1, keepdims=True), 1e-12)

        def rotate_half(x):
            x1, x2 = jnp.split(x, 2, -1)
            return jnp.concatenate([-x2, x1], -1)

        def rotary_tables(n):
            half = jnp.arange(0, DIM_HEAD, 2, dtype=jnp.float32)
            inv_freq = 1.0 / 10000.0 ** (half / DIM_HEAD)
            t = jnp.arange(n, dtype=jnp.float32)
            freqs = t[:, None] * inv_freq[None, :]
            freqs = jnp.concatenate([freqs, freqs], -1)
            base_scale = (half + 0.4 * DIM_HEAD) / (1.4 * DIM_HEAD)
            power = (t - n // 2) / (WINDOW // 2)
            scale = base_scale[None, :] ** power[:, None]
            scale = jnp.concatenate([scale, scale], -1)
            return (freqs, scale)

        def local_attention(q, k, v):
            b, h, n, d = q.shape
            w = WINDOW
            nw = n // w
            bq = q.reshape(b, h, nw, w, d)
            bk = k.reshape(b, h, nw, w, d)
            bv = v.reshape(b, h, nw, w, d)

            def look(t):
                p = jnp.pad(t, ((0, 0), (0, 0), (1, 0), (0, 0), (0, 0)))
                return jnp.concatenate([p[:, :, :nw], p[:, :, 1:]], axis=3)
            bk2, bv2 = (look(bk), look(bv))
            seq = jnp.arange(n).reshape(nw, w)
            seq_p = jnp.pad(seq, ((1, 0), (0, 0)), constant_values=-1)
            jt = jnp.concatenate([seq_p[:nw], seq_p[1:]], axis=1)
            it = seq[:, :, None]
            jb = jt[:, None, :]
            mask = (it < jb) | (it > jb + w) | (jb == -1)
            sim = jnp.einsum('bhwie,bhwje->bhwij', bq, bk2) * QK_SCALE
            sim = jnp.where(mask, -jnp.finfo(sim.dtype).max, sim)
            attn = jax.nn.softmax(sim, -1)
            out = jnp.einsum('bhwij,bhwje->bhwie', attn, bv2)
            return out.reshape(b, h, n, d)

        def attn_layer(x, Wqkv, qs, ksc, Wo):
            b, n, _ = x.shape
            qkv = x @ Wqkv
            q, k, v = jnp.split(qkv, 3, -1)
            sh = lambda t: t.reshape(b, n, HEADS, DIM_HEAD).transpose(0, 2, 1, 3)
            q, k, v = (sh(q), sh(k), sh(v))
            q = l2norm(q) * qs
            k = l2norm(k) * ksc
            freqs, scale = rotary_tables(n)
            cos, sin = (jnp.cos(freqs), jnp.sin(freqs))
            q = q * cos * scale + rotate_half(q) * sin * scale
            inv = 1.0 / scale
            k = k * cos * inv + rotate_half(k) * sin * inv
            out = local_attention(q, k, v)
            out = out.transpose(0, 2, 1, 3).reshape(b, n, INNER)
            return out @ Wo

        def ffn_layer(x, g, bln, W1, b1, W2, b2):
            mu = x.mean(-1, keepdims=True)
            var = ((x - mu) ** 2).mean(-1, keepdims=True)
            xn = (x - mu) / jnp.sqrt(var + 1e-05) * g + bln
            hg = xn @ W1 + b1
            a, gate = jnp.split(hg, 2, -1)
            return a * jax.nn.gelu(gate, approximate=False) @ W2 + b2
        key = jax.random.key(seed)
        ks = jax.random.split(key, 8)
        B, N = (2, 256)
        init = lambda k, shape: jax.random.normal(k, shape, jnp.float32) * 0.02
        return {'x': jax.random.normal(ks[0], (B, N, DIM), jnp.float32), 'Wqkv': init(ks[1], (DEPTH, DIM, 3 * INNER)), 'q_scale': jnp.ones((DEPTH, DIM_HEAD), jnp.float32), 'k_scale': jnp.ones((DEPTH, DIM_HEAD), jnp.float32), 'Wo': init(ks[2], (DEPTH, INNER, DIM)), 'ln_g': jnp.ones((DEPTH, DIM), jnp.float32), 'ln_b': jnp.zeros((DEPTH, DIM), jnp.float32), 'W1': init(ks[3], (DEPTH, DIM, 2 * DIM_INNER)), 'b1': jnp.zeros((DEPTH, 2 * DIM_INNER), jnp.float32), 'W2': init(ks[4], (DEPTH, DIM_INNER, DIM)), 'b2': jnp.zeros((DEPTH, DIM), jnp.float32)}
    _L1_ffn_in = _L1_ffn_setup()
    _d = {'L0_attn_tokens': _L0_attn_in['tokens'], 'L0_attn_wq': _L0_attn_in['wq'], 'L0_attn_wk': _L0_attn_in['wk'], 'L0_attn_wv': _L0_attn_in['wv'], 'L0_attn_wo': _L0_attn_in['wo'], 'L0_attn_w_lr': _L0_attn_in['w_lr'], 'L0_attn_w_target': _L0_attn_in['w_target'], 'L0_attn_w_gates': _L0_attn_in['w_gates'], 'L0_attn_rms_w': _L0_attn_in['rms_w'], 'L0_ffn_gate_w': _L0_ffn_in['gate_w'], 'L0_ffn_gate_bias': _L0_ffn_in['gate_bias'], 'L0_ffn_w1': _L0_ffn_in['w1'], 'L0_ffn_w2': _L0_ffn_in['w2'], 'L0_ffn_w3': _L0_ffn_in['w3'], 'L0_ffn_ws1': _L0_ffn_in['ws1'], 'L0_ffn_ws2': _L0_ffn_in['ws2'], 'L0_ffn_ws3': _L0_ffn_in['ws3'], 'L1_attn_Wq': _L1_attn_in['Wq'], 'L1_attn_Wk': _L1_attn_in['Wk'], 'L1_attn_Wv': _L1_attn_in['Wv'], 'L1_attn_Wo': _L1_attn_in['Wo'], 'L1_ffn_Wqkv': _L1_ffn_in['Wqkv'], 'L1_ffn_q_scale': _L1_ffn_in['q_scale'], 'L1_ffn_k_scale': _L1_ffn_in['k_scale'], 'L1_ffn_Wo': _L1_ffn_in['Wo'], 'L1_ffn_ln_g': _L1_ffn_in['ln_g'], 'L1_ffn_ln_b': _L1_ffn_in['ln_b'], 'L1_ffn_W1': _L1_ffn_in['W1'], 'L1_ffn_b1': _L1_ffn_in['b1'], 'L1_ffn_W2': _L1_ffn_in['W2'], 'L1_ffn_b2': _L1_ffn_in['b2']}
    _x0 = _d['L0_attn_tokens']
    _d['L0_attn_tokens'] = jax.random.normal(jax.random.fold_in(jax.random.key(seed), 1), (8, 512, 128), dtype=_x0.dtype)
    del _x0
    return _d

def reference(L0_attn_tokens, L0_attn_wq, L0_attn_wk, L0_attn_wv, L0_attn_wo, L0_attn_w_lr, L0_attn_w_target, L0_attn_w_gates, L0_attn_rms_w, L0_ffn_gate_w, L0_ffn_gate_bias, L0_ffn_w1, L0_ffn_w2, L0_ffn_w3, L0_ffn_ws1, L0_ffn_ws2, L0_ffn_ws3, L1_attn_Wq, L1_attn_Wk, L1_attn_Wv, L1_attn_Wo, L1_ffn_Wqkv, L1_ffn_q_scale, L1_ffn_k_scale, L1_ffn_Wo, L1_ffn_ln_g, L1_ffn_ln_b, L1_ffn_W1, L1_ffn_b1, L1_ffn_W2, L1_ffn_b2):

    def _L0_attn_ref(tokens, wq, wk, wv, wo, w_lr, w_target, w_gates, rms_w):
        import jax, jax.numpy as jnp
        import numpy as np
        MAX_LR = 0.01
        NS_A, NS_B, NS_C = (3.4445, -4.775, 2.0315)

        def newtonschulz5(G, steps=5, eps=1e-07):
            transpose = G.shape[-2] > G.shape[-1]
            X = jnp.swapaxes(G, -2, -1) if transpose else G
            X = X / (jnp.linalg.norm(X, axis=(-2, -1), keepdims=True) + eps)
            for _ in range(steps):
                A = X @ jnp.swapaxes(X, -2, -1)
                Bm = NS_B * A + NS_C * (A @ A)
                X = NS_A * X + Bm @ X
            return jnp.swapaxes(X, -2, -1) if transpose else X

        def _reference_tuple_inner(tokens, wq, wk, wv, wo, w_lr, w_target, w_gates, rms_w):
            N = tokens.shape[1]
            scale = wq.shape[-1] ** (-0.5)
            eps = jnp.finfo(tokens.dtype).eps
            t = tokens * jax.lax.rsqrt(jnp.mean(tokens * tokens, -1, keepdims=True) + eps) * rms_w
            gates = jnp.swapaxes(jax.nn.sigmoid(t @ w_gates), -2, -1)[..., None]
            q = jnp.einsum('bnd,hde->bhne', t, wq)
            k = jnp.einsum('bnd,hde->bhne', t, wk)
            v = jnp.einsum('bnd,hde->bhne', t, wv)
            score = jnp.einsum('bhie,bhje->bhij', q, k) * scale
            causal_mask = jnp.triu(jnp.ones((N, N), bool), 1)
            score = jnp.where(causal_mask, -jnp.finfo(score.dtype).max, score)
            attn = jax.nn.softmax(score, axis=-1)
            out = jnp.einsum('bhij,bhje->bhie', attn, v) * gates
            pred_values = jnp.einsum('bhne,hed->bnd', out, wo)
            tv = t[:, 1:] @ w_target
            tv = (tv - tv.mean(-1, keepdims=True)) * jax.lax.rsqrt(tv.var(-1, keepdims=True) + 1e-05)
            ts = t[:, :-1]
            pv = pred_values[:, :-1]
            o = out[:, :, :-1]
            g = gates[:, :, :-1]
            a = attn[:, :, :-1, :-1]
            qs, ks_, vs = (q[:, :, :-1], k[:, :, :-1], v[:, :, :-1])
            lrs = jax.nn.sigmoid(ts @ w_lr) * MAX_LR
            lr, mlr = (lrs[..., 0], lrs[..., 1])
            error = tv - pv
            dout = jnp.einsum('bnd,hed->bhne', error, wo)
            du = dout * g
            delta = jnp.sum(dout * o, -1, keepdims=True)
            dv = jnp.einsum('bhij,bhie->bhje', a, du)
            dattn = jnp.einsum('bhje,bhie->bhij', vs, du)
            dscore = scale * a * (dattn - delta)
            dq = jnp.einsum('bhje,bhij->bhie', ks_, dscore)
            dk = jnp.einsum('bhie,bhij->bhje', qs, dscore)
            t_qk = ts * lr[..., None]
            t_v = ts * mlr[..., None]
            o_wo = o * mlr[:, None, :, None]
            dwq = jnp.einsum('bhie,bid->bhde', dq, t_qk)
            dwk = jnp.einsum('bhje,bjd->bhde', dk, t_qk)
            dwv = jnp.einsum('bhje,bjd->bhde', dv, t_v)
            dwo = jnp.einsum('bnd,bhne->bhed', error, o_wo)
            dwv = newtonschulz5(dwv)
            dwo = newtonschulz5(dwo)
            return (pred_values, dwq, dwk, dwv, dwo)
        return _reference_tuple_inner(tokens, wq, wk, wv, wo, w_lr, w_target, w_gates, rms_w)[0]

    def _L0_ffn_ref(x, gate_w, gate_bias, w1, w2, w3, ws1, ws2, ws3):
        import jax, jax.numpy as jnp
        import numpy as np
        DIM = 128
        INTER = 64
        E = 16
        TOPK = 4
        N_GROUPS = 4
        TOPK_GROUPS = 2
        ROUTE_SCALE = 1.0
        INIT_STD = 0.02
        B, S = (2, 128)
        Bx, Sx, D = x.shape
        T = Bx * Sx
        xf = x.reshape(T, D)
        scores = jax.nn.sigmoid(xf @ gate_w.T)
        original_scores = scores
        s = scores + gate_bias
        sg = s.reshape(T, N_GROUPS, E // N_GROUPS)
        group_scores = sg.max(axis=-1)
        _, gidx = jax.lax.top_k(group_scores, TOPK_GROUPS)
        keep = jnp.zeros((T, N_GROUPS), bool).at[jnp.arange(T)[:, None], gidx].set(True)
        s_masked = jnp.where(keep[:, :, None], sg, -jnp.inf).reshape(T, E)
        _, idx = jax.lax.top_k(s_masked, TOPK)
        weights = jnp.take_along_axis(original_scores, idx, axis=1) * ROUTE_SCALE
        comb = jnp.zeros((T, E), x.dtype).at[jnp.arange(T)[:, None], idx].add(weights)
        h1 = jnp.einsum('td,eid->tei', xf, w1)
        h3 = jnp.einsum('td,eid->tei', xf, w3)
        h = jax.nn.silu(h1) * h3
        y = jnp.einsum('tei,edi,te->td', h, w2, comb)
        z = jax.nn.silu(xf @ ws1.T) * (xf @ ws3.T) @ ws2.T
        return (y + z).reshape(Bx, Sx, D)

    def _L1_attn_ref(x, Wq, Wk, Wv, Wo):
        import math
        import jax, jax.numpy as jnp
        import numpy as np
        N_HEADS = 16
        CHUNK = 64

        def _chunked_causal_attention(q, k, v, chunk=CHUNK):
            B, H, S, D = q.shape
            scale = 1.0 / math.sqrt(D)
            nc = S // chunk
            qc = jnp.moveaxis(q.reshape(B, H, nc, chunk, D), 2, 0)
            kpos = jnp.arange(S)

            def body(_, inp):
                qi, ci = inp
                scores = jnp.einsum('bhcd,bhsd->bhcs', qi, k) * scale
                qpos = ci * chunk + jnp.arange(chunk)
                mask = kpos[None, :] <= qpos[:, None]
                scores = jnp.where(mask, scores, jnp.finfo(scores.dtype).min)
                p = jax.nn.softmax(scores, axis=-1)
                return (None, jnp.einsum('bhcs,bhsd->bhcd', p, v))
            _, outs = jax.lax.scan(body, None, (qc, jnp.arange(nc)))
            return jnp.moveaxis(outs, 0, 2).reshape(B, H, S, D)
        B, S, D = x.shape
        H = N_HEADS
        hd = D // H
        q = (x @ Wq.T).reshape(B, S, H, hd).transpose(0, 2, 1, 3)
        k = (x @ Wk.T).reshape(B, S, H, hd).transpose(0, 2, 1, 3)
        v = (x @ Wv.T).reshape(B, S, H, hd).transpose(0, 2, 1, 3)
        out = _chunked_causal_attention(q, k, v)
        out = out.transpose(0, 2, 1, 3).reshape(B, S, D)
        return out @ Wo.T

    def _L1_ffn_ref(x, Wqkv, q_scale, k_scale, Wo, ln_g, ln_b, W1, b1, W2, b2):
        import jax, jax.numpy as jnp
        import numpy as np
        DIM = 128
        DEPTH = 6
        HEADS = 16
        DIM_HEAD = 64
        WINDOW = 32
        INNER = HEADS * DIM_HEAD
        DIM_INNER = int(DIM * 4 * 2 / 3)
        QK_SCALE = 8.0

        def shift_tokens(t):
            a, s = jnp.split(t, 2, -1)
            s = jnp.pad(s, ((0, 0), (1, 0), (0, 0)))[:, :-1]
            return jnp.concatenate([a, s], -1)

        def l2norm(t):
            return t / jnp.maximum(jnp.linalg.norm(t, axis=-1, keepdims=True), 1e-12)

        def rotate_half(x):
            x1, x2 = jnp.split(x, 2, -1)
            return jnp.concatenate([-x2, x1], -1)

        def rotary_tables(n):
            half = jnp.arange(0, DIM_HEAD, 2, dtype=jnp.float32)
            inv_freq = 1.0 / 10000.0 ** (half / DIM_HEAD)
            t = jnp.arange(n, dtype=jnp.float32)
            freqs = t[:, None] * inv_freq[None, :]
            freqs = jnp.concatenate([freqs, freqs], -1)
            base_scale = (half + 0.4 * DIM_HEAD) / (1.4 * DIM_HEAD)
            power = (t - n // 2) / (WINDOW // 2)
            scale = base_scale[None, :] ** power[:, None]
            scale = jnp.concatenate([scale, scale], -1)
            return (freqs, scale)

        def local_attention(q, k, v):
            b, h, n, d = q.shape
            w = WINDOW
            nw = n // w
            bq = q.reshape(b, h, nw, w, d)
            bk = k.reshape(b, h, nw, w, d)
            bv = v.reshape(b, h, nw, w, d)

            def look(t):
                p = jnp.pad(t, ((0, 0), (0, 0), (1, 0), (0, 0), (0, 0)))
                return jnp.concatenate([p[:, :, :nw], p[:, :, 1:]], axis=3)
            bk2, bv2 = (look(bk), look(bv))
            seq = jnp.arange(n).reshape(nw, w)
            seq_p = jnp.pad(seq, ((1, 0), (0, 0)), constant_values=-1)
            jt = jnp.concatenate([seq_p[:nw], seq_p[1:]], axis=1)
            it = seq[:, :, None]
            jb = jt[:, None, :]
            mask = (it < jb) | (it > jb + w) | (jb == -1)
            sim = jnp.einsum('bhwie,bhwje->bhwij', bq, bk2) * QK_SCALE
            sim = jnp.where(mask, -jnp.finfo(sim.dtype).max, sim)
            attn = jax.nn.softmax(sim, -1)
            out = jnp.einsum('bhwij,bhwje->bhwie', attn, bv2)
            return out.reshape(b, h, n, d)

        def attn_layer(x, Wqkv, qs, ksc, Wo):
            b, n, _ = x.shape
            qkv = x @ Wqkv
            q, k, v = jnp.split(qkv, 3, -1)
            sh = lambda t: t.reshape(b, n, HEADS, DIM_HEAD).transpose(0, 2, 1, 3)
            q, k, v = (sh(q), sh(k), sh(v))
            q = l2norm(q) * qs
            k = l2norm(k) * ksc
            freqs, scale = rotary_tables(n)
            cos, sin = (jnp.cos(freqs), jnp.sin(freqs))
            q = q * cos * scale + rotate_half(q) * sin * scale
            inv = 1.0 / scale
            k = k * cos * inv + rotate_half(k) * sin * inv
            out = local_attention(q, k, v)
            out = out.transpose(0, 2, 1, 3).reshape(b, n, INNER)
            return out @ Wo

        def ffn_layer(x, g, bln, W1, b1, W2, b2):
            mu = x.mean(-1, keepdims=True)
            var = ((x - mu) ** 2).mean(-1, keepdims=True)
            xn = (x - mu) / jnp.sqrt(var + 1e-05) * g + bln
            hg = xn @ W1 + b1
            a, gate = jnp.split(hg, 2, -1)
            return a * jax.nn.gelu(gate, approximate=False) @ W2 + b2
        for i in range(DEPTH):
            x = attn_layer(shift_tokens(x), Wqkv[i], q_scale[i], k_scale[i], Wo[i]) + x
            x = ffn_layer(shift_tokens(x), ln_g[i], ln_b[i], W1[i], b1[i], W2[i], b2[i]) + x
        return x
    x = L0_attn_tokens
    xn = _layernorm(x, axis=-1)
    x = x + _L0_attn_ref(xn, L0_attn_wq, L0_attn_wk, L0_attn_wv, L0_attn_wo, L0_attn_w_lr, L0_attn_w_target, L0_attn_w_gates, L0_attn_rms_w) + _L0_ffn_ref(xn, L0_ffn_gate_w, L0_ffn_gate_bias, L0_ffn_w1, L0_ffn_w2, L0_ffn_w3, L0_ffn_ws1, L0_ffn_ws2, L0_ffn_ws3)
    xn = _layernorm(x, axis=-1)
    x = x + _L1_attn_ref(xn, L1_attn_Wq, L1_attn_Wk, L1_attn_Wv, L1_attn_Wo) + _L1_ffn_ref(xn, L1_ffn_Wqkv, L1_ffn_q_scale, L1_ffn_k_scale, L1_ffn_Wo, L1_ffn_ln_g, L1_ffn_ln_b, L1_ffn_W1, L1_ffn_b1, L1_ffn_W2, L1_ffn_b2)
    return x

_drawn_inputs = setup_inputs


def setup_inputs(seed=0):
    import zlib

    import numpy as np

    out = dict(_drawn_inputs(seed))
    spreads = {'L0_attn_rms_w': (1.0, 0.6),
     'L0_ffn_gate_bias': (0.0, 0.8),
     'L1_ffn_q_scale': (1.0, 0.6),
     'L1_ffn_k_scale': (1.0, 0.6),
     'L1_ffn_ln_g': (1.0, 0.6),
     'L1_ffn_ln_b': (0.0, 0.8),
     'L1_ffn_b1': (0.0, 0.8),
     'L1_ffn_b2': (0.0, 0.1)}
    factors = {'L0_ffn_gate_w': 8.0,
     'L0_ffn_w1': 8.0,
     'L0_ffn_w2': 8.0,
     'L0_ffn_w3': 8.0,
     'L0_ffn_ws1': 8.0,
     'L0_ffn_ws2': 8.0,
     'L0_ffn_ws3': 8.0,
     'L1_attn_Wq': 8.0,
     'L1_attn_Wk': 8.0,
     'L1_attn_Wv': 8.0,
     'L1_attn_Wo': 8.0,
     'L1_ffn_W1': 3.681,
     'L1_ffn_W2': 3.617,
     'L0_attn_w_gates': 8.0}
    for name, (base, spread) in spreads.items():
        noise = np.random.default_rng([zlib.crc32(name.encode()), seed]).standard_normal(out[name].shape)
        drawn = base * np.exp(spread * noise) if base else spread * noise
        out[name] = jnp.asarray(drawn.astype(out[name].dtype))
    for name, factor in factors.items():
        out[name] = (out[name] * factor).astype(out[name].dtype)
    return out
```

```python
from contextlib import ExitStack

import numpy as np

import concourse.bass as bass
from concourse import mybir

F32 = mybir.dt.float32
BF16 = mybir.dt.bfloat16
ALU = mybir.AluOpType
ACT = mybir.ActivationFunctionType
AX = mybir.AxisListType

P = 128
D = 128
B, N = 8, 512
T = N // P
NEG = -1.0e30
BANKS, BANK = 8, 512

H0, E0 = 8, 64
PAIRS0 = H0 * E0 // P
EXPERTS, INTER, GROUPS, TOPK, TOPG = 16, 64, 4, 4, 2
CH0 = EXPERTS * INTER // P
H1, E1 = 16, 8
HG = 4
DEPTH, HL, EL, WIN = 6, 16, 64, 32
INNER = HL * EL
PAIRSL = INNER // P
DI = int(D * 4 * 2 / 3)
CW = [114, 114, 113]
QK_SCALE = 8.0
TINY = 2.0 ** 24
LN_TINY_HALF = 12.0 * float(np.log(2.0))



class Steps:

    def __init__(self, sem, keys):
        self.sem, self.keys = sem, list(keys)
        self.at = {k: n + 1 for n, k in enumerate(self.keys)}
        self.n = len(self.keys)
        assert len(self.at) == self.n
        self.sent = 0

    def prime(self, eng):
        eng.sem_inc(self.sem, self.n)

    def value(self, it, key):
        return (it + 1) * self.n + self.at[key]

    def before(self, it, key):
        return it * self.n + self.at[key]

    def wait(self, eng, it, key):
        eng.wait_ge(self.sem, self.value(it, key))

    def wait_before(self, eng, it, key):
        eng.wait_ge(self.sem, self.before(it, key))

    def done(self, ins, key):
        assert self.keys[self.sent % self.n] == key, (key, self.keys[self.sent % self.n])
        self.sent += 1
        ins.then_inc(self.sem, 1)


def settle(eng, passed):
    eng.sem_inc(passed, 1)


class Ring:

    def __init__(self, filled, slots, late):
        order = []
        for key, _ in slots:
            if key not in late:
                order.append(key)
                order += [k for k, after in late.items() if after == key]
        self.steps = Steps(filled, order)
        self.index = {key: n for n, (key, _) in enumerate(slots)}
        self.readers = [r for _, r in slots]

    def bank(self, key):
        return self.index[key] % BANKS

    def take(self, pe, it, key):
        n = self.index[key]
        if n >= BANKS:
            for steps, k in self.readers[n - BANKS]:
                steps.wait(pe, it, k)
        else:
            last = max(m for m in range(len(self.readers)) if m % BANKS == n % BANKS)
            for steps, k in self.readers[last]:
                steps.wait_before(pe, it, k)
        return self.bank(key)

    def full(self, eng, it, key):
        self.steps.wait(eng, it, key)
        return self.bank(key)


class Chain:

    def __init__(self, eng, sem, n):
        self.eng, self.sem, self.n, self.sent = eng, sem, n, 0

    def link(self, it, ins):
        ins.then_inc(self.sem, 1)
        self.sent += 1
        self.eng.wait_ge(self.sem, it * self.n + self.sent)

    def end(self):
        assert self.sent == self.n, self.sent
        self.sent = 0


def units_of(heads):
    return [(h, i) for h in range(heads) for i in range(T)]


def causal_order(heads):
    units = units_of(heads)
    for n in range(len(units) + 3):
        if n < len(units):
            yield "score", n
        if 2 <= n < len(units) + 2:
            yield "turn", n - 2
        if n >= 3:
            yield "pv", n - 3


SCORE_HEADS = [(0, 2, 4), (1, 3, 5), (6, 8, 10), (7, 9, 11), (12, 14), (13, 15)]
OUT_HEADS = [(0, 6), (6, 11), (11, 16)]


def order1():
    def project(t):
        return [("qk", t, j) for j in range(4)] + [("v", t, j) for j in range(2)]

    def turn(t):
        return [("t", t, j) for j in range(4)]

    def score(t):
        return [("s", t, g) for g in range(6)]

    def weigh(t):
        out = [("pt", t, k) for k in range(4)] + ([("pp", t)] if t else [])
        return out + [("o", t, n) for n in range(3)]

    def finish(t):
        return [("ot", t, 0), ("ot", t, 1), ("y", t)]

    out = project(0) + project(1) + turn(0) + score(0)
    out += project(2) + turn(1) + score(1) + weigh(0)
    out += project(3) + finish(0) + turn(2) + score(2) + weigh(1)
    out += turn(3) + finish(1) + score(3) + weigh(2) + finish(2) + weigh(3) + finish(3)
    out += [("xt",), ("xn",)]
    for c in range(3):
        out += [("gate", c), ("up", c)]
    return out + [("y2",)]




class Shared:

    def __init__(self, nc, ctx):
        def sb(name, shape, dt=F32):
            return ctx.enter_context(nc.sbuf_tensor(name, shape, dt))

        self.ident = sb("ident", [P, P])
        self.identb = sb("identb", [P, P], BF16)
        self.maskc = sb("maskc", [P, P], BF16)
        self.maskw = sb("maskw", [P, WIN + P], BF16)
        self.eps5 = sb("eps5", [P, 1])
        self.epst = sb("epst", [P, 1])
        self.lnt = sb("lnt", [P, 1])
        self.state = sb("state", [P, B, N + 1])
        self.psum = [ctx.enter_context(nc.psum_tensor(f"psum{b}", [P, BANK], F32)) for b in range(BANKS)]


def pass0(nc, io, sh, ctx):
    ident, identb, maskc, state, psum = sh.ident, sh.identb, sh.maskc, sh.state, sh.psum
    eps5, epst = sh.eps5, sh.epst

    def sb(name, shape, dt=F32):
        return ctx.enter_context(nc.sbuf_tensor(name, shape, dt))

    def sem(name):
        return ctx.enter_context(nc.semaphore(name))

    def steps(name, keys):
        return Steps(sem(name), keys)

    GR = H0 + EXPERTS
    maskc_f, maskw_f = sb("maskc_f", [P, P]), sb("maskw_f", [P, WIN + P])
    wq, wk, wv = (sb(n, [P, H0 * E0]) for n in ("wq", "wk", "wv"))
    wo = sb("wo", [P, PAIRS0, D])
    wgr = sb("wgr", [P, GR])
    rmsw, gbias = sb("rmsw", [P, 1]), sb("gbias", [P, EXPERTS])
    w1, w3 = sb("w1", [P, (EXPERTS + 1) * INTER]), sb("w3", [P, (EXPERTS + 1) * INTER])
    w2 = sb("w2", [P, CH0 + 1, D])
    sel = sb("sel", [EXPERTS, CH0, P])
    tie16, tie4 = sb("tie16", [P, EXPERTS, EXPERTS]), sb("tie4", [P, GROUPS, GROUPS])
    wq1, wk1 = sb("wq1", [P, HG, P]), sb("wk1", [P, HG, P])
    wv1, wo1 = sb("wv1", [P, D]), sb("wo1", [P, D])

    x, xn, tn = (sb(n, [P, T, D]) for n in ("x", "xn", "tn"))
    square = sb("square", [P, T, D])
    stats, mv = sb("stats", [P, T, 6]), sb("mv", [P, T, 2])
    lnv, rstd, ms, lnm, rrms = (sb(n, [P, T]) for n in ("lnv", "rstd", "ms", "lnm", "rrms"))
    xnT, tT = sb("xnT", [P, N]), sb("tT", [P, N])
    egr, sig = sb("egr", [P, T, GR]), sb("sig", [P, T, GR])
    biased, gmax = sb("biased", [P, T, EXPERTS]), sb("gmax", [P, T, GROUPS])
    gt4, eq4 = sb("gt4", [P, T, GROUPS, GROUPS]), sb("eq4", [P, T, GROUPS, GROUPS])
    rank4, keep, pen = (sb(n, [P, T, GROUPS]) for n in ("rank4", "keep", "pen"))
    kept = sb("kept", [P, T, EXPERTS])
    gt16, eq16 = sb("gt16", [P, T, EXPERTS, EXPERTS]), sb("eq16", [P, T, EXPERTS, EXPERTS])
    rank16, comb = sb("rank16", [P, T, EXPERTS]), sb("comb", [P, T, EXPERTS])
    combT = sb("combT", [EXPERTS, N])
    qT, kT = sb("qT", [P, PAIRS0, N]), sb("kT", [P, PAIRS0, N])
    v = sb("v", [P, T, H0, E0 + 1])
    negmax = sb("negmax", [P, 4])
    prob, probT = sb("prob", [P, 3, N]), sb("probT", [P, 3, N])
    rsum, rgate = sb("rsum", [P, 2, T]), sb("rgate", [P, 2, T])
    o, oT = sb("o", [P, T, H0 * E0]), sb("oT", [P, PAIRS0, N])
    act1, prod, hT = sb("act1", [P, 2, N]), sb("prod", [P, 2, N]), sb("hT", [P, CH0 + 1, N])
    x1, x1n, x1T = sb("x1", [P, T, D]), sb("x1n", [P, T, D]), sb("x1T", [P, N])
    qT1, kT1 = sb("qT1", [P, HG, N]), sb("kT1", [P, HG, N])
    v1 = sb("v1", [P, T, H1, E1 + 1])
    o1, oT1, sumout = sb("o1", [P, T, D]), sb("oT1", [P, N]), sb("sumout", [P, T, D])

    ua, ub = units_of(H0), units_of(H1)
    units = [("a", n) for n in range(len(ua))] + [("b", n) for n in range(len(ub))]
    const_loaded, const_made, x_loaded, stored = sem("const_loaded"), sem("const_made"), sem("x_loaded"), sem("stored")
    measured = steps("measured", ["var", "ms", "var1"])
    normed = steps("normed", ["xn", "tn", "x1n"])
    maxed = steps("maxed", units)
    turned_v = steps("turned_v", [u for u in units if u[1] % 2 == 0])
    o_ready = steps("o_ready", [("a", h) for h in range(H0)] + [("b", h) for h in range(H1)])
    moved = steps("moved", ["tT", "comb", "x1", "sum"])
    gated = steps("gated", range(CH0 + 1))
    rooted = steps("rooted", ["rstd", "rrms", "rstd1"])
    copied = steps("copied", ["xnT", "gr"] + [(a, p) for p in range(PAIRS0) for a in "qk"]
                   + [("v", t) for t in range(T)] + ["ct"] + [("ot", t) for t in range(T)]
                   + ["x1T"] + [(a, g) for g in range(HG) for a in ("q1", "k1")] + ["v1", "ot1"])
    exped = steps("exped", units)
    turned_s = steps("turned_s", [u for u in units if u[1] % 2 == 1])
    silued = steps("silued", range(CH0 + 1))
    link, rlink, passed = sem("link"), sem("rlink"), sem("passed")

    def causal_slots(tag, heads):
        for what, n in causal_order(heads):
            if what == "score":
                yield (tag + "s", n), [(exped, (tag, n))]
            elif what == "turn":
                yield (tag + "pt", n), [(turned_v if n % 2 == 0 else turned_s, (tag, n))]
            elif n % T == 0:
                yield (tag + "o", n // T), [(o_ready, (tag, n // T))]

    slots = [("xt", [(copied, "xnT")]), ("tt", [(moved, "tT")]), ("gr", [(copied, "gr")])]
    slots += [((a, p), [(copied, (a, p))]) for p in range(PAIRS0) for a in "qk"]
    slots += [(("v", t), [(copied, ("v", t))]) for t in range(T)]
    slots += list(causal_slots("a", H0))
    slots += [("ct", [(copied, "ct")])] + [(("ot", t), [(copied, ("ot", t))]) for t in range(T)]
    for c in range(CH0):
        slots += [(("h1", c), [(silued, c)]), (("h3", c), [(gated, c)]), (("cb", c), [(gated, c)])]
    slots += [(("h1", CH0), [(silued, CH0)]), (("h3", CH0), [(gated, CH0)])]
    slots += [("y", [(moved, "x1")]), ("x1t", [(copied, "x1T")])]
    slots += [((a, g), [(copied, (a, g))]) for g in range(HG) for a in ("q1", "k1")]
    slots += [("v1", [(copied, "v1")])]
    slots += list(causal_slots("b", H1))
    slots += [("ot1", [(copied, "ot1")]), ("y1", [(moved, "sum")])]
    late = {(tag + "o", h): (tag + "pt", min(T * h + T, T * heads - 1))
            for tag, heads in (("a", H0), ("b", H1)) for h in range(heads)}
    ring = Ring(sem("filled"), slots, late)

    def chunk(c):
        return P if c < CH0 else INTER

    loads = [(ident, "ident"), (maskc_f, "maskc"), (maskw_f, "maskw"), (wq, "wq0"), (wk, "wk0"), (wv, "wv0"),
             (wo, "wo0"), (rmsw, "rmsw"), (w1, "w1"), (w3, "w3"), (sel, "sel"), (wq1, "wq1"), (wk1, "wk1"),
             (wv1, "wv1"), (wo1, "wo1")]
    ALL_LOADED = 16 * (len(loads) + 7)
    ALL_MADE = 9

    with nc.Block() as block:
        @block.sync
        def _(sp):
            for dst, name in loads:
                sp.dma_start(dst[tuple(slice(None) for _ in dst.shape)], io[name]).then_inc(const_loaded, 16)
            sp.dma_start(wgr[:, 0:H0], io["wgates"]).then_inc(const_loaded, 16)
            sp.dma_start(wgr[:, H0:GR], io["wroute"]).then_inc(const_loaded, 16)
            sp.dma_start(gbias[:, :], io["gbias"].partition_broadcast(P)).then_inc(const_loaded, 16)
            sp.dma_start(tie16[:, :, :], io["tie16"].partition_broadcast(P)).then_inc(const_loaded, 16)
            sp.dma_start(tie4[:, :, :], io["tie4"].partition_broadcast(P)).then_inc(const_loaded, 16)
            sp.dma_start(w2[:, 0:CH0, :], io["w2"]).then_inc(const_loaded, 16)
            sp.dma_start(w2[0:INTER, CH0, :], io["ws2"]).then_inc(const_loaded, 16)
            sp.sem_inc(stored, 16)
            with sp.Fori(0, B) as it:
                moved.wait_before(sp, it, "x1")
                settle(sp, passed)
                sp.dma_start(x[:, :, :], io["x"][bass.ds(it, 1)].rearrange("s (t p) d -> p (s t) d", p=P)
                             ).then_inc(x_loaded, 16)
                moved.wait(sp, it, "sum")
                settle(sp, passed)
                sp.dma_start(io["sums"][bass.ds(it, 1)].rearrange("s (t p) d -> p (s t) d", p=P), sumout[:, :, :]
                             ).then_inc(stored, 16)
            sp.wait_ge(stored, 16 * B + 16)

        @block.gpsimd
        def _(pool):
            for dst, value in ((eps5[:, :], 1e-5), (epst[:, :], float(np.finfo(np.float32).eps)),
                               (sh.lnt[:, :], LN_TINY_HALF), (v[:, :, :, E0:E0 + 1], 1.0),
                               (v1[:, :, :, E1:E1 + 1], 1.0), (state[:, :, :], 0.0)):
                nc.gpsimd.memset(dst, value).then_inc(const_made, 1)
            pool.wait_ge(const_loaded, ALL_LOADED)
            nc.gpsimd.tensor_copy(identb[:, :], ident[:, :]).then_inc(const_made, 1)
            nc.gpsimd.tensor_copy(maskc[:, :], maskc_f[:, :]).then_inc(const_made, 1)
            nc.gpsimd.tensor_copy(sh.maskw[:, :], maskw_f[:, :]).then_inc(const_made, 1)

        @block.tensor
        def _(pe):
            ring.steps.prime(pe)
            pe.wait_ge(const_loaded, ALL_LOADED)
            pe.wait_ge(const_made, ALL_MADE)

            def take(it, key):
                return psum[ring.take(pe, it, key)]

            def turn4(it, key, src):
                ps = take(it, key)
                for t in range(T):
                    last = nc.tensor.transpose(ps[:, t * P:(t + 1) * P], src(t), ident[:, :])
                ring.steps.done(last, key)

            def product(it, key, lhsT, rhs, m=P):
                ps = take(it, key)
                ring.steps.done(nc.tensor.matmul(ps[0:m, :], lhsT, rhs, start=True, stop=True), key)

            def causal(it, tag, heads, q_of, k_of, v_of, width):
                for what, n in causal_order(heads):
                    h, i = divmod(n, T)
                    nk = (i + 1) * P
                    if what == "score":
                        ps = take(it, (tag + "s", n))
                        nc.tensor.matmul(ps[:, 0:nk], q_of(h, i), k_of(h, nk), start=True, stop=False)
                        ring.steps.done(nc.tensor.matmul(ps[:, i * P:nk], identb[:, :], maskc[:, :],
                                                         start=False, stop=True), (tag + "s", n))
                    elif what == "turn":
                        exped.wait(pe, it, (tag, n))
                        ps = take(it, (tag + "pt", n))
                        for j in range(i + 1):
                            last = nc.tensor.transpose(ps[:, j * P:(j + 1) * P], prob[:, n % 3, j * P:(j + 1) * P],
                                                       ident[:, :])
                        ring.steps.done(last, (tag + "pt", n))
                    else:
                        if i == 0:
                            take(it, (tag + "o", h))
                        ps = psum[ring.bank((tag + "o", h))]
                        (turned_v if n % 2 == 0 else turned_s).wait(pe, it, (tag, n))
                        for j in range(i + 1):
                            last = nc.tensor.matmul(ps[:, i * width:(i + 1) * width], probT[:, n % 3, j * P:(j + 1) * P],
                                                    v_of(h, j), start=(j == 0), stop=(j == i))
                        if i == T - 1:
                            ring.steps.done(last, (tag + "o", h))

            with pe.Fori(0, B) as it:
                normed.wait(pe, it, "xn")
                turn4(it, "xt", lambda t: xn[:, t, :])
                normed.wait(pe, it, "tn")
                turn4(it, "tt", lambda t: tn[:, t, :])
                copied.wait(pe, it, "xnT")
                moved.wait(pe, it, "tT")
                ps = take(it, "gr")
                for t in range(T):
                    nc.tensor.matmul(ps[:, t * GR:t * GR + H0], tT[:, t * P:(t + 1) * P], wgr[:, 0:H0],
                                     start=True, stop=True)
                    last = nc.tensor.matmul(ps[:, t * GR + H0:(t + 1) * GR], xnT[:, t * P:(t + 1) * P], wgr[:, H0:GR],
                                            start=True, stop=True)
                ring.steps.done(last, "gr")
                for p in range(PAIRS0):
                    product(it, ("q", p), wq[:, p * P:(p + 1) * P], tT[:, :])
                    product(it, ("k", p), wk[:, p * P:(p + 1) * P], tT[:, :])
                for t in range(T):
                    product(it, ("v", t), tT[:, t * P:(t + 1) * P], wv[:, :])
                copied.wait(pe, it, ("v", T - 1))
                causal(it, "a", H0,
                       lambda h, i: qT[64 * (h % 2):64 * (h % 2) + 64, h // 2, i * P:(i + 1) * P],
                       lambda h, nk: kT[64 * (h % 2):64 * (h % 2) + 64, h // 2, 0:nk],
                       lambda h, j: v[:, j, h, :], E0 + 1)
                moved.wait(pe, it, "comb")
                ps = take(it, "ct")
                for t in range(T):
                    last = nc.tensor.transpose(ps[0:EXPERTS, t * P:(t + 1) * P], comb[:, t, :], ident[:, :])
                ring.steps.done(last, "ct")
                o_ready.wait(pe, it, ("a", H0 - 1))
                for t in range(T):
                    turn4(it, ("ot", t), lambda p: o[:, t, p * P:(p + 1) * P])
                copied.wait(pe, it, "ct")
                for c in range(CH0 + 1):
                    m = chunk(c)
                    product(it, ("h1", c), w1[:, c * P:c * P + m], xnT[:, :], m)
                    product(it, ("h3", c), w3[:, c * P:c * P + m], xnT[:, :], m)
                    if c < CH0:
                        product(it, ("cb", c), sel[:, c, :], combT[:, :])
                ps = take(it, "y")
                copied.wait(pe, it, ("ot", T - 1))
                gated.wait(pe, it, CH0)
                for t in range(T):
                    yt = ps[:, t * D:(t + 1) * D]
                    for p in range(PAIRS0):
                        nc.tensor.matmul(yt, oT[:, p, t * P:(t + 1) * P], wo[:, p, :], start=(p == 0), stop=False)
                    for c in range(CH0 + 1):
                        m = chunk(c)
                        last = nc.tensor.matmul(yt, hT[0:m, c, t * P:(t + 1) * P], w2[0:m, c, :],
                                                start=False, stop=(c == CH0))
                ring.steps.done(last, "y")
                normed.wait(pe, it, "x1n")
                turn4(it, "x1t", lambda t: x1n[:, t, :])
                copied.wait(pe, it, "x1T")
                for g in range(HG):
                    product(it, ("q1", g), wq1[:, g, :], x1T[:, :])
                    product(it, ("k1", g), wk1[:, g, :], x1T[:, :])
                ps = take(it, "v1")
                for t in range(T):
                    last = nc.tensor.matmul(ps[:, t * D:(t + 1) * D], x1T[:, t * P:(t + 1) * P], wv1[:, :],
                                            start=True, stop=True)
                ring.steps.done(last, "v1")
                copied.wait(pe, it, "v1")
                causal(it, "b", H1,
                       lambda h, i: qT1[32 * (h % HG):32 * (h % HG) + E1, h // HG, i * P:(i + 1) * P],
                       lambda h, nk: kT1[32 * (h % HG):32 * (h % HG) + E1, h // HG, 0:nk],
                       lambda h, j: v1[:, j, h, :], E1 + 1)
                o_ready.wait(pe, it, ("b", H1 - 1))
                turn4(it, "ot1", lambda t: o1[:, t, :])
                copied.wait(pe, it, "ot1")
                ps = take(it, "y1")
                for t in range(T):
                    last = nc.tensor.matmul(ps[:, t * D:(t + 1) * D], oT1[:, t * P:(t + 1) * P], wo1[:, :],
                                            start=True, stop=True)
                ring.steps.done(last, "y1")

        @block.scalar
        def _(act):
            for s in (rooted, copied, exped, turned_s, silued):
                s.prime(act)
            act.wait_ge(const_loaded, ALL_LOADED)
            act.wait_ge(const_made, ALL_MADE)
            chain = Chain(act, rlink, 3)

            def full(it, key):
                return psum[ring.full(act, it, key)]

            def rsqrt(it, key, out, tmp, src, scale, eps):
                chain.link(it, nc.scalar.activation(tmp, src, ACT.Ln, bias=eps[:, 0:1], scale=scale))
                rooted.done(nc.scalar.activation(out, tmp, ACT.Exp, scale=-0.5), key)

            def copy(it, key, dst, src=None, scale=1.0):
                ps = full(it, key)
                copied.done(nc.scalar.activation(dst, ps[:, :] if src is None else src(ps), ACT.Copy, scale=scale),
                            key if key not in names else names[key])

            names = {"xt": "xnT", "x1t": "x1T"}

            def causal(it, tag, heads):
                us = units_of(heads)
                for n in range(len(us) + 2):
                    if n < len(us):
                        nk = (us[n][1] + 1) * P
                        maxed.wait(act, it, (tag, n))
                        exped.done(nc.scalar.activation(prob[:, n % 3, 0:nk], full(it, (tag + "s", n))[:, 0:nk], ACT.Exp,
                                                        bias=negmax[:, n % 4:n % 4 + 1]), (tag, n))
                    if n >= 2 and n % 2 == 1:
                        nk = (us[n - 2][1] + 1) * P
                        turned_s.done(nc.scalar.copy(probT[:, (n - 2) % 3, 0:nk],
                                                     full(it, (tag + "pt", n - 2))[:, 0:nk]), (tag, n - 2))

            with act.Fori(0, B) as it:
                measured.wait(act, it, "var")
                rsqrt(it, "rstd", rstd[:, :], lnv[:, :], mv[:, :, 1], 1.0, eps5)
                measured.wait(act, it, "ms")
                rsqrt(it, "rrms", rrms[:, :], lnm[:, :], ms[:, :], 1.0 / D, epst)
                copy(it, "xt", xnT[:, :])
                ps = full(it, "gr")
                copied.done(nc.scalar.activation(egr[:, :, :], ps[:, 0:T * GR].rearrange("p (t c) -> p t c", t=T),
                                                 ACT.Exp, scale=-1.0), "gr")
                for p in range(PAIRS0):
                    copy(it, ("q", p), qT[:, p, :], scale=float(E0) ** -0.5)
                    copy(it, ("k", p), kT[:, p, :])
                for t in range(T):
                    copy(it, ("v", t), v[:, t, :, 0:E0], lambda ps: ps[:, :].rearrange("p (h e) -> p h e", h=H0))
                causal(it, "a", H0)
                copy(it, "ct", combT[:, :], lambda ps: ps[0:EXPERTS, :])
                for t in range(T):
                    copy(it, ("ot", t), oT[:, :, t * P:(t + 1) * P],
                         lambda ps: ps[:, :].rearrange("p (c n) -> p c n", c=PAIRS0))
                for c in range(CH0 + 1):
                    m = chunk(c)
                    if c >= 2:
                        gated.wait(act, it, c - 2)
                    silued.done(nc.scalar.activation(act1[0:m, c % 2, :], full(it, ("h1", c))[0:m, :], ACT.Silu), c)
                measured.wait(act, it, "var1")
                rsqrt(it, "rstd1", rstd[:, :], lnv[:, :], mv[:, :, 1], 1.0, eps5)
                copy(it, "x1t", x1T[:, :])
                for g in range(HG):
                    copy(it, ("q1", g), qT1[:, g, :], scale=float(E1) ** -0.5)
                    copy(it, ("k1", g), kT1[:, g, :])
                copy(it, "v1", v1[:, :, :, 0:E1].rearrange("p t h e -> p (t h) e"),
                     lambda ps: ps[:, :].rearrange("p (g e) -> p g e", e=E1))
                causal(it, "b", H1)
                copy(it, "ot1", oT1[:, :])
                chain.end()

        @block.vector
        def _(dve):
            for s in (measured, normed, maxed, turned_v, o_ready, moved, gated):
                s.prime(dve)
            dve.wait_ge(const_loaded, ALL_LOADED)
            dve.wait_ge(const_made, ALL_MADE)
            chain = Chain(dve, link, LINKS0)
            V = nc.vector

            def full(it, key):
                return psum[ring.full(dve, it, key)]

            def moments(it, src, key):
                for t in range(T):
                    last = V.bn_stats(stats[:, t, :], src[:, t, :])
                chain.link(it, last)
                settle(dve, passed)
                for t in range(T):
                    last = V.bn_aggr(mv[:, t, :], stats[:, t, :])
                measured.done(last, key)

            def normalize(it, dst, src, key, root, norm):
                measured.wait(dve, it, key)
                rooted.wait(dve, it, root)
                for t in range(T):
                    last = V.tensor_scalar(dst[:, t, :], src[:, t, :], mv[:, t, 0:1], rstd[:, t:t + 1],
                                           ALU.subtract, ALU.mult)
                normed.done(last, norm)
                normed.wait(dve, it, norm)

            def rank(it, values, gt, eq, tie, out, n):
                other = values.unsqueeze(2).to_broadcast([P, T, n, n])
                own = values.unsqueeze(3).to_broadcast([P, T, n, n])
                V.tensor_tensor(gt[:, :, :, :], other, own, ALU.is_gt)
                chain.link(it, V.tensor_tensor(eq[:, :, :, :], other, own, ALU.is_equal))
                chain.link(it, V.tensor_tensor(eq[:, :, :, :], eq[:, :, :, :],
                                               tie[:, :, :].unsqueeze(1).to_broadcast([P, T, n, n]), ALU.mult))
                chain.link(it, V.tensor_tensor(gt[:, :, :, :], gt[:, :, :, :], eq[:, :, :, :], ALU.add))
                chain.link(it, V.tensor_reduce(out[:, :, :], gt[:, :, :, :], AX.X, ALU.add))

            def route(it):
                copied.wait(dve, it, "gr")
                chain.link(it, V.tensor_scalar(sig[:, :, :], egr[:, :, :], 1.0, None, ALU.add))
                chain.link(it, V.reciprocal(sig[:, :, :], sig[:, :, :]))
                score = sig[:, :, H0:GR]
                chain.link(it, V.tensor_tensor(biased[:, :, :], score,
                                               gbias[:, :].unsqueeze(1).to_broadcast([P, T, EXPERTS]), ALU.add))
                chain.link(it, V.tensor_reduce(gmax[:, :, :], biased[:, :, :].rearrange("p t (g e) -> p t g e", g=GROUPS),
                                               AX.X, ALU.max))
                rank(it, gmax[:, :, :], gt4, eq4, tie4, rank4, GROUPS)
                chain.link(it, V.tensor_scalar(keep[:, :, :], rank4[:, :, :], float(TOPG), None, ALU.is_lt))
                chain.link(it, V.tensor_scalar(pen[:, :, :], keep[:, :, :], -NEG, NEG, ALU.mult, ALU.add))
                groups = [P, T * GROUPS, EXPERTS // GROUPS]
                wide = lambda a: a[:, :, :].rearrange("p t g -> p (t g)").unsqueeze(2).to_broadcast(groups)
                by_group = lambda a: a[:, :, :].rearrange("p t (g e) -> p (t g) e", g=GROUPS)
                chain.link(it, V.tensor_tensor(by_group(kept), by_group(biased), wide(keep), ALU.mult))
                chain.link(it, V.tensor_tensor(by_group(kept), by_group(kept), wide(pen), ALU.add))
                rank(it, kept[:, :, :], gt16, eq16, tie16, rank16, EXPERTS)
                chain.link(it, V.tensor_scalar(rank16[:, :, :], rank16[:, :, :], float(TOPK), None, ALU.is_lt))
                moved.done(V.tensor_tensor(comb[:, :, :], rank16[:, :, :], score, ALU.mult), "comb")

            def causal(it, tag, heads, width, out, gate):
                us = units_of(heads)
                for n in range(len(us) + 4):
                    if n >= 7 and n % T == 3:
                        h = (n - 7) // T
                        e = width - 1
                        ps = full(it, (tag + "o", h))[:, 0:T * width].rearrange("p (t e) -> p t e", t=T)
                        r = rsum[:, h % 2, :]
                        chain.link(it, V.reciprocal(r, ps[:, :, e]))
                        if gate:
                            r = rgate[:, h % 2, :]
                            chain.link(it, V.tensor_tensor(r, rsum[:, h % 2, :], sig[:, :, h], ALU.mult))
                        o_ready.done(V.tensor_tensor(out[:, :, h * e:(h + 1) * e], ps[:, :, 0:e],
                                                     r.unsqueeze(2).to_broadcast([P, T, e]), ALU.mult), (tag, h))
                    if n < len(us):
                        nk = (us[n][1] + 1) * P
                        maxed.done(V.tensor_reduce(negmax[:, n % 4:n % 4 + 1], full(it, (tag + "s", n))[:, 0:nk],
                                                   AX.X, ALU.max, negate=True), (tag, n))
                    if n >= 2 and n % 2 == 0 and n - 2 < len(us):
                        nk = (us[n - 2][1] + 1) * P
                        turned_v.done(V.tensor_copy(probT[:, (n - 2) % 3, 0:nk],
                                                    full(it, (tag + "pt", n - 2))[:, 0:nk]), (tag, n - 2))
                    if gate and n == 4:
                        route(it)

            with dve.Fori(0, B) as it:
                dve.wait_ge(x_loaded, it * 16 + 16)
                moments(it, x, "var")
                ring.steps.wait_before(dve, it, "tt")
                normalize(it, xn, x, "var", "rstd", "xn")
                for t in range(T):
                    last = V.tensor_tensor_reduce(square[:, t, :], xn[:, t, :], xn[:, t, :], 1.0, 0.0, ALU.mult, ALU.add,
                                                  ms[:, t:t + 1])
                measured.done(last, "ms")
                rooted.wait(dve, it, "rrms")
                for t in range(T):
                    last = V.tensor_scalar(tn[:, t, :], xn[:, t, :], rrms[:, t:t + 1], None, ALU.mult)
                normed.done(last, "tn")
                moved.done(V.tensor_scalar(tT[:, :], full(it, "tt")[:, :], rmsw[:, 0:1], None, ALU.mult), "tT")
                causal(it, "a", H0, E0 + 1, o, True)
                for c in range(CH0 + 1):
                    m = chunk(c)
                    silued.wait(dve, it, c)
                    ps = full(it, ("h3", c))
                    if c < CH0:
                        chain.link(it, V.tensor_tensor(prod[:, c % 2, :], ps[:, :], act1[:, c % 2, :], ALU.mult))
                        gated.done(V.tensor_tensor(hT[:, c, :], full(it, ("cb", c))[:, :], prod[:, c % 2, :], ALU.mult), c)
                    else:
                        gated.done(V.tensor_tensor(hT[0:m, c, :], ps[0:m, :], act1[0:m, c % 2, :], ALU.mult), c)
                moved.done(V.tensor_tensor(x1[:, :, :], full(it, "y")[:, :].rearrange("p (t d) -> p t d", t=T), x[:, :, :],
                                           ALU.add), "x1")
                moved.wait(dve, it, "x1")
                moments(it, x1, "var1")
                normalize(it, x1n, x1, "var1", "rstd1", "x1n")
                copied.wait(dve, it, "x1T")
                V.tensor_copy(state[0:D // 2, bass.ds(it, 1), 0:N].rearrange("p s n -> p (s n)"), x1T[0:D // 2, :])
                V.tensor_copy(state[D // 2:D, bass.ds(it, 1), 1:N + 1].rearrange("p s n -> p (s n)"), x1T[D // 2:D, :])
                causal(it, "b", H1, E1 + 1, o1, False)
                ps = full(it, "y1")
                dve.wait_ge(stored, it * 16 + 16)
                moved.done(V.tensor_tensor(sumout[:, :, :], ps[:, :].rearrange("p (t d) -> p t d", t=T), x1[:, :, :],
                                           ALU.add), "sum")
                chain.end()


def pass1(nc, io, sh, ctx):
    ident, identb, maskw, state, psum = sh.ident, sh.identb, sh.maskw, sh.state, sh.psum

    def sb(name, shape, dt=F32):
        return ctx.enter_context(nc.sbuf_tensor(name, shape, dt))

    def sem(name):
        return ctx.enter_context(nc.semaphore(name))

    def steps(name, keys):
        return Steps(sem(name), keys)

    WK = WIN + P
    wqkv, wol = sb("wqkv", [P, 3 * INNER]), sb("wol", [P, PAIRSL, D])
    w1l, w2l = sb("w1l", [P, 2 * DI]), sb("w2l", [P, 3, D])
    b1l = sb("b1l", [P, 2, 3])
    lng, lnb, b2l = sb("lng", [P, 1]), sb("lnb", [P, 1]), sb("b2l", [P, 1])
    qks = sb("qks", [P, 2, EL])
    rot = sb("rot", [P, 4, T, EL])
    rots = sb("rots", [P, 4, T, EL])

    xw = sb("xw", [P, N + 1])
    xm = sb("xm", [P, N + 1])
    sq = sb("sq", [P, 2, BANK])
    ss, ssc = sb("ss", [P, 2 * HL]), sb("ssc", [P, 2, 2 * HL])
    lns, rn = sb("lns", [P, 2 * HL]), sb("rn", [P, 2, 2 * HL])
    cosd, sind = sb("cosd", [P, 2, 4, BANK]), sb("sind", [P, 2, 4, BANK])
    qk = sb("qk", [P, 4, BANK])
    qTl, kTl = sb("qTl", [P, 2, PAIRSL, P]), sb("kTl", [P, PAIRSL, N])
    vl = sb("vl", [P, T, HL, EL + 1])
    negmaxl = sb("negmaxl", [P, 2, HL])
    probl = sb("probl", [P, 2, HL, WK])
    pT = sb("pT", [P, HL, P])
    pP = sb("pP", [P, HL, WIN])
    rs, on = sb("rs", [P, 2, HL]), sb("on", [P, 2, INNER])
    oTl = sb("oTl", [P, 2, PAIRSL, P])
    stats, mv = sb("statsl", [P, T, 6]), sb("mvl", [P, T, 2])
    lnv, rstd = sb("lnvl", [P, T]), sb("rstdl", [P, T])
    x2, x2T = sb("x2", [P, T, D]), sb("x2T", [P, N])
    gel, hf = sb("gel", [P, 2, N]), sb("hf", [P, 3, N])

    order = order1()
    pieces = [(t, j) for t in range(T) for j in range(4)]
    groups = [(t, g) for t in range(T) for g in range(len(SCORE_HEADS))]
    qkv_loaded, o_loaded, ffn_loaded, rot_loaded, made = (sem(n) for n in ("qkv_loaded", "o_loaded", "ffn_loaded",
                                                                            "rot_loaded", "made"))
    fetched = steps("fetched", ["xw"])
    scaled = sem("scaled")
    summed_rot = steps("summed_rot", pieces)
    rotated = steps("rotated", pieces)
    parts = steps("parts", pieces)
    summed = steps("summed", pieces)
    clamped = steps("clamped", range(T))
    maxed = steps("maxedl", groups)
    turned_v = steps("turned_vl", [(t, k) for t in range(T) for k in (0, 2)])
    o_ready = steps("o_readyl", [(t, n) for t in range(T) for n in range(3)])
    mid = steps("mid", range(T))
    ffn = steps("ffn", ["var", "x2", "x2T"])
    hidden = steps("hidden", range(3))
    left = steps("left", ["state"])
    squared = steps("squared", pieces)
    vcopied = steps("vcopied", [(t, j) for t in range(T) for j in range(2)])
    rooted = steps("rootedl", [*range(T), "ffn"])
    tcopied = steps("tcopied", pieces)
    exped = steps("expedl", groups)
    turned_s = steps("turned_sl", [(t, k) for t in range(T) for k in ([1, 3] + (["pp"] if t else []))])
    ocopied = steps("ocopied", [(t, j) for t in range(T) for j in range(2)])
    gelued = steps("gelued", range(3))
    link, rlink, passed = sem("linkl"), sem("rlinkl"), sem("passedl")

    def readers(key):
        kind, at = key[0], key[1:]
        if kind == "qk":
            return [(squared, at)]
        if kind == "v":
            return [(vcopied, at)]
        if kind == "t":
            return [(tcopied, at)]
        if kind == "s":
            return [(exped, at)]
        if kind == "pt":
            return [(turned_s if at[1] % 2 else turned_v, at)]
        if kind == "pp":
            return [(turned_s, (at[0], "pp"))]
        if kind == "o":
            return [(o_ready, at)]
        if kind == "ot":
            return [(ocopied, at)]
        if kind == "y":
            return [(mid, at[0])]
        if kind == "xt":
            return [(ffn, "x2")]
        if kind == "xn":
            return [(ffn, "x2T")]
        if kind == "gate":
            return [(gelued, at[0])]
        if kind == "up":
            return [(hidden, at[0])]
        return [(left, "state")]

    ring = Ring(sem("filledl"), [(key, readers(key)) for key in order], {})

    def keys0(t):
        return (t * P - WIN, 0) if t else (0, WIN)

    with nc.Block() as block:
        @block.sync
        def _(sp):
            sp.dma_start(rot[:, :, :, :], io["rot"]).then_inc(rot_loaded, 16)
            with sp.Fori(0, DEPTH) as l:
                it = l * B
                one = bass.ds(l, 1)
                ring.steps.wait_before(sp, it, ("v", T - 1, 1))
                settle(sp, passed)
                sp.dma_start(wqkv[:, :], io["wqkv"][one].rearrange("l p n -> p (l n)")).then_inc(qkv_loaded, 16)
                parts.wait_before(sp, it, pieces[-1])
                settle(sp, passed)
                sp.wait_ge(scaled, l * 4 + 4)
                settle(sp, passed)
                sp.dma_start(qks[:, 0, :], io["qs"][one].to_broadcast([P, EL])).then_inc(qkv_loaded, 16)
                sp.dma_start(qks[:, 1, :], io["ks"][one].to_broadcast([P, EL])).then_inc(qkv_loaded, 16)
                ring.steps.wait_before(sp, it, ("y", T - 1))
                settle(sp, passed)
                sp.dma_start(wol[:, :, :], io["wol"][one].rearrange("l (c p) d -> p (l c) d", p=P)).then_inc(o_loaded, 16)
                left.wait_before(sp, it, "state")
                settle(sp, passed)
                sp.dma_start(w1l[:, :], io["w1l"][one].rearrange("l p n -> p (l n)")).then_inc(ffn_loaded, 16)
                for dst, name in ((lng, "lng"), (lnb, "lnb"), (b2l, "b2l")):
                    sp.dma_start(dst[:, :], io[name][one].rearrange("l p -> p l")).then_inc(ffn_loaded, 16)
                at = 0
                for c, m in enumerate(CW):
                    sp.dma_start(w2l[0:m, c, :], io["w2l"][one][:, at:at + m, :].rearrange("l p d -> p (l d)")
                                 ).then_inc(ffn_loaded, 16)
                    for a in range(2):
                        sp.dma_start(b1l[0:m, a, c:c + 1], io["b1l"][one][:, a * DI + at:a * DI + at + m]
                                     .rearrange("l p -> p l")).then_inc(ffn_loaded, 16)
                    at += m

        FFN_LOADS = 4 + 3 * 3

        @block.gpsimd
        def _(pool):
            for s in (fetched, summed_rot, rotated):
                s.prime(pool)
            pool.sem_inc(scaled, 4)
            nc.gpsimd.memset(vl[:, :, :, EL:EL + 1], 1.0).then_inc(made, 1)
            nc.gpsimd.memset(xm[:, :], 0.0).then_inc(made, 1)
            pool.wait_ge(rot_loaded, 16)
            with pool.Fori(0, DEPTH) as l:
                pool.wait_ge(qkv_loaded, l * 48 + 48)
                parts.wait_before(pool, l * B, pieces[-1])
                for a in range(2):
                    scale = qks[:, a, :].rearrange("p (two c) -> p two c", two=2)
                    for b, own in ((2 * a, scale), (2 * a + 1, scale[:, ::-1, :])):
                        nc.gpsimd.tensor_tensor(
                            rots[:, b, :, :].rearrange("p t (two c) -> p t two c", two=2),
                            rot[:, b, :, :].rearrange("p t (two c) -> p t two c", two=2),
                            own.unsqueeze(1).to_broadcast([P, T, 2, EL // 2]), ALU.mult).then_inc(scaled, 1)
                with pool.Fori(0, B) as s:
                    it = l * B + s
                    mid.wait_before(pool, it, T - 1)
                    fetched.done(nc.gpsimd.tensor_copy(xw[:, :], state[:, bass.ds(s, 1), :].rearrange("p s n -> p (s n)")), "xw")
                    for t in range(T):
                        for j in range(4):
                            parts.wait(pool, it, (t, j))
                            summed_rot.done(nc.gpsimd.tensor_tensor(cosd[:, t % 2, j, :], cosd[:, t % 2, j, :],
                                                                    sind[:, t % 2, j, :], ALU.add), (t, j))
                        rooted.wait(pool, it, t)
                        for j in range(4):
                            if t:
                                ring.steps.wait(pool, it, ("t", t - 1, j))
                            else:
                                ring.steps.wait_before(pool, it, ("t", T - 1, j))
                            summed_rot.wait(pool, it, (t, j))
                            rotated.done(nc.gpsimd.tensor_tensor(
                                qk[:, j, :].rearrange("p (h c) -> p h c", c=EL),
                                cosd[:, t % 2, j, :].rearrange("p (h c) -> p h c", c=EL),
                                rn[:, t % 2, 8 * j:8 * j + 8].unsqueeze(2).to_broadcast([P, 8, EL]), ALU.mult), (t, j))

        @block.tensor
        def _(pe):
            ring.steps.prime(pe)
            pe.wait_ge(made, 2)

            def fill(it, key):
                ps = psum[ring.take(pe, it, key)]
                kind, at = key[0], key[1:]
                t = at[0] if at else 0
                if kind in ("qk", "v"):
                    col = (4 if kind == "v" else 0) * BANK + at[1] * BANK
                    last = nc.tensor.matmul(ps[:, :], xw[:, t * P:(t + 1) * P], wqkv[:, col:col + BANK],
                                            start=True, stop=True)
                elif kind == "t":
                    rotated.wait(pe, it, at)
                    for c in range(4):
                        last = nc.tensor.transpose(ps[:, c * P:(c + 1) * P], qk[:, at[1], c * P:(c + 1) * P], ident[:, :])
                elif kind == "s":
                    if at[1] == 0:
                        tcopied.wait(pe, it, (t, 3))
                    heads = SCORE_HEADS[at[1]]
                    k0, c0 = keys0(t)
                    blocks = ps[:, 0:len(heads) * WK].rearrange("p (h k) -> p h k", k=WK)
                    nc.tensor.matmul(blocks[:, :, c0:WK], identb[:, :],
                                     maskw[:, c0:WK].unsqueeze(1).to_broadcast([P, len(heads), WK - c0]),
                                     start=True, stop=False, skip_group_check=True)
                    for n, h in enumerate(heads):
                        rows = slice(64 * (h % 2), 64 * (h % 2) + 64)
                        last = nc.tensor.matmul(blocks[:, n, c0:WK], qTl[rows, t % 2, h // 2, :],
                                                kTl[rows, h // 2, k0:(t + 1) * P],
                                                start=False, stop=(n == len(heads) - 1), skip_group_check=True)
                elif kind == "pt":
                    if at[1] == 0:
                        exped.wait(pe, it, (t, len(SCORE_HEADS) - 1))
                    for c in range(4):
                        last = nc.tensor.transpose(ps[:, c * P:(c + 1) * P], probl[:, t % 2, 4 * at[1] + c, WIN:WK], ident[:, :])
                elif kind == "pp":
                    settle(pe, passed)
                    for h in range(HL):
                        last = nc.tensor.transpose(ps[0:WIN, h * WIN:(h + 1) * WIN], probl[0:WIN, t % 2, h, 0:WIN],
                                                   ident[0:WIN, 0:WIN])
                elif kind == "o":
                    if at[1] == 0:
                        turned_v.wait(pe, it, (t, 2))
                        turned_s.wait(pe, it, (t, "pp" if t else 3))
                        vcopied.wait(pe, it, (t, 1))
                    a, b = OUT_HEADS[at[1]]
                    width = EL + 1
                    for h in range(a, b):
                        last = nc.tensor.matmul(ps[:, (h - a) * width:(h - a + 1) * width], pT[:, h, :], vl[:, t, h, :],
                                                start=(h == a), stop=(h == b - 1 and t == 0), skip_group_check=True)
                    if t:
                        for h in range(a, b):
                            last = nc.tensor.matmul(ps[0:WIN, (h - a) * width:(h - a + 1) * width],
                                                    pP[P - WIN:P, h, :], vl[P - WIN:P, t - 1, h, :],
                                                    start=False, stop=(h == b - 1), skip_group_check=True)
                elif kind == "ot":
                    o_ready.wait(pe, it, (t, 2))
                    for c in range(4):
                        n = 4 * at[1] + c
                        last = nc.tensor.transpose(ps[:, c * P:(c + 1) * P], on[:, t % 2, n * P:(n + 1) * P], ident[:, :])
                elif kind == "y":
                    pe.wait_ge(o_loaded, o_layers(it))
                    ocopied.wait(pe, it, (t, 1))
                    for c in range(PAIRSL):
                        last = nc.tensor.matmul(ps[:, 0:P], wol[:, c, :], oTl[:, t % 2, c, :],
                                                start=(c == 0), stop=(c == PAIRSL - 1))
                elif kind == "xt":
                    mid.wait(pe, it, T - 1)
                    for c in range(T):
                        last = nc.tensor.transpose(ps[:, c * P:(c + 1) * P], xm[:, c * P:(c + 1) * P], ident[:, :])
                elif kind == "xn":
                    ffn.wait(pe, it, "x2")
                    for c in range(T):
                        last = nc.tensor.transpose(ps[:, c * P:(c + 1) * P], x2[:, c, :], ident[:, :])
                elif kind in ("gate", "up"):
                    if key == ("gate", 0):
                        ffn.wait(pe, it, "x2T")
                    col = (DI if kind == "gate" else 0) + sum(CW[:t])
                    last = nc.tensor.matmul(ps[0:CW[t], :], w1l[:, col:col + CW[t]], x2T[:, :], start=True, stop=True)
                else:
                    hidden.wait(pe, it, 2)
                    for c, m in enumerate(CW):
                        last = nc.tensor.matmul(ps[:, :], w2l[0:m, c, :], hf[0:m, c, :], start=(c == 0), stop=(c == 2))
                ring.steps.done(last, key)

            with pe.Fori(0, DEPTH) as l:
                o_layers = lambda it: l * 16 + 16
                with pe.Fori(0, B) as s:
                    it = l * B + s
                    pe.wait_ge(qkv_loaded, l * 48 + 48)
                    fetched.wait(pe, it, "xw")
                    for key in order:
                        if key == ("xt",):
                            pe.wait_ge(ffn_loaded, (l + 1) * (16 * FFN_LOADS))
                        fill(it, key)

        @block.scalar
        def _(act):
            for s in (squared, vcopied, rooted, tcopied, exped, turned_s, ocopied, gelued):
                s.prime(act)
            act.wait_ge(made, 2)
            chain = Chain(act, rlink, T + 1)

            def read(it, key):
                kind, at = key[0], key[1:]
                t = at[0] if at else 0
                if kind in ("up", "y2", "y", "o", "xn") or (kind == "pt" and at[1] % 2 == 0):
                    return
                ps = psum[ring.full(act, it, key)]
                if kind == "qk":
                    parts.wait(act, it, at)
                    n = 4 * t + at[1]
                    if n >= 2:
                        summed.wait(act, it, pieces[n - 2])
                    else:
                        summed.wait_before(act, it, pieces[n - 2])
                    squared.done(nc.scalar.activation(sq[:, n % 2, :], ps[:, :], ACT.Square), at)
                elif kind == "v":
                    vcopied.done(nc.scalar.copy(vl[:, t, 8 * at[1]:8 * at[1] + 8, 0:EL],
                                                ps[:, :].rearrange("p (h c) -> p h c", c=EL)), at)
                    if at[1] == 1:
                        clamped.wait(act, it, t)
                        chain.link(it, nc.scalar.activation(lns[:, :], ssc[:, t % 2, :], ACT.Ln))
                        rooted.done(nc.scalar.activation(rn[:, t % 2, :], lns[:, :], ACT.Exp, scale=-0.5,
                                                         bias=sh.lnt[:, 0:1]), t)
                elif kind == "t":
                    src = ps[:, :].rearrange("p (c n) -> p c n", n=P)
                    dst = qTl[:, t % 2, 4 * at[1]:4 * at[1] + 4, :] if at[1] < 2 else \
                        kTl[:, 4 * at[1] - 8:4 * at[1] - 4, t * P:(t + 1) * P]
                    tcopied.done(nc.scalar.copy(dst, src), at)
                elif kind == "s":
                    maxed.wait(act, it, at)
                    _, c0 = keys0(t)
                    for n, h in enumerate(SCORE_HEADS[at[1]]):
                        col = 3 * at[1] + n - (at[1] == 5)
                        last = nc.scalar.activation(probl[:, t % 2, h, c0:WK], ps[:, n * WK + c0:(n + 1) * WK], ACT.Exp,
                                                    bias=negmaxl[:, t % 2, col:col + 1])
                    exped.done(last, at)
                elif kind == "pt":
                    turned_s.done(nc.scalar.copy(pT[:, 4 * at[1]:4 * at[1] + 4, :], ps[:, :].rearrange("p (h n) -> p h n", n=P)), at)
                elif kind == "pp":
                    turned_s.done(nc.scalar.copy(pP[P - WIN:P, :, :], ps[0:WIN, :].rearrange("p (h n) -> p h n", n=WIN)), (t, "pp"))
                elif kind == "ot":
                    ocopied.done(nc.scalar.copy(oTl[:, t % 2, 4 * at[1]:4 * at[1] + 4, :],
                                                ps[:, :].rearrange("p (c n) -> p c n", n=P)), at)
                elif kind == "xt":
                    ffn.wait(act, it, "var")
                    chain.link(it, nc.scalar.activation(lnv[:, :], mv[:, :, 1], ACT.Ln, bias=sh.eps5[:, 0:1]))
                    rooted.done(nc.scalar.activation(rstd[:, :], lnv[:, :], ACT.Exp, scale=-0.5), "ffn")
                elif kind == "gate":
                    if t == 2:
                        hidden.wait(act, it, 0)
                    m = CW[t]
                    gelued.done(nc.scalar.activation(gel[0:m, t % 2, :], ps[0:m, :], ACT.Gelu, bias=b1l[0:m, 1, t:t + 1]), t)

            with act.Fori(0, DEPTH) as l:
                with act.Fori(0, B) as s:
                    it = l * B + s
                    for key in order:
                        if key == ("gate", 0):
                            act.wait_ge(ffn_loaded, (l + 1) * (16 * FFN_LOADS))
                        read(it, key)
                    chain.end()

        @block.vector
        def _(dve):
            for s in (parts, summed, clamped, maxed, turned_v, o_ready, mid, ffn, hidden, left):
                s.prime(dve)
            dve.wait_ge(made, 2)
            V = nc.vector
            chain = Chain(dve, link, LINKS1)
            HALF = D // 2

            def unshift(ins_of, it_rows=((0, HALF, 0), (HALF, D, 1))):
                for a, b, d in it_rows:
                    last = ins_of(a, b, d)
                return last

            def sum_squares(it, piece):
                squared.wait(dve, it, piece)
                j = piece[1]
                summed.done(V.tensor_reduce(ss[:, 8 * j:8 * j + 8], sq[:, j % 2, :].rearrange("p (h c) -> p h c", c=EL),
                                            AX.X, ALU.add), piece)

            def read(it, s, key):
                kind, at = key[0], key[1:]
                t = at[0] if at else 0
                if kind == "v" and at[1] == 0:
                    sum_squares(it, (t, 3))
                    summed.wait(dve, it, (t, 3))
                    clamped.done(V.tensor_scalar(ssc[:, t % 2, :], ss[:, :], 1e-24, TINY, ALU.max, ALU.mult), t)
                if kind in ("v", "t", "pp", "ot", "gate") or (kind == "pt" and at[1] % 2):
                    return
                ps = psum[ring.full(dve, it, key)]
                if kind == "qk":
                    j = at[1]
                    if t >= 2:
                        rotated.wait(dve, it, (t - 2, j))
                    else:
                        rotated.wait_before(dve, it, (t + 2, j))
                    table = 2 * (j // 2)
                    heads = ps[:, :].rearrange("p (h two c) -> p h two c", two=2, c=EL // 2)
                    by_head = lambda a: a.rearrange("p (h c) -> p h c", c=EL)
                    wide = lambda a: a.unsqueeze(1).to_broadcast([P, 8, EL])
                    V.tensor_tensor(by_head(cosd[:, t % 2, j, :]), by_head(ps[:, :]), wide(rots[:, table, t, :]), ALU.mult)
                    halves = lambda a: a.rearrange("p h (two c) -> p h two c", two=2)
                    parts.done(V.tensor_tensor(halves(by_head(sind[:, t % 2, j, :])), heads[:, :, ::-1, :],
                                               halves(wide(rots[:, table + 1, t, :])), ALU.mult), at)
                    if j:
                        sum_squares(it, (t, j - 1))
                elif kind == "s":
                    _, c0 = keys0(t)
                    nh = len(SCORE_HEADS[at[1]])
                    col = 3 * at[1] - (at[1] == 5)
                    blocks = ps[:, 0:nh * WK].rearrange("p (h k) -> p h k", k=WK)
                    maxed.done(V.tensor_reduce(negmaxl[:, t % 2, col:col + nh], blocks[:, :, c0:WK], AX.X, ALU.max, negate=True), at)
                elif kind == "pt":
                    turned_v.done(V.tensor_copy(pT[:, 4 * at[1]:4 * at[1] + 4, :], ps[:, :].rearrange("p (h n) -> p h n", n=P)), at)
                elif kind == "o":
                    a, b = OUT_HEADS[at[1]]
                    width = EL + 1
                    blocks = ps[:, 0:(b - a) * width].rearrange("p (h c) -> p h c", c=width)
                    chain.link(it, V.reciprocal(rs[:, t % 2, a:b], blocks[:, :, EL]))
                    o_ready.done(V.tensor_tensor(on[:, t % 2, a * EL:b * EL].rearrange("p (h c) -> p h c", c=EL),
                                                 blocks[:, :, 0:EL],
                                                 rs[:, t % 2, a:b].unsqueeze(2).to_broadcast([P, b - a, EL]), ALU.mult), at)
                elif kind == "y":
                    last = unshift(lambda a, b, d: V.tensor_tensor(xm[a:b, t * P + d:(t + 1) * P + d], ps[a:b, 0:P],
                                                                   xw[a:b, t * P + d:(t + 1) * P + d], ALU.add))
                    mid.done(last, t)
                elif kind == "xt":
                    for c in range(T):
                        last = V.bn_stats(stats[:, c, :], ps[:, c * P:(c + 1) * P])
                    chain.link(it, last)
                    settle(dve, passed)
                    for c in range(T):
                        last = V.bn_aggr(mv[:, c, :], stats[:, c, :])
                    ffn.done(last, "var")
                    ffn.wait(dve, it, "var")
                    rooted.wait(dve, it, "ffn")
                    for c in range(T):
                        last = V.tensor_scalar(x2[:, c, :], ps[:, c * P:(c + 1) * P], mv[:, c, 0:1], rstd[:, c:c + 1],
                                               ALU.subtract, ALU.mult)
                    ffn.done(last, "x2")
                elif kind == "xn":
                    ffn.done(V.tensor_scalar(x2T[:, :], ps[:, :], lng[:, 0:1], lnb[:, 0:1], ALU.mult, ALU.add), "x2T")
                elif kind == "up":
                    m = CW[t]
                    gelued.wait(dve, it, t)
                    hidden.done(V.scalar_tensor_tensor(out=hf[0:m, t, :], in0=ps[0:m, :], scalar=b1l[0:m, 0, t:t + 1],
                                                       in1=gel[0:m, t % 2, :], op0=ALU.add, op1=ALU.mult), t)
                else:
                    last = unshift(lambda a, b, d: V.scalar_tensor_tensor(
                        out=state[a:b, bass.ds(s, 1), d:N + d].rearrange("p s n -> p (s n)"), in0=ps[a:b, :],
                        scalar=b2l[a:b, 0:1], in1=xm[a:b, d:N + d], op0=ALU.add, op1=ALU.add))
                    left.done(last, "state")

            with dve.Fori(0, DEPTH) as l:
                with dve.Fori(0, B) as s:
                    it = l * B + s
                    dve.wait_ge(scaled, l * 4 + 8)
                    for key in order:
                        if key == ("xn",):
                            dve.wait_ge(ffn_loaded, (l + 1) * (16 * FFN_LOADS))
                        read(it, s, key)
                    chain.end()


def pass2(nc, io, sh, ctx):
    ident, state, psum = sh.ident, sh.state, sh.psum

    def sb(name, shape, dt=F32):
        return ctx.enter_context(nc.sbuf_tensor(name, shape, dt))

    def sem(name):
        return ctx.enter_context(nc.semaphore(name))

    xf, sums, out = sb("xf", [P, N]), sb("sums_in", [P, T, D]), sb("outs", [P, T, D])
    straight, turned, added, loaded, stored, passed = (sem(n) for n in ("straight", "turned", "added", "loaded",
                                                                         "stored2", "passed2"))
    tokens = "s (t p) d -> p (s t) d"
    with nc.Block() as block:
        @block.sync
        def _(sp):
            sp.sem_inc(stored, 16)
            with sp.Fori(0, B) as s:
                sp.wait_ge(added, s + 1)
                settle(sp, passed)
                sp.dma_start(sums[:, :, :], io["sums"][bass.ds(s, 1)].rearrange(tokens, p=P)).then_inc(loaded, 16)
                sp.wait_ge(added, s + 2)
                settle(sp, passed)
                sp.dma_start(io["out"][bass.ds(s, 1)].rearrange(tokens, p=P), out[:, :, :]).then_inc(stored, 16)
            sp.wait_ge(stored, 16 * B + 16)

        @block.scalar
        def _(act):
            with act.Fori(0, B) as s:
                act.wait_ge(turned, s + 1)
                one = bass.ds(s, 1)
                nc.scalar.copy(xf[0:D // 2, :], state[0:D // 2, one, 0:N].rearrange("p s n -> p (s n)"))
                nc.scalar.copy(xf[D // 2:D, :], state[D // 2:D, one, 1:N + 1].rearrange("p s n -> p (s n)")
                               ).then_inc(straight, 1)

        @block.tensor
        def _(pe):
            pe.sem_inc(turned, 1)
            with pe.Fori(0, B) as s:
                pe.wait_ge(straight, s + 1)
                pe.wait_ge(added, s + 1)
                for t in range(T):
                    last = nc.tensor.transpose(psum[0][:, t * P:(t + 1) * P], xf[:, t * P:(t + 1) * P], ident[:, :])
                last.then_inc(turned, 1)

        @block.vector
        def _(dve):
            dve.sem_inc(added, 1)
            with dve.Fori(0, B) as s:
                dve.wait_ge(turned, s + 2)
                dve.wait_ge(loaded, s * 16 + 16)
                dve.wait_ge(stored, s * 16 + 16)
                nc.vector.tensor_tensor(out[:, :, :], psum[0][:, :].rearrange("p (t d) -> p t d", t=T), sums[:, :, :],
                                        ALU.add).then_inc(added, 1)


LINKS0 = 59
LINKS1 = 13


def build(nc, io):
    with ExitStack() as ctx:
        sh = Shared(nc, ctx)
        with ExitStack() as inner:
            pass0(nc, io, sh, inner)
        with ExitStack() as inner:
            pass1(nc, io, sh, inner)
        with ExitStack() as inner:
            pass2(nc, io, sh, inner)


def rotary():
    f = np.float32
    half = np.arange(0, EL, 2, dtype=f)
    inv_freq = (f(1.0) / f(10000.0) ** (half / f(EL))).astype(f)
    tok = np.arange(N, dtype=f)
    freqs = tok[:, None] * inv_freq[None, :]
    freqs = np.concatenate([freqs, freqs], -1).astype(np.float64)
    base = ((half + f(0.4 * EL)) / f(1.4 * EL)).astype(np.float64)
    power = (tok - N // 2) / (WIN // 2)
    scale = base[None, :] ** power[:, None].astype(np.float64)
    scale = np.concatenate([scale, scale], -1)
    cos, sin = np.cos(freqs), np.sin(freqs)
    sin[:, :EL // 2] *= -1
    tables = np.stack([QK_SCALE * cos * scale, QK_SCALE * sin * scale, cos / scale, sin / scale])
    return np.ascontiguousarray(tables.reshape(4, T, P, EL).transpose(2, 0, 1, 3).astype(f))


def masks():
    q, k = np.arange(P)[:, None], np.arange(P)[None, :]
    causal = np.where(k <= q, 0.0, NEG)
    r = np.arange(WIN + P)[None, :] - WIN
    window = np.where((r <= q) & (q <= r + WIN), 0.0, NEG)
    return causal.astype(np.float32), window.astype(np.float32)


def kernel(**inputs):
    from concourse import bacc
    from concourse.bass_utils import run_bass_kernel_spmd

    a = {k: np.asarray(v) for k, v in inputs.items()}
    f = np.float32
    causal, window = masks()
    pick = np.zeros((EXPERTS, CH0, P), f)
    for e in range(EXPERTS):
        pick[e, e // 2, (e % 2) * INTER:(e % 2 + 1) * INTER] = 1.0
    earlier = lambda n: np.tril(np.ones((n, n), f), -1)

    def quadrants(w):
        out = np.zeros((D, HG, HG, 32), f)
        out[:, :, :, :E1] = w.T.reshape(D, HG, HG, E1)
        return out.reshape(D, HG, P)

    flat = lambda w: w.transpose(1, 0, 2).reshape(D, H0 * E0)
    up = lambda w, shared: np.concatenate([w.reshape(EXPERTS * INTER, D), shared], 0).T
    arrays = {
        "ident": np.eye(P, dtype=f), "maskc": causal, "maskw": window, "sel": pick,
        "tie16": earlier(EXPERTS), "tie4": earlier(GROUPS), "rot": rotary(),
        "x": a["L0_attn_tokens"],
        "wq0": flat(a["L0_attn_wq"]), "wk0": flat(a["L0_attn_wk"]), "wv0": flat(a["L0_attn_wv"]),
        "wo0": a["L0_attn_wo"].reshape(PAIRS0, P, D).transpose(1, 0, 2),
        "wgates": a["L0_attn_w_gates"], "wroute": a["L0_ffn_gate_w"].T,
        "rmsw": a["L0_attn_rms_w"].reshape(D, 1), "gbias": a["L0_ffn_gate_bias"],
        "w1": up(a["L0_ffn_w1"], a["L0_ffn_ws1"]), "w3": up(a["L0_ffn_w3"], a["L0_ffn_ws3"]),
        "w2": a["L0_ffn_w2"].transpose(0, 2, 1).reshape(CH0, P, D).transpose(1, 0, 2), "ws2": a["L0_ffn_ws2"].T,
        "wq1": quadrants(a["L1_attn_Wq"]), "wk1": quadrants(a["L1_attn_Wk"]),
        "wv1": a["L1_attn_Wv"].T, "wo1": a["L1_attn_Wo"].T,
        "wqkv": a["L1_ffn_Wqkv"], "qs": a["L1_ffn_q_scale"], "ks": a["L1_ffn_k_scale"], "wol": a["L1_ffn_Wo"],
        "lng": a["L1_ffn_ln_g"], "lnb": a["L1_ffn_ln_b"], "w1l": a["L1_ffn_W1"], "b1l": a["L1_ffn_b1"],
        "w2l": a["L1_ffn_W2"], "b2l": a["L1_ffn_b2"],
    }
    arrays = {f"in_{k}": np.ascontiguousarray(v) for k, v in arrays.items()}
    nc = bacc.Bacc("TRN2", target_bir_lowering=False, num_devices=1)
    io = {k[3:]: nc.dram_tensor(k, v.shape, mybir.dt.from_np(v.dtype), kind="ExternalInput").ap()
          for k, v in arrays.items()}
    io["out"] = nc.dram_tensor("out", (B, N, D), F32, kind="ExternalOutput").ap()
    io["sums"] = nc.dram_tensor("sums", (B, N, D), F32, kind="Internal").ap()
    build(nc, io)
    r = run_bass_kernel_spmd(nc, [arrays], core_ids=[0])
    return r.results[0]["out"]
```

```python
from contextlib import ExitStack

import numpy as np

import concourse.bass as bass
from concourse import mybir

F32 = mybir.dt.float32
BF16 = mybir.dt.bfloat16
ALU = mybir.AluOpType
ACT = mybir.ActivationFunctionType
AX = mybir.AxisListType

P = 128
D = 128
B, N = 8, 512
T = N // P
NEG = -1.0e30
BANKS, BANK = 8, 512

H0, E0 = 8, 64
PAIRS0 = H0 * E0 // P
EXPERTS, INTER, GROUPS, TOPK, TOPG = 16, 64, 4, 4, 2
CH0 = EXPERTS * INTER // P
H1, E1 = 16, 8
HG = 4
DEPTH, HL, EL, WIN = 6, 16, 64, 32
INNER = HL * EL
PAIRSL = INNER // P
DI = int(D * 4 * 2 / 3)
CW = [114, 114, 113]
QK_SCALE = 8.0
LN_EXP = "natural_log_exp_and_others"
TINY = 2.0 ** 24
LN_TINY_HALF = 12.0 * float(np.log(2.0))



class Steps:

    def __init__(self, sem, keys):
        self.sem, self.keys = sem, list(keys)
        self.at = {k: n + 1 for n, k in enumerate(self.keys)}
        self.n = len(self.keys)
        assert len(self.at) == self.n
        self.sent = 0

    def prime(self, eng):
        eng.sem_inc(self.sem, self.n)

    def value(self, it, key):
        return (it + 1) * self.n + self.at[key]

    def before(self, it, key):
        return it * self.n + self.at[key]

    def wait(self, eng, it, key):
        eng.wait_ge(self.sem, self.value(it, key))

    def wait_before(self, eng, it, key):
        eng.wait_ge(self.sem, self.before(it, key))

    def done(self, ins, key):
        assert self.keys[self.sent % self.n] == key, (key, self.keys[self.sent % self.n])
        self.sent += 1
        ins.then_inc(self.sem, 1)


def settle(eng, passed):
    eng.sem_inc(passed, 1)


class Ring:

    def __init__(self, filled, slots, banks=BANKS):
        self.steps = Steps(filled, [key for key, _ in slots])
        self.banks = banks
        self.index = {key: n for n, (key, _) in enumerate(slots)}
        self.readers = [r for _, r in slots]

    def bank(self, key):
        return self.index[key] % self.banks

    def take(self, pe, it, key):
        n = self.index[key]
        if n >= self.banks:
            for steps, k in self.readers[n - self.banks]:
                steps.wait(pe, it, k)
        else:
            last = max(m for m in range(len(self.readers)) if m % self.banks == n % self.banks)
            for steps, k in self.readers[last]:
                steps.wait_before(pe, it, k)
        return self.bank(key)

    def full(self, eng, it, key):
        self.steps.wait(eng, it, key)
        return self.bank(key)


class Chain:

    def __init__(self, eng, sem, n):
        self.eng, self.sem, self.n, self.sent = eng, sem, n, 0

    def link(self, it, ins):
        ins.then_inc(self.sem, 1)
        self.sent += 1
        self.eng.wait_ge(self.sem, it * self.n + self.sent)

    def end(self):
        assert self.sent == self.n, self.sent
        self.sent = 0


def units_of(heads):
    return [(h, i) for h in range(heads) for i in range(T)]


TURN_LAG, PV_LAG = 4, 6
PROBS, PROBTS = 6, 3
SUMS = 8


def causal_order(heads):
    units = units_of(heads)
    for n in range(len(units) + PV_LAG):
        if n < len(units):
            yield "score", n
        if n - TURN_LAG in range(len(units)):
            yield "turn", n - TURN_LAG
        if n >= PV_LAG:
            yield "pv", n - PV_LAG


SCORE_HEADS = [(0, 3), (3, 6), (6, 9), (9, 12), (12, 14), (14, 16)]


def order1():
    def project(t):
        return [("qk", t, j) for j in range(4)] + [("v", t, j) for j in range(2)]

    def turn(t):
        return [("t", t, j) for j in range(4)]

    def score(t):
        return [("s", t, g) for g in range(6)]

    def weigh(t):
        out = [("pt", t, k) for k in range(4)] + ([("pp", t)] if t else [])
        return out + [("o", t, n) for n in range(2)]

    out = project(0) + project(1) + turn(0) + score(0)
    out += project(2) + turn(1) + score(1) + weigh(0)
    out += project(3) + turn(2) + score(2) + weigh(1)
    out += turn(3) + score(3) + weigh(2) + weigh(3)
    out += [("y",), ("xt",), ("xn",)]
    for c in range(3):
        out += [("gate", c), ("up", c)]
    return out + [("y2",)]




class Shared:

    def __init__(self, nc, ctx):
        def sb(name, shape, dt=F32):
            return ctx.enter_context(nc.sbuf_tensor(name, shape, dt))

        self.ident = sb("ident", [P, P])
        self.identb = sb("identb", [P, P], BF16)
        self.maskc = sb("maskc", [P, P], BF16)
        self.maskw = sb("maskw", [P, WIN + P], BF16)
        self.eps5 = sb("eps5", [P, 1])
        self.epst = sb("epst", [P, 1])
        self.lnt = sb("lnt", [P, 1])
        self.state = sb("state", [P, B, N + 1])
        self.psum = [ctx.enter_context(nc.psum_tensor(f"psum{b}", [P, BANK], F32)) for b in range(BANKS)]


def pass0(nc, io, sh, ctx):
    ident, identb, maskc, state, psum = sh.ident, sh.identb, sh.maskc, sh.state, sh.psum
    eps5, epst = sh.eps5, sh.epst

    def sb(name, shape, dt=F32):
        return ctx.enter_context(nc.sbuf_tensor(name, shape, dt))

    def sem(name):
        return ctx.enter_context(nc.semaphore(name))

    def steps(name, keys):
        return Steps(sem(name), keys)

    GR = H0 + EXPERTS
    maskc_f, maskw_f = sb("maskc_f", [P, P]), sb("maskw_f", [P, WIN + P])
    wq, wk, wv = (sb(n, [P, H0 * E0]) for n in ("wq", "wk", "wv"))
    wo = sb("wo", [P, PAIRS0, D])
    wgr = sb("wgr", [P, GR])
    rmsw, gbias = sb("rmsw", [P, 1]), sb("gbias", [P, EXPERTS])
    w1, w3 = sb("w1", [P, (EXPERTS + 1) * INTER]), sb("w3", [P, (EXPERTS + 1) * INTER])
    w2 = sb("w2", [P, CH0 + 1, D])
    sel = sb("sel", [EXPERTS, CH0, P])
    tie16, tie4 = sb("tie16", [P, EXPERTS, EXPERTS]), sb("tie4", [P, GROUPS, GROUPS])
    headmask = sb("headmask", [P, H1])
    wq1, wk1 = sb("wq1", [P, D]), sb("wk1", [P, D])
    wv1, wo1 = sb("wv1", [P, D]), sb("wo1", [P, D])

    x, xn, tn = (sb(n, [P, T, D]) for n in ("x", "xn", "tn"))
    square = sb("square", [P, T, D])
    stats, mv = sb("stats", [P, T, 6]), sb("mv", [P, T, 2])
    lnv, rstd, ms, lnm, rrms = (sb(n, [P, T]) for n in ("lnv", "rstd", "ms", "lnm", "rrms"))
    xnT, tT = sb("xnT", [P, N]), sb("tT", [P, N])
    egr, sig = sb("egr", [P, T, GR]), sb("sig", [P, T, GR])
    biased, gmax = sb("biased", [P, T, EXPERTS]), sb("gmax", [P, T, GROUPS])
    gt4, eq4 = sb("gt4", [P, T, GROUPS, GROUPS]), sb("eq4", [P, T, GROUPS, GROUPS])
    rank4, keep, pen = (sb(n, [P, T, GROUPS]) for n in ("rank4", "keep", "pen"))
    kept = sb("kept", [P, T, EXPERTS])
    gt16, eq16 = sb("gt16", [P, T, EXPERTS, EXPERTS]), sb("eq16", [P, T, EXPERTS, EXPERTS])
    rank16, comb = sb("rank16", [P, T, EXPERTS]), sb("comb", [P, T, EXPERTS])
    combT = sb("combT", [EXPERTS, N])
    qz = sb("qz", [P, H0, N])
    kT = sb("kT", [P, PAIRS0, N])
    v = sb("v", [P, T, H0 * E0])
    negmax = sb("negmax", [P, SUMS])
    prob, probT = sb("prob", [P, PROBS, N]), sb("probT", [P, PROBTS, N])
    sums, rsum = sb("psums", [P, SUMS]), sb("rsum", [P, SUMS])
    oT = sb("oT", [P, PAIRS0, N])
    act1, prod, hT = sb("act1", [P, 2, N]), sb("prod", [P, 2, N]), sb("hT", [P, CH0 + 1, N])
    x1, x1n, x1T = sb("x1", [P, T, D]), sb("x1n", [P, T, D]), sb("x1T", [P, N])
    qT1, kT1 = sb("qT1", [P, N]), sb("kT1", [P, N])
    qz1 = sb("qz1", [P, HG, N])
    v1z = sb("v1z", [P, T, H1, 32])
    oT1, sumout = sb("oT1", [P, N]), sb("sumout", [P, T, D])

    ua, ub = units_of(H0), units_of(H1)
    units = [("a", n) for n in range(len(ua))] + [("b", n) for n in range(len(ub))]
    const_loaded, const_made, x_loaded, stored = sem("const_loaded"), sem("const_made"), sem("x_loaded"), sem("stored")
    measured = steps("measured", ["var", "ms", "var1"])
    normed = steps("normed", ["xn", "tn", "x1n"])
    maxed = steps("maxed", units)
    turned_v = steps("turned_v", [u for u in units if u[1] % 2 == 0])
    inverted = steps("inverted", units)
    moved = steps("moved", ["tT", "sig", "comb", "x1", "sum"])
    gated = steps("gated", range(CH0 + 1))
    rooted = steps("rooted", ["rstd", "rrms", "rstd1"])
    copied = steps("copied", ["xnT", "gr"] + [(a, p) for p in range(PAIRS0) for a in "qk"]
                   + [("v", t) for t in range(T)] + [("ot", p) for p in range(PAIRS0)] + ["ct"]
                   + ["x1T", "q1", "k1", "v1", "ot1"])
    spread = steps("spread", range(H1))
    exped = steps("exped", units)
    turned_s = steps("turned_s", [u for u in units if u[1] % 2 == 1])
    silued = steps("silued", range(CH0 + 1))
    scaled = steps("scaled0", units)
    outs = steps("outs", [("a", p) for p in range(PAIRS0)] + [("b", 0)])
    link, rlink, passed = sem("link"), sem("rlink"), sem("passed")

    def causal_slots(tag, heads):
        for what, n in causal_order(heads):
            if what == "score":
                yield (tag + "s", n), [(exped, (tag, n))]
            elif what == "turn":
                yield (tag + "pt", n), [(turned_v if n % 2 == 0 else turned_s, (tag, n))]

    slots = [("xt", [(copied, "xnT")]), ("tt", [(moved, "tT")]), ("gr", [(copied, "gr")])]
    slots += [((a, p), [(copied, (a, p))]) for p in range(PAIRS0) for a in "qk"]
    slots += [(("v", t), [(copied, ("v", t))]) for t in range(T)]
    slots += list(causal_slots("a", H0))
    slots += [("ct", [(copied, "ct")])]
    for c in range(CH0):
        slots += [(("h1", c), [(silued, c)]), (("h3", c), [(gated, c)]), (("cb", c), [(gated, c)])]
    slots += [(("h1", CH0), [(silued, CH0)]), (("h3", CH0), [(gated, CH0)])]
    slots += [("y", [(moved, "x1")]), ("x1t", [(copied, "x1T")])]
    slots += [(a, [(copied, a)]) for a in ("q1", "k1", "v1")]
    slots += list(causal_slots("b", H1))
    slots += [("y1", [(moved, "sum")])]
    ring = Ring(sem("filled"), slots, BANKS - 2)
    out_bank = lambda tag, p: BANKS - 2 + (p % 2 if tag == "a" else 0)
    out_before = {("a", 2): ("ot", 0), ("a", 3): ("ot", 1), ("b", 0): ("ot", 2)}
    out_before_it = {("a", 0): "ot1", ("a", 1): ("ot", 3)}

    def chunk(c):
        return P if c < CH0 else INTER

    loads = [(ident, "ident"), (maskc_f, "maskc"), (maskw_f, "maskw"), (wq, "wq0"), (wk, "wk0"), (wv, "wv0"),
             (wo, "wo0"), (rmsw, "rmsw"), (w1, "w1"), (w3, "w3"), (sel, "sel"), (headmask, "headmask"), (wq1, "wq1"), (wk1, "wk1"),
             (wv1, "wv1"), (wo1, "wo1")]
    ALL_LOADED = 16 * (len(loads) + 7)
    ALL_MADE = 9

    with nc.Block() as block:
        @block.sync
        def _(sp):
            for dst, name in loads:
                sp.dma_start(dst[tuple(slice(None) for _ in dst.shape)], io[name]).then_inc(const_loaded, 16)
            sp.dma_start(wgr[:, 0:H0], io["wgates"]).then_inc(const_loaded, 16)
            sp.dma_start(wgr[:, H0:GR], io["wroute"]).then_inc(const_loaded, 16)
            sp.dma_start(gbias[:, :], io["gbias"].partition_broadcast(P)).then_inc(const_loaded, 16)
            sp.dma_start(tie16[:, :, :], io["tie16"].partition_broadcast(P)).then_inc(const_loaded, 16)
            sp.dma_start(tie4[:, :, :], io["tie4"].partition_broadcast(P)).then_inc(const_loaded, 16)
            sp.dma_start(w2[:, 0:CH0, :], io["w2"]).then_inc(const_loaded, 16)
            sp.dma_start(w2[0:INTER, CH0, :], io["ws2"]).then_inc(const_loaded, 16)
            sp.sem_inc(stored, 16)
            with sp.Fori(0, B) as it:
                moved.wait_before(sp, it, "x1")
                settle(sp, passed)
                sp.dma_start(x[:, :, :], io["x"][bass.ds(it, 1)].rearrange("s (t p) d -> p (s t) d", p=P)
                             ).then_inc(x_loaded, 16)
                moved.wait(sp, it, "sum")
                settle(sp, passed)
                sp.dma_start(io["sums"][bass.ds(it, 1)].rearrange("s (t p) d -> p (s t) d", p=P), sumout[:, :, :]
                             ).then_inc(stored, 16)
            sp.wait_ge(stored, 16 * B + 16)

        @block.gpsimd
        def _(pool):
            for dst, value in ((eps5[:, :], 1e-5), (epst[:, :], float(np.finfo(np.float32).eps)),
                               (sh.lnt[:, :], LN_TINY_HALF), (qz[:, :, :], 0.0),
                               (v1z[:, :, :, :], 0.0), (state[:, :, :], 0.0)):
                nc.gpsimd.memset(dst, value).then_inc(const_made, 1)
            pool.wait_ge(const_loaded, ALL_LOADED)
            nc.gpsimd.tensor_copy(identb[:, :], ident[:, :]).then_inc(const_made, 1)
            nc.gpsimd.tensor_copy(maskc[:, :], maskc_f[:, :]).then_inc(const_made, 1)
            nc.gpsimd.tensor_copy(sh.maskw[:, :], maskw_f[:, :]).then_inc(const_made, 1)
            scaled.prime(pool)

            def causal(it, tag, heads):
                for n, (h, i) in enumerate(units_of(heads)):
                    p = prob[:, n % PROBS, 0:(i + 1) * P]
                    inverted.wait(pool, it, (tag, n))
                    settle(pool, passed)
                    r = rsum[:, n % SUMS:n % SUMS + 1]
                    if tag == "a":
                        ins = nc.gpsimd.tensor_scalar(p, p, r, sig[:, i, h:h + 1], ALU.mult, ALU.mult)
                    else:
                        ins = nc.gpsimd.tensor_scalar(p, p, r, None, ALU.mult)
                    scaled.done(ins, (tag, n))

            with pool.Fori(0, B) as it:
                moved.wait(pool, it, "sig")
                causal(it, "a", H0)
                causal(it, "b", H1)

        @block.tensor
        def _(pe):
            ring.steps.prime(pe)
            outs.prime(pe)
            pe.wait_ge(const_loaded, ALL_LOADED)
            pe.wait_ge(const_made, ALL_MADE)

            def take(it, key):
                return psum[ring.take(pe, it, key)]

            def turn4(it, key, src):
                ps = take(it, key)
                for t in range(T):
                    last = nc.tensor.transpose(ps[:, t * P:(t + 1) * P], src(t), ident[:, :])
                ring.steps.done(last, key)

            def product(it, key, lhsT, rhs, m=P):
                ps = take(it, key)
                ring.steps.done(nc.tensor.matmul(ps[0:m, :], lhsT, rhs, start=True, stop=True), key)

            def causal(it, tag, heads, q_of, k_of, v_of):
                for what, n in causal_order(heads):
                    h, i = divmod(n, T)
                    nk = (i + 1) * P
                    if what == "score":
                        if tag == "b" and i == 0:
                            spread.wait(pe, it, h)
                        ps = take(it, (tag + "s", n))
                        nc.tensor.matmul(ps[:, 0:nk], q_of(h, i), k_of(h, nk), start=True, stop=False)
                        ring.steps.done(nc.tensor.matmul(ps[:, i * P:nk], identb[:, :], maskc[:, :],
                                                         start=False, stop=True), (tag + "s", n))
                    elif what == "turn":
                        scaled.wait(pe, it, (tag, n))
                        ps = take(it, (tag + "pt", n))
                        for j in range(i + 1):
                            last = nc.tensor.transpose(ps[:, j * P:(j + 1) * P], prob[:, n % PROBS, j * P:(j + 1) * P],
                                                       ident[:, :])
                        ring.steps.done(last, (tag + "pt", n))
                    else:
                        group, p = h // HG, h // 2 if tag == "a" else 0
                        rows = slice(64 * (h % 2), 64 * (h % 2) + 64) if tag == "a" else slice(32 * group, 32 * group + 32)
                        if i == 0 and (h % 2 == 0 if tag == "a" else h == 0):
                            if (tag, p) in out_before:
                                copied.wait(pe, it, out_before[tag, p])
                            else:
                                copied.wait_before(pe, it, out_before_it[tag, p])
                        first = i == 0 and (tag == "a" or h % HG == 0)
                        ps = psum[out_bank(tag, p)]
                        (turned_v if n % 2 == 0 else turned_s).wait(pe, it, (tag, n))
                        for j in range(i + 1):
                            last = nc.tensor.matmul(ps[rows, i * P:(i + 1) * P], v_of(h, j), probT[:, n % PROBTS, j * P:(j + 1) * P],
                                                    start=(first and j == 0), stop=(j == i), skip_group_check=True)
                        if i == T - 1 and (h % 2 == 1 if tag == "a" else h == heads - 1):
                            outs.done(last, (tag, p))

            with pe.Fori(0, B) as it:
                normed.wait(pe, it, "xn")
                turn4(it, "xt", lambda t: xn[:, t, :])
                normed.wait(pe, it, "tn")
                turn4(it, "tt", lambda t: tn[:, t, :])
                copied.wait(pe, it, "xnT")
                moved.wait(pe, it, "tT")
                ps = take(it, "gr")
                for t in range(T):
                    nc.tensor.matmul(ps[:, t * GR:t * GR + H0], tT[:, t * P:(t + 1) * P], wgr[:, 0:H0],
                                     start=True, stop=True)
                    last = nc.tensor.matmul(ps[:, t * GR + H0:(t + 1) * GR], xnT[:, t * P:(t + 1) * P], wgr[:, H0:GR],
                                            start=True, stop=True)
                ring.steps.done(last, "gr")
                for p in range(PAIRS0):
                    product(it, ("q", p), wq[:, p * P:(p + 1) * P], tT[:, :])
                    product(it, ("k", p), wk[:, p * P:(p + 1) * P], tT[:, :])
                for t in range(T):
                    product(it, ("v", t), tT[:, t * P:(t + 1) * P], wv[:, :])
                copied.wait(pe, it, ("v", T - 1))
                causal(it, "a", H0,
                       lambda h, i: qz[:, h, i * P:(i + 1) * P],
                       lambda h, nk: kT[:, h // 2, 0:nk],
                       lambda h, j: v[:, j, h * E0:(h + 1) * E0])
                moved.wait(pe, it, "comb")
                ps = take(it, "ct")
                for t in range(T):
                    last = nc.tensor.transpose(ps[0:EXPERTS, t * P:(t + 1) * P], comb[:, t, :], ident[:, :])
                ring.steps.done(last, "ct")
                copied.wait(pe, it, "ct")
                for c in range(CH0 + 1):
                    m = chunk(c)
                    product(it, ("h1", c), w1[:, c * P:c * P + m], xnT[:, :], m)
                    product(it, ("h3", c), w3[:, c * P:c * P + m], xnT[:, :], m)
                    if c < CH0:
                        product(it, ("cb", c), sel[:, c, :], combT[:, :])
                ps = take(it, "y")
                copied.wait(pe, it, ("ot", PAIRS0 - 1))
                gated.wait(pe, it, CH0)
                for t in range(T):
                    yt = ps[:, t * D:(t + 1) * D]
                    for p in range(PAIRS0):
                        nc.tensor.matmul(yt, oT[:, p, t * P:(t + 1) * P], wo[:, p, :], start=(p == 0), stop=False)
                    for c in range(CH0 + 1):
                        m = chunk(c)
                        last = nc.tensor.matmul(yt, hT[0:m, c, t * P:(t + 1) * P], w2[0:m, c, :],
                                                start=False, stop=(c == CH0))
                ring.steps.done(last, "y")
                normed.wait(pe, it, "x1n")
                turn4(it, "x1t", lambda t: x1n[:, t, :])
                copied.wait(pe, it, "x1T")
                product(it, "q1", wq1[:, :], x1T[:, :])
                product(it, "k1", wk1[:, :], x1T[:, :])
                ps = take(it, "v1")
                for t in range(T):
                    last = nc.tensor.matmul(ps[:, t * D:(t + 1) * D], x1T[:, t * P:(t + 1) * P], wv1[:, :],
                                            start=True, stop=True)
                ring.steps.done(last, "v1")
                copied.wait(pe, it, "v1")
                causal(it, "b", H1,
                       lambda h, i: qz1[:, h % HG, i * P:(i + 1) * P],
                       lambda h, nk: kT1[:, 0:nk],
                       lambda h, j: v1z[:, j, h, :])
                copied.wait(pe, it, "ot1")
                ps = take(it, "y1")
                for t in range(T):
                    last = nc.tensor.matmul(ps[:, t * D:(t + 1) * D], oT1[:, t * P:(t + 1) * P], wo1[:, :],
                                            start=True, stop=True)
                ring.steps.done(last, "y1")

        @block.scalar
        def _(act):
            for s in (rooted, copied, spread, exped, turned_s, silued):
                s.prime(act)
            act.wait_ge(const_loaded, ALL_LOADED)
            act.wait_ge(const_made, ALL_MADE)
            chain = Chain(act, rlink, 3)

            def full(it, key):
                return psum[ring.full(act, it, key)]

            def rsqrt(it, key, out, tmp, src, scale, eps):
                chain.link(it, nc.scalar.activation(tmp, src, ACT.Ln, bias=eps[:, 0:1], scale=scale))
                rooted.done(nc.scalar.activation(out, tmp, ACT.Exp, scale=-0.5), key)

            def copy(it, key, dst, src=None, scale=1.0):
                ps = full(it, key)
                copied.done(nc.scalar.activation(dst, ps[:, :] if src is None else src(ps), ACT.Copy, scale=scale),
                            key if key not in names else names[key])

            names = {"xt": "xnT", "x1t": "x1T"}

            def spread_head(it, h):
                spread.done(nc.scalar.activation(qz1[:, h % HG, :], qT1[:, :], ACT.Copy, scale=headmask[:, h:h + 1]), h)

            def causal(it, tag, heads):
                us = units_of(heads)
                for n in range(len(us) + PV_LAG + 2):
                    if n < len(us):
                        nk = (us[n][1] + 1) * P
                        maxed.wait(act, it, (tag, n))
                        exped.done(nc.scalar.activation(prob[:, n % PROBS, 0:nk], full(it, (tag + "s", n))[:, 0:nk], ACT.Exp,
                                                        bias=negmax[:, n % SUMS:n % SUMS + 1],
                                                        accum_out=sums[:, n % SUMS:n % SUMS + 1]), (tag, n))
                    m = n - TURN_LAG
                    if m in range(len(us)) and m % 2 == 1:
                        nk = (us[m][1] + 1) * P
                        turned_s.done(nc.scalar.copy(probT[:, m % PROBTS, 0:nk],
                                                     full(it, (tag + "pt", m))[:, 0:nk]), (tag, m))
                    if tag == "b" and n % T == 1 and n // T + 3 in range(HG, heads):
                        spread_head(it, n // T + 3)
                    m = n - PV_LAG - 1
                    if tag == "a" and m >= 0 and m % (2 * T) == 2 * T - 1 and m < len(us):
                        p = m // (2 * T)
                        outs.wait(act, it, ("a", p))
                        copied.done(nc.scalar.copy(oT[:, p, :], psum[out_bank("a", p)][:, :]), ("ot", p))

            with act.Fori(0, B) as it:
                nc.scalar.preload_act_table_set(LN_EXP)
                measured.wait(act, it, "var")
                rsqrt(it, "rstd", rstd[:, :], lnv[:, :], mv[:, :, 1], 1.0, eps5)
                measured.wait(act, it, "ms")
                rsqrt(it, "rrms", rrms[:, :], lnm[:, :], ms[:, :], 1.0 / D, epst)
                copy(it, "xt", xnT[:, :])
                ps = full(it, "gr")
                copied.done(nc.scalar.activation(egr[:, :, :], ps[:, 0:T * GR].rearrange("p (t c) -> p t c", t=T),
                                                 ACT.Exp, scale=-1.0), "gr")
                for p in range(PAIRS0):
                    ps = full(it, ("q", p))
                    nc.scalar.activation(qz[0:E0, 2 * p, :], ps[0:E0, :], ACT.Copy, scale=float(E0) ** -0.5)
                    copied.done(nc.scalar.activation(qz[E0:P, 2 * p + 1, :], ps[E0:P, :], ACT.Copy,
                                                     scale=float(E0) ** -0.5), ("q", p))
                    copy(it, ("k", p), kT[:, p, :])
                for t in range(T):
                    copy(it, ("v", t), v[:, t, :])
                causal(it, "a", H0)
                copy(it, "ct", combT[:, :], lambda ps: ps[0:EXPERTS, :])
                for c in range(CH0 + 1):
                    m = chunk(c)
                    if c >= 2:
                        gated.wait(act, it, c - 2)
                    silued.done(nc.scalar.activation(act1[0:m, c % 2, :], full(it, ("h1", c))[0:m, :], ACT.Silu), c)
                nc.scalar.preload_act_table_set(LN_EXP)
                measured.wait(act, it, "var1")
                rsqrt(it, "rstd1", rstd[:, :], lnv[:, :], mv[:, :, 1], 1.0, eps5)
                copy(it, "x1t", x1T[:, :])
                copy(it, "q1", qT1[:, :], scale=float(E1) ** -0.5)
                copied.wait(act, it, "q1")
                copy(it, "k1", kT1[:, :])
                ps = full(it, "v1")[:, :].rearrange("p (t g r e) -> p t g r e", t=T, g=HG, r=HG)
                for r in range(HG):
                    last = nc.scalar.copy(v1z[:, :, :, :].rearrange("p t (g r) c -> p t g r c", r=HG)
                                          [:, :, :, r, r * E1:(r + 1) * E1], ps[:, :, :, r, :])
                copied.done(last, "v1")
                for h in range(HG):
                    spread_head(it, h)
                causal(it, "b", H1)
                outs.wait(act, it, ("b", 0))
                copied.done(nc.scalar.copy(oT1[:, :], psum[out_bank("b", 0)][:, :]), "ot1")
                chain.end()

        @block.vector
        def _(dve):
            for s in (measured, normed, maxed, turned_v, inverted, moved, gated):
                s.prime(dve)
            dve.wait_ge(const_loaded, ALL_LOADED)
            dve.wait_ge(const_made, ALL_MADE)
            chain = Chain(dve, link, LINKS0)
            V = nc.vector

            def full(it, key):
                return psum[ring.full(dve, it, key)]

            def moments(it, src, key):
                for t in range(T):
                    last = V.bn_stats(stats[:, t, :], src[:, t, :])
                chain.link(it, last)
                settle(dve, passed)
                for t in range(T):
                    last = V.bn_aggr(mv[:, t, :], stats[:, t, :])
                measured.done(last, key)

            def normalize(it, dst, src, key, root, norm):
                measured.wait(dve, it, key)
                rooted.wait(dve, it, root)
                for t in range(T):
                    last = V.tensor_scalar(dst[:, t, :], src[:, t, :], mv[:, t, 0:1], rstd[:, t:t + 1],
                                           ALU.subtract, ALU.mult)
                normed.done(last, norm)
                normed.wait(dve, it, norm)

            def rank(it, values, gt, eq, tie, out, n):
                other = values.unsqueeze(2).to_broadcast([P, T, n, n])
                own = values.unsqueeze(3).to_broadcast([P, T, n, n])
                V.tensor_tensor(gt[:, :, :, :], other, own, ALU.is_gt)
                yield
                chain.link(it, V.tensor_tensor(eq[:, :, :, :], other, own, ALU.is_equal))
                yield
                chain.link(it, V.tensor_tensor(eq[:, :, :, :], eq[:, :, :, :],
                                               tie[:, :, :].unsqueeze(1).to_broadcast([P, T, n, n]), ALU.mult))
                yield
                chain.link(it, V.tensor_tensor(gt[:, :, :, :], gt[:, :, :, :], eq[:, :, :, :], ALU.add))
                yield
                chain.link(it, V.tensor_reduce(out[:, :, :], gt[:, :, :, :], AX.X, ALU.add))

            def gates(it):
                copied.wait(dve, it, "gr")
                chain.link(it, V.tensor_scalar(sig[:, :, :], egr[:, :, :], 1.0, None, ALU.add))
                moved.done(V.reciprocal(sig[:, :, :], sig[:, :, :]), "sig")

            def route(it):
                moved.wait(dve, it, "sig")
                score = sig[:, :, H0:GR]
                chain.link(it, V.tensor_tensor(biased[:, :, :], score,
                                               gbias[:, :].unsqueeze(1).to_broadcast([P, T, EXPERTS]), ALU.add))
                chain.link(it, V.tensor_reduce(gmax[:, :, :], biased[:, :, :].rearrange("p t (g e) -> p t g e", g=GROUPS),
                                               AX.X, ALU.max))
                yield
                yield from rank(it, gmax[:, :, :], gt4, eq4, tie4, rank4, GROUPS)
                chain.link(it, V.tensor_scalar(keep[:, :, :], rank4[:, :, :], float(TOPG), None, ALU.is_lt))
                chain.link(it, V.tensor_scalar(pen[:, :, :], keep[:, :, :], -NEG, NEG, ALU.mult, ALU.add))
                yield
                groups = [P, T * GROUPS, EXPERTS // GROUPS]
                wide = lambda a: a[:, :, :].rearrange("p t g -> p (t g)").unsqueeze(2).to_broadcast(groups)
                by_group = lambda a: a[:, :, :].rearrange("p t (g e) -> p (t g) e", g=GROUPS)
                chain.link(it, V.tensor_tensor(by_group(kept), by_group(biased), wide(keep), ALU.mult))
                chain.link(it, V.tensor_tensor(by_group(kept), by_group(kept), wide(pen), ALU.add))
                yield
                yield from rank(it, kept[:, :, :], gt16, eq16, tie16, rank16, EXPERTS)
                chain.link(it, V.tensor_scalar(rank16[:, :, :], rank16[:, :, :], float(TOPK), None, ALU.is_lt))
                moved.done(V.tensor_tensor(comb[:, :, :], rank16[:, :, :], score, ALU.mult), "comb")

            def causal(it, tag, heads, other_work):
                us = units_of(heads)
                for n in range(len(us) + PV_LAG):
                    if n < len(us):
                        nk = (us[n][1] + 1) * P
                        maxed.done(V.tensor_reduce(negmax[:, n % SUMS:n % SUMS + 1], full(it, (tag + "s", n))[:, 0:nk],
                                                   AX.X, ALU.max, negate=True), (tag, n))
                    m = n - 2
                    if m in range(len(us)):
                        exped.wait(dve, it, (tag, m))
                        inverted.done(V.reciprocal(rsum[:, m % SUMS:m % SUMS + 1], sums[:, m % SUMS:m % SUMS + 1]), (tag, m))
                    m = n - TURN_LAG
                    if m in range(len(us)) and m % 2 == 0:
                        nk = (us[m][1] + 1) * P
                        turned_v.done(V.tensor_copy(probT[:, m % PROBTS, 0:nk],
                                                    full(it, (tag + "pt", m))[:, 0:nk]), (tag, m))
                    next(other_work, None)
                for _ in other_work:
                    pass

            with dve.Fori(0, B) as it:
                dve.wait_ge(x_loaded, it * 16 + 16)
                moments(it, x, "var")
                ring.steps.wait_before(dve, it, "tt")
                normalize(it, xn, x, "var", "rstd", "xn")
                for t in range(T):
                    last = V.tensor_tensor_reduce(square[:, t, :], xn[:, t, :], xn[:, t, :], 1.0, 0.0, ALU.mult, ALU.add,
                                                  ms[:, t:t + 1])
                measured.done(last, "ms")
                rooted.wait(dve, it, "rrms")
                for t in range(T):
                    last = V.tensor_scalar(tn[:, t, :], xn[:, t, :], rrms[:, t:t + 1], None, ALU.mult)
                normed.done(last, "tn")
                moved.done(V.tensor_scalar(tT[:, :], full(it, "tt")[:, :], rmsw[:, 0:1], None, ALU.mult), "tT")
                gates(it)
                causal(it, "a", H0, route(it))
                for c in range(CH0 + 1):
                    m = chunk(c)
                    silued.wait(dve, it, c)
                    ps = full(it, ("h3", c))
                    if c < CH0:
                        chain.link(it, V.tensor_tensor(prod[:, c % 2, :], ps[:, :], act1[:, c % 2, :], ALU.mult))
                        gated.done(V.tensor_tensor(hT[:, c, :], full(it, ("cb", c))[:, :], prod[:, c % 2, :], ALU.mult), c)
                    else:
                        gated.done(V.tensor_tensor(hT[0:m, c, :], ps[0:m, :], act1[0:m, c % 2, :], ALU.mult), c)
                moved.done(V.tensor_tensor(x1[:, :, :], full(it, "y")[:, :].rearrange("p (t d) -> p t d", t=T), x[:, :, :],
                                           ALU.add), "x1")
                moved.wait(dve, it, "x1")
                moments(it, x1, "var1")
                normalize(it, x1n, x1, "var1", "rstd1", "x1n")
                copied.wait(dve, it, "x1T")
                V.tensor_copy(state[0:D // 2, bass.ds(it, 1), 0:N].rearrange("p s n -> p (s n)"), x1T[0:D // 2, :])
                V.tensor_copy(state[D // 2:D, bass.ds(it, 1), 1:N + 1].rearrange("p s n -> p (s n)"), x1T[D // 2:D, :])
                causal(it, "b", H1, iter(()))
                ps = full(it, "y1")
                dve.wait_ge(stored, it * 16 + 16)
                moved.done(V.tensor_tensor(sumout[:, :, :], ps[:, :].rearrange("p (t d) -> p t d", t=T), x1[:, :, :],
                                           ALU.add), "sum")
                chain.end()


def pass1(nc, io, sh, ctx):
    ident, identb, maskw, state, psum = sh.ident, sh.identb, sh.maskw, sh.state, sh.psum

    def sb(name, shape, dt=F32):
        return ctx.enter_context(nc.sbuf_tensor(name, shape, dt))

    def sem(name):
        return ctx.enter_context(nc.semaphore(name))

    def steps(name, keys):
        return Steps(sem(name), keys)

    WK = WIN + P
    wqkv, wol = sb("wqkv", [P, 3 * INNER]), sb("wol", [P, PAIRSL, D])
    w1l, w2l = sb("w1l", [P, 2 * DI]), sb("w2l", [P, 3, D])
    b1l = sb("b1l", [P, 2, 3])
    lng, lnb, b2l = sb("lng", [P, 1]), sb("lnb", [P, 1]), sb("b2l", [P, 1])
    qks = sb("qks", [P, 2, EL])
    rot = sb("rot", [P, 4, T, EL])
    rots = sb("rots", [P, 4, T, EL])

    xw = sb("xw", [P, N + 1])
    xm = sb("xm", [P, N + 1])
    sq = sb("sq", [P, 2, BANK])
    ss, ssc = sb("ss", [P, 2 * HL]), sb("ssc", [P, 2, 2 * HL])
    lns, rn = sb("lns", [P, 2 * HL]), sb("rn", [P, 2, 2 * HL])
    cosd, sind = sb("cosd", [P, 2, 4, BANK]), sb("sind", [P, 2, 4, BANK])
    qk = sb("qk", [P, 4, BANK])
    qzl = sb("qzl", [P, 2, HL, P])
    kTl = sb("kTl", [P, PAIRSL, N])
    vl = sb("vl", [P, T, INNER])
    negmaxl = sb("negmaxl", [P, 2, HL])
    probl = sb("probl", [P, 2, HL, WK])
    pT = sb("pT", [P, HL, P])
    pP = sb("pP", [P, HL, WIN])
    suml, rs = sb("suml", [P, 2, HL]), sb("rs", [P, 2, HL])
    oTl = sb("oTl", [P, PAIRSL, N])
    stats, mv = sb("statsl", [P, T, 6]), sb("mvl", [P, T, 2])
    lnv, rstd = sb("lnvl", [P, T]), sb("rstdl", [P, T])
    x2, x2T = sb("x2", [P, T, D]), sb("x2T", [P, N])
    gel, hf = sb("gel", [P, 2, N]), sb("hf", [P, 3, N])

    order = order1()
    pieces = [(t, j) for t in range(T) for j in range(4)]
    groups = [(t, g) for t in range(T) for g in range(len(SCORE_HEADS))]
    qkv_loaded, o_loaded, ffn_loaded, rot_loaded, made = (sem(n) for n in ("qkv_loaded", "o_loaded", "ffn_loaded",
                                                                            "rot_loaded", "made"))
    fetched = steps("fetched", ["xw"])
    scaled = sem("scaled")
    summed_rot = steps("summed_rot", pieces)
    rotated = steps("rotated", pieces)
    weighed = steps("weighed", groups)
    parts = steps("parts", pieces)
    summed = steps("summed", pieces)
    clamped = steps("clamped", range(T))
    maxed = steps("maxedl", groups)
    turned_v = steps("turned_vl", [(t, k) for t in range(T) for k in (0, 2)])
    inverted = steps("invertedl", groups)
    mid = steps("mid", ["xm"])
    ffn = steps("ffn", ["var", "x2", "x2T"])
    hidden = steps("hidden", range(3))
    left = steps("left", ["state"])
    squared = steps("squared", pieces)
    vcopied = steps("vcopied", [(t, j) for t in range(T) for j in range(2)])
    rooted = steps("rootedl", [*range(T), "ffn"])
    tcopied = steps("tcopied", pieces)
    exped = steps("expedl", groups)
    turned_s = steps("turned_sl", [(t, k) for t in range(T) for k in ([1, 3] + (["pp"] if t else []))])
    ocopied = steps("ocopied", [(t, j) for t in range(T) for j in range(2)])
    gelued = steps("gelued", range(3))
    link, rlink, passed = sem("linkl"), sem("rlinkl"), sem("passedl")

    def readers(key):
        kind, at = key[0], key[1:]
        if kind == "qk":
            return [(squared, at)]
        if kind == "v":
            return [(vcopied, at)]
        if kind == "t":
            return [(tcopied, at)]
        if kind == "s":
            return [(exped, at)]
        if kind == "pt":
            return [(turned_s if at[1] % 2 else turned_v, at)]
        if kind == "pp":
            return [(turned_s, (at[0], "pp"))]
        if kind == "o":
            return [(ocopied, at)]
        if kind == "y":
            return [(mid, "xm")]
        if kind == "xt":
            return [(ffn, "x2")]
        if kind == "xn":
            return [(ffn, "x2T")]
        if kind == "gate":
            return [(gelued, at[0])]
        if kind == "up":
            return [(hidden, at[0])]
        return [(left, "state")]

    ring = Ring(sem("filledl"), [(key, readers(key)) for key in order])

    def keys0(t):
        return (t * P - WIN, 0) if t else (0, WIN)

    with nc.Block() as block:
        @block.sync
        def _(sp):
            sp.dma_start(rot[:, :, :, :], io["rot"]).then_inc(rot_loaded, 16)
            with sp.Fori(0, DEPTH) as l:
                it = l * B
                one = bass.ds(l, 1)
                ring.steps.wait_before(sp, it, ("v", T - 1, 1))
                settle(sp, passed)
                sp.dma_start(wqkv[:, :], io["wqkv"][one].rearrange("l p n -> p (l n)")).then_inc(qkv_loaded, 16)
                parts.wait_before(sp, it, pieces[-1])
                settle(sp, passed)
                sp.wait_ge(scaled, l * 4 + 4)
                settle(sp, passed)
                sp.dma_start(qks[:, 0, :], io["qs"][one].to_broadcast([P, EL])).then_inc(qkv_loaded, 16)
                sp.dma_start(qks[:, 1, :], io["ks"][one].to_broadcast([P, EL])).then_inc(qkv_loaded, 16)
                ring.steps.wait_before(sp, it, ("y",))
                settle(sp, passed)
                sp.dma_start(wol[:, :, :], io["wol"][one].rearrange("l (c p) d -> p (l c) d", p=P)).then_inc(o_loaded, 16)
                left.wait_before(sp, it, "state")
                settle(sp, passed)
                sp.dma_start(w1l[:, :], io["w1l"][one].rearrange("l p n -> p (l n)")).then_inc(ffn_loaded, 16)
                for dst, name in ((lng, "lng"), (lnb, "lnb"), (b2l, "b2l")):
                    sp.dma_start(dst[:, :], io[name][one].rearrange("l p -> p l")).then_inc(ffn_loaded, 16)
                at = 0
                for c, m in enumerate(CW):
                    sp.dma_start(w2l[0:m, c, :], io["w2l"][one][:, at:at + m, :].rearrange("l p d -> p (l d)")
                                 ).then_inc(ffn_loaded, 16)
                    for a in range(2):
                        sp.dma_start(b1l[0:m, a, c:c + 1], io["b1l"][one][:, a * DI + at:a * DI + at + m]
                                     .rearrange("l p -> p l")).then_inc(ffn_loaded, 16)
                    at += m

        FFN_LOADS = 4 + 3 * 3

        @block.gpsimd
        def _(pool):
            for s in (fetched, summed_rot, rotated, weighed):
                s.prime(pool)
            pool.sem_inc(scaled, 4)
            nc.gpsimd.memset(qzl[:, :, :, :], 0.0).then_inc(made, 1)
            nc.gpsimd.memset(xm[:, :], 0.0).then_inc(made, 1)
            pool.wait_ge(rot_loaded, 16)

            def work(it, key):
                kind, at = key[0], key[1:]
                if kind == "qk":
                    t, j = at
                    parts.wait(pool, it, at)
                    summed_rot.done(nc.gpsimd.tensor_tensor(cosd[:, t % 2, j, :], cosd[:, t % 2, j, :],
                                                            sind[:, t % 2, j, :], ALU.add), at)
                elif kind == "v" and at[1] == 1:
                    t = at[0]
                    rooted.wait(pool, it, t)
                    for j in range(4):
                        if t:
                            ring.steps.wait(pool, it, ("t", t - 1, j))
                        else:
                            ring.steps.wait_before(pool, it, ("t", T - 1, j))
                        summed_rot.wait(pool, it, (t, j))
                        rotated.done(nc.gpsimd.tensor_tensor(
                            qk[:, j, :].rearrange("p (h c) -> p h c", c=EL),
                            cosd[:, t % 2, j, :].rearrange("p (h c) -> p h c", c=EL),
                            rn[:, t % 2, 8 * j:8 * j + 8].unsqueeze(2).to_broadcast([P, 8, EL]), ALU.mult), (t, j))
                elif kind == "s":
                    t, g = at
                    a, b = SCORE_HEADS[g]
                    _, c0 = keys0(t)
                    inverted.wait(pool, it, at)
                    p = probl[:, t % 2, a:b, c0:WK]
                    weighed.done(nc.gpsimd.tensor_tensor(
                        p, p, rs[:, t % 2, a:b].unsqueeze(2).to_broadcast([P, b - a, WK - c0]), ALU.mult), at)

            with pool.Fori(0, DEPTH) as l:
                pool.wait_ge(qkv_loaded, l * 48 + 48)
                parts.wait_before(pool, l * B, pieces[-1])
                for a in range(2):
                    scale = qks[:, a, :].rearrange("p (two c) -> p two c", two=2)
                    for b, own in ((2 * a, scale), (2 * a + 1, scale[:, ::-1, :])):
                        nc.gpsimd.tensor_tensor(
                            rots[:, b, :, :].rearrange("p t (two c) -> p t two c", two=2),
                            rot[:, b, :, :].rearrange("p t (two c) -> p t two c", two=2),
                            own.unsqueeze(1).to_broadcast([P, T, 2, EL // 2]), ALU.mult).then_inc(scaled, 1)
                with pool.Fori(0, B) as s:
                    it = l * B + s
                    mid.wait_before(pool, it, "xm")
                    fetched.done(nc.gpsimd.tensor_copy(xw[:, :], state[:, bass.ds(s, 1), :].rearrange("p s n -> p (s n)")), "xw")
                    for key in order:
                        work(it, key)

        @block.tensor
        def _(pe):
            ring.steps.prime(pe)
            pe.wait_ge(made, 2)

            def fill(it, key):
                ps = psum[ring.take(pe, it, key)]
                kind, at = key[0], key[1:]
                t = at[0] if at else 0
                if kind in ("qk", "v"):
                    col = (4 if kind == "v" else 0) * BANK + at[1] * BANK
                    last = nc.tensor.matmul(ps[:, :], xw[:, t * P:(t + 1) * P], wqkv[:, col:col + BANK],
                                            start=True, stop=True)
                elif kind == "t":
                    rotated.wait(pe, it, at)
                    for c in range(4):
                        last = nc.tensor.transpose(ps[:, c * P:(c + 1) * P], qk[:, at[1], c * P:(c + 1) * P], ident[:, :])
                elif kind == "s":
                    if at[1] == 0:
                        tcopied.wait(pe, it, (t, 3))
                    heads = range(*SCORE_HEADS[at[1]])
                    k0, c0 = keys0(t)
                    blocks = ps[:, 0:len(heads) * WK].rearrange("p (h k) -> p h k", k=WK)
                    nc.tensor.matmul(blocks[:, :, c0:WK], identb[:, :],
                                     maskw[:, c0:WK].unsqueeze(1).to_broadcast([P, len(heads), WK - c0]),
                                     start=True, stop=False, skip_group_check=True)
                    for n, h in enumerate(heads):
                        last = nc.tensor.matmul(blocks[:, n, c0:WK], qzl[:, t % 2, h, :],
                                                kTl[:, h // 2, k0:(t + 1) * P],
                                                start=False, stop=(n == len(heads) - 1), skip_group_check=True)
                elif kind == "pt":
                    weighed.wait(pe, it, (t, next(g for g, (a, b) in enumerate(SCORE_HEADS) if b >= 4 * at[1] + 4)))
                    for c in range(4):
                        last = nc.tensor.transpose(ps[:, c * P:(c + 1) * P], probl[:, t % 2, 4 * at[1] + c, WIN:WK], ident[:, :])
                elif kind == "pp":
                    settle(pe, passed)
                    for h in range(HL):
                        last = nc.tensor.transpose(ps[0:WIN, h * WIN:(h + 1) * WIN], probl[0:WIN, t % 2, h, 0:WIN],
                                                   ident[0:WIN, 0:WIN])
                elif kind == "o":
                    if at[1] == 0:
                        turned_v.wait(pe, it, (t, 2))
                        turned_s.wait(pe, it, (t, "pp" if t else 3))
                        vcopied.wait(pe, it, (t, 1))
                    for n, h in enumerate(range(8 * at[1], 8 * at[1] + 8)):
                        half, col = slice(64 * (h % 2), 64 * (h % 2) + 64), n // 2 * P
                        last = nc.tensor.matmul(ps[half, col:col + P], vl[:, t, h * EL:(h + 1) * EL], pT[:, h, :],
                                                start=(n < 2), stop=(t == 0), skip_group_check=True)
                    for n, h in enumerate(range(8 * at[1], 8 * at[1] + 8) if t else ()):
                        half, col = slice(64 * (h % 2), 64 * (h % 2) + 64), n // 2 * P
                        last = nc.tensor.matmul(ps[half, col:col + WIN], vl[P - WIN:P, t - 1, h * EL:(h + 1) * EL],
                                                pP[P - WIN:P, h, :], start=False, stop=True, skip_group_check=True,
                                                tile_position=(P - WIN, 64 * (h % 2)))
                elif kind == "y":
                    pe.wait_ge(o_loaded, o_layers(it))
                    ocopied.wait(pe, it, (T - 1, 1))
                    for c in range(PAIRSL):
                        last = nc.tensor.matmul(ps[:, :], wol[:, c, :], oTl[:, c, :],
                                                start=(c == 0), stop=(c == PAIRSL - 1))
                elif kind == "xt":
                    mid.wait(pe, it, "xm")
                    for c in range(T):
                        last = nc.tensor.transpose(ps[:, c * P:(c + 1) * P], xm[:, c * P:(c + 1) * P], ident[:, :])
                elif kind == "xn":
                    ffn.wait(pe, it, "x2")
                    for c in range(T):
                        last = nc.tensor.transpose(ps[:, c * P:(c + 1) * P], x2[:, c, :], ident[:, :])
                elif kind in ("gate", "up"):
                    if key == ("gate", 0):
                        ffn.wait(pe, it, "x2T")
                    col = (DI if kind == "gate" else 0) + sum(CW[:t])
                    last = nc.tensor.matmul(ps[0:CW[t], :], w1l[:, col:col + CW[t]], x2T[:, :], start=True, stop=True)
                else:
                    hidden.wait(pe, it, 2)
                    for c, m in enumerate(CW):
                        last = nc.tensor.matmul(ps[:, :], w2l[0:m, c, :], hf[0:m, c, :], start=(c == 0), stop=(c == 2))
                ring.steps.done(last, key)

            with pe.Fori(0, DEPTH) as l:
                o_layers = lambda it: l * 16 + 16
                with pe.Fori(0, B) as s:
                    it = l * B + s
                    pe.wait_ge(qkv_loaded, l * 48 + 48)
                    fetched.wait(pe, it, "xw")
                    for key in order:
                        if key == ("xt",):
                            pe.wait_ge(ffn_loaded, (l + 1) * (16 * FFN_LOADS))
                        fill(it, key)

        @block.scalar
        def _(act):
            for s in (squared, vcopied, rooted, tcopied, exped, turned_s, ocopied, gelued):
                s.prime(act)
            act.wait_ge(made, 2)
            chain = Chain(act, rlink, T + 1)

            def read(it, key):
                kind, at = key[0], key[1:]
                t = at[0] if at else 0
                if kind in ("up", "y2", "y", "xn") or (kind == "pt" and at[1] % 2 == 0):
                    return
                ps = psum[ring.full(act, it, key)]
                if kind == "qk":
                    parts.wait(act, it, at)
                    n = 4 * t + at[1]
                    if n >= 2:
                        summed.wait(act, it, pieces[n - 2])
                    else:
                        summed.wait_before(act, it, pieces[n - 2])
                    squared.done(nc.scalar.activation(sq[:, n % 2, :], ps[:, :], ACT.Square), at)
                elif kind == "v":
                    vcopied.done(nc.scalar.copy(vl[:, t, BANK * at[1]:BANK * (at[1] + 1)], ps[:, :]), at)
                    if at[1] == 1:
                        clamped.wait(act, it, t)
                        chain.link(it, nc.scalar.activation(lns[:, :], ssc[:, t % 2, :], ACT.Ln))
                        rooted.done(nc.scalar.activation(rn[:, t % 2, :], lns[:, :], ACT.Exp, scale=-0.5,
                                                         bias=sh.lnt[:, 0:1]), t)
                elif kind == "t":
                    src = ps[:, :].rearrange("p (c n) -> p c n", n=P)
                    if at[1] < 2:
                        dst = qzl[:, t % 2, 8 * at[1]:8 * at[1] + 8, :].rearrange("p (c two) n -> p c two n", two=2)
                        nc.scalar.copy(dst[0:EL, :, 0, :], src[0:EL, :, :])
                        last = nc.scalar.copy(dst[EL:P, :, 1, :], src[EL:P, :, :])
                    else:
                        last = nc.scalar.copy(kTl[:, 4 * at[1] - 8:4 * at[1] - 4, t * P:(t + 1) * P], src)
                    tcopied.done(last, at)
                elif kind == "s":
                    maxed.wait(act, it, at)
                    _, c0 = keys0(t)
                    for n, h in enumerate(range(*SCORE_HEADS[at[1]])):
                        last = nc.scalar.activation(probl[:, t % 2, h, c0:WK], ps[:, n * WK + c0:(n + 1) * WK], ACT.Exp,
                                                    bias=negmaxl[:, t % 2, h:h + 1], accum_out=suml[:, t % 2, h:h + 1])
                    exped.done(last, at)
                elif kind == "pt":
                    turned_s.done(nc.scalar.copy(pT[:, 4 * at[1]:4 * at[1] + 4, :], ps[:, :].rearrange("p (h n) -> p h n", n=P)), at)
                elif kind == "pp":
                    turned_s.done(nc.scalar.copy(pP[P - WIN:P, :, :], ps[0:WIN, :].rearrange("p (h n) -> p h n", n=WIN)), (t, "pp"))
                elif kind == "o":
                    ocopied.done(nc.scalar.copy(oTl[:, 4 * at[1]:4 * at[1] + 4, t * P:(t + 1) * P],
                                                ps[:, :].rearrange("p (c n) -> p c n", n=P)), at)
                elif kind == "xt":
                    ffn.wait(act, it, "var")
                    chain.link(it, nc.scalar.activation(lnv[:, :], mv[:, :, 1], ACT.Ln, bias=sh.eps5[:, 0:1]))
                    rooted.done(nc.scalar.activation(rstd[:, :], lnv[:, :], ACT.Exp, scale=-0.5), "ffn")
                elif kind == "gate":
                    if t == 2:
                        hidden.wait(act, it, 0)
                    m = CW[t]
                    gelued.done(nc.scalar.activation(gel[0:m, t % 2, :], ps[0:m, :], ACT.Gelu, bias=b1l[0:m, 1, t:t + 1]), t)

            with act.Fori(0, DEPTH) as l:
                with act.Fori(0, B) as s:
                    it = l * B + s
                    nc.scalar.preload_act_table_set(LN_EXP)
                    for key in order:
                        if key == ("gate", 0):
                            act.wait_ge(ffn_loaded, (l + 1) * (16 * FFN_LOADS))
                        read(it, key)
                    chain.end()

        @block.vector
        def _(dve):
            for s in (parts, summed, clamped, maxed, turned_v, inverted, mid, ffn, hidden, left):
                s.prime(dve)
            dve.wait_ge(made, 2)
            V = nc.vector
            chain = Chain(dve, link, LINKS1)
            HALF = D // 2

            def unshift(ins_of, it_rows=((0, HALF, 0), (HALF, D, 1))):
                for a, b, d in it_rows:
                    last = ins_of(a, b, d)
                return last

            def sum_squares(it, piece):
                squared.wait(dve, it, piece)
                j = piece[1]
                summed.done(V.tensor_reduce(ss[:, 8 * j:8 * j + 8], sq[:, j % 2, :].rearrange("p (h c) -> p h c", c=EL),
                                            AX.X, ALU.add), piece)

            def invert(it, t, g):
                a, b = SCORE_HEADS[g]
                exped.wait(dve, it, (t, g))
                inverted.done(V.reciprocal(rs[:, t % 2, a:b], suml[:, t % 2, a:b]), (t, g))

            def read(it, s, key):
                kind, at = key[0], key[1:]
                t = at[0] if at else 0
                if kind == "v" and at[1] == 0:
                    sum_squares(it, (t, 3))
                    summed.wait(dve, it, (t, 3))
                    clamped.done(V.tensor_scalar(ssc[:, t % 2, :], ss[:, :], 1e-24, TINY, ALU.max, ALU.mult), t)
                if kind in ("v", "t", "pp", "o", "gate") or (kind == "pt" and at[1] % 2):
                    return
                ps = psum[ring.full(dve, it, key)]
                if kind == "qk":
                    j = at[1]
                    if t >= 2:
                        rotated.wait(dve, it, (t - 2, j))
                    else:
                        rotated.wait_before(dve, it, (t + 2, j))
                    table = 2 * (j // 2)
                    heads = ps[:, :].rearrange("p (h two c) -> p h two c", two=2, c=EL // 2)
                    by_head = lambda a: a.rearrange("p (h c) -> p h c", c=EL)
                    wide = lambda a: a.unsqueeze(1).to_broadcast([P, 8, EL])
                    V.tensor_tensor(by_head(cosd[:, t % 2, j, :]), by_head(ps[:, :]), wide(rots[:, table, t, :]), ALU.mult)
                    halves = lambda a: a.rearrange("p h (two c) -> p h two c", two=2)
                    parts.done(V.tensor_tensor(halves(by_head(sind[:, t % 2, j, :])), heads[:, :, ::-1, :],
                                               halves(wide(rots[:, table + 1, t, :])), ALU.mult), at)
                    if j:
                        sum_squares(it, (t, j - 1))
                elif kind == "s":
                    _, c0 = keys0(t)
                    a, b = SCORE_HEADS[at[1]]
                    nh = b - a
                    blocks = ps[:, 0:nh * WK].rearrange("p (h k) -> p h k", k=WK)
                    maxed.done(V.tensor_reduce(negmaxl[:, t % 2, a:b], blocks[:, :, c0:WK], AX.X, ALU.max, negate=True), at)
                    if at[1]:
                        invert(it, t, at[1] - 1)
                elif kind == "pt":
                    turned_v.done(V.tensor_copy(pT[:, 4 * at[1]:4 * at[1] + 4, :], ps[:, :].rearrange("p (h n) -> p h n", n=P)), at)
                elif kind == "y":
                    mid.done(unshift(lambda a, b, d: V.tensor_tensor(xm[a:b, d:N + d], ps[a:b, :], xw[a:b, d:N + d], ALU.add)), "xm")
                elif kind == "xt":
                    for c in range(T):
                        last = V.bn_stats(stats[:, c, :], ps[:, c * P:(c + 1) * P])
                    chain.link(it, last)
                    settle(dve, passed)
                    for c in range(T):
                        last = V.bn_aggr(mv[:, c, :], stats[:, c, :])
                    ffn.done(last, "var")
                    ffn.wait(dve, it, "var")
                    rooted.wait(dve, it, "ffn")
                    for c in range(T):
                        last = V.tensor_scalar(x2[:, c, :], ps[:, c * P:(c + 1) * P], mv[:, c, 0:1], rstd[:, c:c + 1],
                                               ALU.subtract, ALU.mult)
                    ffn.done(last, "x2")
                elif kind == "xn":
                    ffn.done(V.tensor_scalar(x2T[:, :], ps[:, :], lng[:, 0:1], lnb[:, 0:1], ALU.mult, ALU.add), "x2T")
                elif kind == "up":
                    m = CW[t]
                    gelued.wait(dve, it, t)
                    hidden.done(V.scalar_tensor_tensor(out=hf[0:m, t, :], in0=ps[0:m, :], scalar=b1l[0:m, 0, t:t + 1],
                                                       in1=gel[0:m, t % 2, :], op0=ALU.add, op1=ALU.mult), t)
                else:
                    last = unshift(lambda a, b, d: V.scalar_tensor_tensor(
                        out=state[a:b, bass.ds(s, 1), d:N + d].rearrange("p s n -> p (s n)"), in0=ps[a:b, :],
                        scalar=b2l[a:b, 0:1], in1=xm[a:b, d:N + d], op0=ALU.add, op1=ALU.add))
                    left.done(last, "state")

            with dve.Fori(0, DEPTH) as l:
                with dve.Fori(0, B) as s:
                    it = l * B + s
                    dve.wait_ge(scaled, l * 4 + 8)
                    for key in order:
                        if key == ("xn",):
                            dve.wait_ge(ffn_loaded, (l + 1) * (16 * FFN_LOADS))
                        read(it, s, key)
                        if key[0] == "s" and key[2] == len(SCORE_HEADS) - 1:
                            invert(it, *key[1:])
                    chain.end()


def pass2(nc, io, sh, ctx):
    ident, state, psum = sh.ident, sh.state, sh.psum

    def sb(name, shape, dt=F32):
        return ctx.enter_context(nc.sbuf_tensor(name, shape, dt))

    def sem(name):
        return ctx.enter_context(nc.semaphore(name))

    xf, sums, out = sb("xf", [P, N]), sb("sums_in", [P, T, D]), sb("outs", [P, T, D])
    straight, turned, added, loaded, stored, passed = (sem(n) for n in ("straight", "turned", "added", "loaded",
                                                                         "stored2", "passed2"))
    tokens = "s (t p) d -> p (s t) d"
    with nc.Block() as block:
        @block.sync
        def _(sp):
            sp.sem_inc(stored, 16)
            with sp.Fori(0, B) as s:
                sp.wait_ge(added, s + 1)
                settle(sp, passed)
                sp.dma_start(sums[:, :, :], io["sums"][bass.ds(s, 1)].rearrange(tokens, p=P)).then_inc(loaded, 16)
                sp.wait_ge(added, s + 2)
                settle(sp, passed)
                sp.dma_start(io["out"][bass.ds(s, 1)].rearrange(tokens, p=P), out[:, :, :]).then_inc(stored, 16)
            sp.wait_ge(stored, 16 * B + 16)

        @block.scalar
        def _(act):
            with act.Fori(0, B) as s:
                act.wait_ge(turned, s + 1)
                one = bass.ds(s, 1)
                nc.scalar.copy(xf[0:D // 2, :], state[0:D // 2, one, 0:N].rearrange("p s n -> p (s n)"))
                nc.scalar.copy(xf[D // 2:D, :], state[D // 2:D, one, 1:N + 1].rearrange("p s n -> p (s n)")
                               ).then_inc(straight, 1)

        @block.tensor
        def _(pe):
            pe.sem_inc(turned, 1)
            with pe.Fori(0, B) as s:
                pe.wait_ge(straight, s + 1)
                pe.wait_ge(added, s + 1)
                for t in range(T):
                    last = nc.tensor.transpose(psum[0][:, t * P:(t + 1) * P], xf[:, t * P:(t + 1) * P], ident[:, :])
                last.then_inc(turned, 1)

        @block.vector
        def _(dve):
            dve.sem_inc(added, 1)
            with dve.Fori(0, B) as s:
                dve.wait_ge(turned, s + 2)
                dve.wait_ge(loaded, s * 16 + 16)
                dve.wait_ge(stored, s * 16 + 16)
                nc.vector.tensor_tensor(out[:, :, :], psum[0][:, :].rearrange("p (t d) -> p t d", t=T), sums[:, :, :],
                                        ALU.add).then_inc(added, 1)


LINKS0 = 26
LINKS1 = 1 


def build(nc, io):
    with ExitStack() as ctx:
        sh = Shared(nc, ctx)
        with ExitStack() as inner:
            pass0(nc, io, sh, inner)
        with ExitStack() as inner:
            pass1(nc, io, sh, inner)
        with ExitStack() as inner:
            pass2(nc, io, sh, inner)


def rotary():
    f = np.float32
    half = np.arange(0, EL, 2, dtype=f)
    inv_freq = (f(1.0) / f(10000.0) ** (half / f(EL))).astype(f)
    tok = np.arange(N, dtype=f)
    freqs = tok[:, None] * inv_freq[None, :]
    freqs = np.concatenate([freqs, freqs], -1).astype(np.float64)
    base = ((half + f(0.4 * EL)) / f(1.4 * EL)).astype(np.float64)
    power = (tok - N // 2) / (WIN // 2)
    scale = base[None, :] ** power[:, None].astype(np.float64)
    scale = np.concatenate([scale, scale], -1)
    cos, sin = np.cos(freqs), np.sin(freqs)
    sin[:, :EL // 2] *= -1
    tables = np.stack([QK_SCALE * cos * scale, QK_SCALE * sin * scale, cos / scale, sin / scale])
    return np.ascontiguousarray(tables.reshape(4, T, P, EL).transpose(2, 0, 1, 3).astype(f))


def masks():
    q, k = np.arange(P)[:, None], np.arange(P)[None, :]
    causal = np.where(k <= q, 0.0, NEG)
    r = np.arange(WIN + P)[None, :] - WIN
    window = np.where((r <= q) & (q <= r + WIN), 0.0, NEG)
    return causal.astype(np.float32), window.astype(np.float32)


def kernel(**inputs):
    from concourse import bacc
    from concourse.bass_utils import run_bass_kernel_spmd

    a = {k: np.asarray(v) for k, v in inputs.items()}
    f = np.float32
    causal, window = masks()
    pick = np.zeros((EXPERTS, CH0, P), f)
    for e in range(EXPERTS):
        pick[e, e // 2, (e % 2) * INTER:(e % 2 + 1) * INTER] = 1.0
    earlier = lambda n: np.tril(np.ones((n, n), f), -1)

    flat = lambda w: w.transpose(1, 0, 2).reshape(D, H0 * E0)
    up = lambda w, shared: np.concatenate([w.reshape(EXPERTS * INTER, D), shared], 0).T
    arrays = {
        "ident": np.eye(P, dtype=f), "maskc": causal, "maskw": window, "sel": pick,
        "tie16": earlier(EXPERTS), "tie4": earlier(GROUPS), "rot": rotary(),
        "x": a["L0_attn_tokens"],
        "wq0": flat(a["L0_attn_wq"]), "wk0": flat(a["L0_attn_wk"]), "wv0": flat(a["L0_attn_wv"]),
        "wo0": a["L0_attn_wo"].reshape(PAIRS0, P, D).transpose(1, 0, 2),
        "wgates": a["L0_attn_w_gates"], "wroute": a["L0_ffn_gate_w"].T,
        "rmsw": a["L0_attn_rms_w"].reshape(D, 1), "gbias": a["L0_ffn_gate_bias"],
        "w1": up(a["L0_ffn_w1"], a["L0_ffn_ws1"]), "w3": up(a["L0_ffn_w3"], a["L0_ffn_ws3"]),
        "w2": a["L0_ffn_w2"].transpose(0, 2, 1).reshape(CH0, P, D).transpose(1, 0, 2), "ws2": a["L0_ffn_ws2"].T,
        "wq1": a["L1_attn_Wq"].T, "wk1": a["L1_attn_Wk"].T, "headmask": np.repeat(np.eye(H1, dtype=f), E1, axis=0),
        "wv1": a["L1_attn_Wv"].T, "wo1": a["L1_attn_Wo"].T,
        "wqkv": a["L1_ffn_Wqkv"], "qs": a["L1_ffn_q_scale"], "ks": a["L1_ffn_k_scale"], "wol": a["L1_ffn_Wo"],
        "lng": a["L1_ffn_ln_g"], "lnb": a["L1_ffn_ln_b"], "w1l": a["L1_ffn_W1"], "b1l": a["L1_ffn_b1"],
        "w2l": a["L1_ffn_W2"], "b2l": a["L1_ffn_b2"],
    }
    arrays = {f"in_{k}": np.ascontiguousarray(v) for k, v in arrays.items()}
    nc = bacc.Bacc("TRN2", target_bir_lowering=False, num_devices=1)
    io = {k[3:]: nc.dram_tensor(k, v.shape, mybir.dt.from_np(v.dtype), kind="ExternalInput").ap()
          for k, v in arrays.items()}
    io["out"] = nc.dram_tensor("out", (B, N, D), F32, kind="ExternalOutput").ap()
    io["sums"] = nc.dram_tensor("sums", (B, N, D), F32, kind="Internal").ap()
    build(nc, io)
    r = run_bass_kernel_spmd(nc, [arrays], core_ids=[0])
    return r.results[0]["out"]
```

```python
from contextlib import ExitStack

import numpy as np

import concourse.bass as bass
from concourse import mybir

F32 = mybir.dt.float32
BF16 = mybir.dt.bfloat16
ALU = mybir.AluOpType
ACT = mybir.ActivationFunctionType
AX = mybir.AxisListType

P = 128
D = 128
B, N = 8, 512
T = N // P
NEG = -1.0e30
BANKS, BANK = 8, 512

H0, E0 = 8, 64
PAIRS0 = H0 * E0 // P
EXPERTS, INTER, GROUPS, TOPK, TOPG = 16, 64, 4, 4, 2
CH0 = EXPERTS * INTER // P
H1, E1 = 16, 8
HG = 4
DEPTH, HL, EL, WIN = 6, 16, 64, 32
INNER = HL * EL
PAIRSL = INNER // P
DI = int(D * 4 * 2 / 3)
CW = [114, 114, 113]
QK_SCALE = 8.0
LN_EXP = "natural_log_exp_and_others"
TINY = 2.0 ** 24
LN_TINY_HALF = 12.0 * float(np.log(2.0))



class Steps:

    def __init__(self, sem, keys, past=()):
        self.sem, self.keys, self.past = sem, list(keys), set(past)
        self.at = {k: n + 1 for n, k in enumerate(self.keys)}
        self.n = len(self.keys)
        assert len(self.at) == self.n
        self.sent = 0

    def prime(self, eng, but=0):
        if self.n > but:
            eng.sem_inc(self.sem, self.n - but)
        self.sent = self.n - but

    def value(self, it, key):
        return (it + 1) * self.n + self.at[key]

    def before(self, it, key):
        return it * self.n + self.at[key]

    def wait(self, eng, it, key):
        if key not in self.past:
            eng.wait_ge(self.sem, self.value(it, key))

    def wait_before(self, eng, it, key):
        if key not in self.past:
            eng.wait_ge(self.sem, self.before(it, key))

    def done(self, ins, key):
        assert self.keys[self.sent % self.n] == key, (key, self.keys[self.sent % self.n])
        self.sent += 1
        ins.then_inc(self.sem, 1)


def settle(eng, passed):
    eng.sem_inc(passed, 1)


class Ring:

    def __init__(self, filled, slots, banks=BANKS):
        self.steps = Steps(filled, [key for key, _ in slots])
        self.banks = banks
        self.index = {key: n for n, (key, _) in enumerate(slots)}
        self.readers = [r for _, r in slots]

    def bank(self, key):
        return self.index[key] % self.banks

    def take(self, pe, it, key):
        n = self.index[key]
        if n >= self.banks:
            for steps, k in self.readers[n - self.banks]:
                steps.wait(pe, it, k)
        else:
            last = max(m for m in range(len(self.readers)) if m % self.banks == n % self.banks)
            for steps, k in self.readers[last]:
                steps.wait_before(pe, it, k)
        return self.bank(key)

    def full(self, eng, it, key):
        self.steps.wait(eng, it, key)
        return self.bank(key)


class Chain:

    def __init__(self, eng, sem, n, once=False):
        self.eng, self.sem, self.n, self.sent, self.once = eng, sem, n, 0, once

    def link(self, it, ins):
        ins.then_inc(self.sem, 1)
        self.sent += 1
        self.eng.wait_ge(self.sem, self.sent if self.once else it * self.n + self.sent)

    def end(self):
        assert self.sent == self.n, self.sent
        self.sent = 0


def units_of(heads):
    return [(h, i) for h in range(heads) for i in range(T)]


TURN_LAG, PV_LAG = 5, 7
PROBS, PROBTS = 7, 3
SUMS = 8


def by_vector(n):
    return n % T == 2


def causal_order(heads):
    units = units_of(heads)
    for n in range(len(units) + PV_LAG):
        if n < len(units):
            yield "score", n
        if n - TURN_LAG in range(len(units)):
            yield "turn", n - TURN_LAG
        if n >= PV_LAG:
            yield "pv", n - PV_LAG


SCORE_HEADS = [(0, 3), (3, 6), (6, 9), (9, 12), (12, 14), (14, 16)]


NEXT_AT = 8


def later(n, work):
    for _ in range(n):
        yield
    yield from work


def project(t):
    return [("qk", t, j) for j in range(4)] + [("v", t, j) for j in range(2)]


def turn(t):
    return [("t", t, j) for j in range(4)]


def score(t):
    return [("s", t, g) for g in range(len(SCORE_HEADS))]


def turn_probs(t):
    return [("pt", t, k) for k in range(4)] + ([("pp", t)] if t else [])


def output(t):
    return [("o", t, n) for n in range(2)]


def hidden_chunks():
    return [(a, c) for c in range(3) for a in ("gate", "up")]


def mix(a, b):
    at = [((n + 0.5) / len(x), key) for x in (a, b) for n, key in enumerate(x)]
    return [key for _, key in sorted(at, key=lambda p: p[0])]


BODY = (mix(project(0), turn(3) + turn_probs(2)) + score(3) + output(2)
        + mix(project(1), turn(0) + turn_probs(3)) + score(0) + output(3)
        + mix(project(2), turn(1) + [("y",)] + turn_probs(0)) + [("xt",)] + score(1) + output(0) + [("xn",)]
        + mix(project(3), turn(2) + turn_probs(1)) + score(2)[:3] + hidden_chunks() + score(2)[3:] + output(1) + [("y2",)])
OF_LAST = (turn(3) + turn_probs(2) + score(3) + output(2) + turn_probs(3) + output(3)
           + [("y",), ("xt",), ("xn",)] + hidden_chunks() + [("y2",)])
TRIPS = DEPTH * B


class Shared:

    def __init__(self, nc, ctx):
        def sb(name, shape, dt=F32):
            return ctx.enter_context(nc.sbuf_tensor(name, shape, dt))

        self.ident = sb("ident", [P, P])
        self.identb = sb("identb", [P, P], BF16)
        self.maskc = sb("maskc", [P, P], BF16)
        self.maskw = sb("maskw", [P, WIN + P], BF16)
        self.eps5 = sb("eps5", [P, 1])
        self.epst = sb("epst", [P, 1])
        self.lnt = sb("lnt", [P, 1])
        self.state = sb("state", [P, B + 1, N + 1])
        self.psum = [ctx.enter_context(nc.psum_tensor(f"psum{b}", [P, BANK], F32)) for b in range(BANKS)]


def pass0(nc, io, sh, ctx):
    ident, identb, maskc, state, psum = sh.ident, sh.identb, sh.maskc, sh.state, sh.psum
    eps5, epst = sh.eps5, sh.epst

    def sb(name, shape, dt=F32):
        return ctx.enter_context(nc.sbuf_tensor(name, shape, dt))

    def sem(name):
        return ctx.enter_context(nc.semaphore(name))

    def steps(name, keys):
        return Steps(sem(name), keys)

    GR = H0 + EXPERTS
    maskc_f, maskw_f = sb("maskc_f", [P, P]), sb("maskw_f", [P, WIN + P])
    wq, wk, wv = (sb(n, [P, H0 * E0]) for n in ("wq", "wk", "wv"))
    wo = sb("wo", [P, PAIRS0, D])
    wgr = sb("wgr", [P, GR])
    rmsw, gbias = sb("rmsw", [P, 1]), sb("gbias", [P, EXPERTS])
    w1, w3 = sb("w1", [P, (EXPERTS + 1) * INTER]), sb("w3", [P, (EXPERTS + 1) * INTER])
    w2 = sb("w2", [P, CH0 + 1, D])
    sel = sb("sel", [EXPERTS, CH0, P])
    tie16, tie4 = sb("tie16", [P, EXPERTS, EXPERTS]), sb("tie4", [P, GROUPS, GROUPS])
    headmask = sb("headmask", [P, H1])
    wq1, wk1 = sb("wq1", [P, D]), sb("wk1", [P, D])
    wv1, wo1 = sb("wv1", [P, D]), sb("wo1", [P, D])

    x, xn, tn = (sb(n, [P, T, D]) for n in ("x", "xn", "tn"))
    square = sb("square", [P, T, D])
    stats, mv = sb("stats", [P, T, 6]), sb("mv", [P, T, 2])
    lnv, rstd, ms, lnm, rrms = (sb(n, [P, T]) for n in ("lnv", "rstd", "ms", "lnm", "rrms"))
    xnT, tT = sb("xnT", [P, N]), sb("tT", [P, N])
    egr, sig = sb("egr", [P, T, GR]), sb("sig", [P, T, GR])
    biased, gmax = sb("biased", [P, T, EXPERTS]), sb("gmax", [P, T, GROUPS])
    gt4, eq4 = sb("gt4", [P, T, GROUPS, GROUPS]), sb("eq4", [P, T, GROUPS, GROUPS])
    rank4, keep, pen = (sb(n, [P, T, GROUPS]) for n in ("rank4", "keep", "pen"))
    kept = sb("kept", [P, T, EXPERTS])
    gt16, eq16 = sb("gt16", [P, T, EXPERTS, EXPERTS]), sb("eq16", [P, T, EXPERTS, EXPERTS])
    rank16, comb = sb("rank16", [P, T, EXPERTS]), sb("comb", [P, T, EXPERTS])
    combT = sb("combT", [EXPERTS, N])
    qz = sb("qz", [P, H0, N])
    kT = sb("kT", [P, PAIRS0, N])
    v = sb("v", [P, T, H0 * E0])
    negmax = sb("negmax", [P, SUMS])
    prob, probT = sb("prob", [P, PROBS, N]), sb("probT", [P, PROBTS, N])
    sums, rsum = sb("psums", [P, SUMS]), sb("rsum", [P, SUMS])
    oT = sb("oT", [P, PAIRS0, N])
    act1, prod, hT = sb("act1", [P, 2, N]), sb("prod", [P, 2, N]), sb("hT", [P, CH0 + 1, N])
    x1, x1n, x1T = sb("x1", [P, T, D]), sb("x1n", [P, T, D]), sb("x1T", [P, N])
    qT1, kT1 = sb("qT1", [P, N]), sb("kT1", [P, N])
    qz1 = sb("qz1", [P, HG, N])
    v1z = sb("v1z", [P, T, H1, 32])
    oT1, sumout = sb("oT1", [P, N]), sb("sumout", [P, T, D])

    ua, ub = units_of(H0), units_of(H1)
    units = [("a", n) for n in range(len(ua))] + [("b", n) for n in range(len(ub))]
    const_loaded, const_made, x_loaded, stored = sem("const_loaded"), sem("const_made"), sem("x_loaded"), sem("stored")
    measured = steps("measured", ["var1", "var", "ms"])
    normed = steps("normed", ["x1n", "xn", "tn"])
    maxed = steps("maxed", units)
    turned_v = steps("turned_v", [u for u in units if u[1] % 2 == 0])
    inverted = steps("inverted", units)
    scaled_v = steps("scaled_v", [u for u in units if by_vector(u[1])])
    moved = steps("moved", ["tT", "sig", "comb", "x1", "sum"])
    gated = steps("gated", range(CH0 + 1))
    rooted = steps("rooted", ["rstd1", "rstd", "rrms"])
    copied = steps("copied", ["xnT", "gr"] + [(a, p) for p in range(PAIRS0) for a in "qk"]
                   + [("v", t) for t in range(T)] + [("ot", p) for p in range(PAIRS0)] + ["ct"]
                   + ["x1T", "q1", "k1", "v1", "ot1"])
    spread = steps("spread", range(H1))
    exped = steps("exped", units)
    turned_s = steps("turned_s", [u for u in units if u[1] % 2 == 1])
    silued = steps("silued", range(CH0 + 1))
    scaled = steps("scaled0", [u for u in units if not by_vector(u[1])])
    outs = steps("outs", [("a", p) for p in range(PAIRS0)] + [("b", 0)])
    link, rlink, passed = sem("link"), sem("rlink"), sem("passed")
    first_link, first_rlink = sem("first_link"), sem("first_rlink")

    def causal_slots(tag, heads):
        for what, n in causal_order(heads):
            if what == "score":
                yield (tag + "s", n), [(exped, (tag, n))]
            elif what == "turn":
                yield (tag + "pt", n), [(turned_v if n % 2 == 0 else turned_s, (tag, n))]

    slots = [("xt", [(copied, "xnT")]), ("tt", [(moved, "tT")]), ("gr", [(copied, "gr")])]
    slots += [((a, p), [(copied, (a, p))]) for p in range(PAIRS0) for a in "qk"]
    slots += [(("v", t), [(copied, ("v", t))]) for t in range(T)]
    slots += list(causal_slots("a", H0))
    slots += [("ct", [(copied, "ct")])]
    for c in range(CH0):
        slots += [(("h1", c), [(silued, c)]), (("h3", c), [(gated, c)]), (("cb", c), [(gated, c)])]
    slots += [(("h1", CH0), [(silued, CH0)]), (("h3", CH0), [(gated, CH0)])]
    slots += [("y", [(moved, "x1")]), ("x1t", [(copied, "x1T")])]
    slots += [(a, [(copied, a)]) for a in ("q1", "k1", "v1")]
    slots += list(causal_slots("b", H1))
    slots += [("y1", [(moved, "sum")])]
    ring = Ring(sem("filled"), slots, BANKS - 2)
    out_bank = lambda tag, p: BANKS - 2 + (p % 2 if tag == "a" else 0)
    out_before = {("a", 2): ("ot", 0), ("a", 3): ("ot", 1), ("b", 0): ("ot", 2)}
    out_before_it = {("a", 0): "ot1", ("a", 1): ("ot", 3)}

    def chunk(c):
        return P if c < CH0 else INTER

    loads = [(ident, "ident"), (maskc_f, "maskc"), (maskw_f, "maskw"), (wq, "wq0"), (wk, "wk0"), (wv, "wv0"),
             (wo, "wo0"), (rmsw, "rmsw"), (w1, "w1"), (w3, "w3"), (sel, "sel"), (headmask, "headmask"), (wq1, "wq1"), (wk1, "wk1"),
             (wv1, "wv1"), (wo1, "wo1")]
    ALL_LOADED = 16 * (len(loads) + 7)
    ALL_MADE = 9

    with nc.Block() as block:
        @block.sync
        def _(sp):
            for dst, name in loads:
                sp.dma_start(dst[tuple(slice(None) for _ in dst.shape)], io[name]).then_inc(const_loaded, 16)
            sp.dma_start(wgr[:, 0:H0], io["wgates"]).then_inc(const_loaded, 16)
            sp.dma_start(wgr[:, H0:GR], io["wroute"]).then_inc(const_loaded, 16)
            sp.dma_start(gbias[:, :], io["gbias"].partition_broadcast(P)).then_inc(const_loaded, 16)
            sp.dma_start(tie16[:, :, :], io["tie16"].partition_broadcast(P)).then_inc(const_loaded, 16)
            sp.dma_start(tie4[:, :, :], io["tie4"].partition_broadcast(P)).then_inc(const_loaded, 16)
            sp.dma_start(w2[:, 0:CH0, :], io["w2"]).then_inc(const_loaded, 16)
            sp.dma_start(w2[0:INTER, CH0, :], io["ws2"]).then_inc(const_loaded, 16)
            def load_x(one):
                sp.dma_start(x[:, :, :], io["x"][one].rearrange("s (t p) d -> p (s t) d", p=P)).then_inc(x_loaded, 16)

            load_x(slice(0, 1))
            sp.sem_inc(stored, 16)
            with sp.Fori(0, B) as it:
                moved.wait(sp, it, "x1")
                settle(sp, passed)
                load_x(bass.ds((it + 1) % B, 1))
                moved.wait(sp, it, "sum")
                settle(sp, passed)
                sp.dma_start(io["sums"][bass.ds(it, 1)].rearrange("s (t p) d -> p (s t) d", p=P), sumout[:, :, :]
                             ).then_inc(stored, 16)
            sp.wait_ge(stored, 16 * B + 16)

        @block.gpsimd
        def _(pool):
            for dst, value in ((eps5[:, :], 1e-5), (epst[:, :], float(np.finfo(np.float32).eps)),
                               (sh.lnt[:, :], LN_TINY_HALF), (qz[:, :, :], 0.0),
                               (v1z[:, :, :, :], 0.0), (state[:, :, :], 0.0)):
                nc.gpsimd.memset(dst, value).then_inc(const_made, 1)
            pool.wait_ge(const_loaded, ALL_LOADED)
            nc.gpsimd.tensor_copy(identb[:, :], ident[:, :]).then_inc(const_made, 1)
            nc.gpsimd.tensor_copy(maskc[:, :], maskc_f[:, :]).then_inc(const_made, 1)
            nc.gpsimd.tensor_copy(sh.maskw[:, :], maskw_f[:, :]).then_inc(const_made, 1)
            scaled.prime(pool)

            def causal(it, tag, heads):
                for n, (h, i) in enumerate(units_of(heads)):
                    if by_vector(n):
                        continue
                    p = prob[:, n % PROBS, 0:(i + 1) * P]
                    inverted.wait(pool, it, (tag, n))
                    settle(pool, passed)
                    r = rsum[:, n % SUMS:n % SUMS + 1]
                    if tag == "a":
                        ins = nc.gpsimd.tensor_scalar(p, p, r, sig[:, i, h:h + 1], ALU.mult, ALU.mult)
                    else:
                        ins = nc.gpsimd.tensor_scalar(p, p, r, None, ALU.mult)
                    scaled.done(ins, (tag, n))

            with pool.Fori(0, B) as it:
                moved.wait(pool, it, "sig")
                causal(it, "a", H0)
                causal(it, "b", H1)

        @block.tensor
        def _(pe):
            ring.steps.prime(pe)
            outs.prime(pe)
            pe.wait_ge(const_loaded, ALL_LOADED)
            pe.wait_ge(const_made, ALL_MADE)

            def take(it, key):
                return psum[ring.take(pe, it, key)]

            def turn4(it, key, src):
                ps = take(it, key)
                for t in range(T):
                    last = nc.tensor.transpose(ps[:, t * P:(t + 1) * P], src(t), ident[:, :])
                ring.steps.done(last, key)

            def product(it, key, lhsT, rhs, m=P):
                ps = take(it, key)
                ring.steps.done(nc.tensor.matmul(ps[0:m, :], lhsT, rhs, start=True, stop=True), key)

            def causal(it, tag, heads, q_of, k_of, v_of):
                for what, n in causal_order(heads):
                    h, i = divmod(n, T)
                    nk = (i + 1) * P
                    if what == "score":
                        if tag == "b" and i == 0:
                            spread.wait(pe, it, h)
                        ps = take(it, (tag + "s", n))
                        nc.tensor.matmul(ps[:, 0:nk], q_of(h, i), k_of(h, nk), start=True, stop=False)
                        ring.steps.done(nc.tensor.matmul(ps[:, i * P:nk], identb[:, :], maskc[:, :],
                                                         start=False, stop=True), (tag + "s", n))
                    elif what == "turn":
                        (scaled_v if by_vector(n) else scaled).wait(pe, it, (tag, n))
                        ps = take(it, (tag + "pt", n))
                        for j in range(i + 1):
                            last = nc.tensor.transpose(ps[:, j * P:(j + 1) * P], prob[:, n % PROBS, j * P:(j + 1) * P],
                                                       ident[:, :])
                        ring.steps.done(last, (tag + "pt", n))
                    else:
                        group, p = h // HG, h // 2 if tag == "a" else 0
                        rows = slice(64 * (h % 2), 64 * (h % 2) + 64) if tag == "a" else slice(32 * group, 32 * group + 32)
                        if i == 0 and (h % 2 == 0 if tag == "a" else h == 0):
                            if (tag, p) in out_before:
                                copied.wait(pe, it, out_before[tag, p])
                            else:
                                copied.wait_before(pe, it, out_before_it[tag, p])
                        first = i == 0 and (tag == "a" or h % HG == 0)
                        ps = psum[out_bank(tag, p)]
                        (turned_v if n % 2 == 0 else turned_s).wait(pe, it, (tag, n))
                        for j in range(i + 1):
                            last = nc.tensor.matmul(ps[rows, i * P:(i + 1) * P], v_of(h, j), probT[:, n % PROBTS, j * P:(j + 1) * P],
                                                    start=(first and j == 0), stop=(j == i), skip_group_check=True)
                        if i == T - 1 and (h % 2 == 1 if tag == "a" else h == heads - 1):
                            outs.done(last, (tag, p))

            with pe.Fori(0, B) as it:
                normed.wait_before(pe, it, "xn")
                turn4(it, "xt", lambda t: xn[:, t, :])
                normed.wait_before(pe, it, "tn")
                turn4(it, "tt", lambda t: tn[:, t, :])
                copied.wait(pe, it, "xnT")
                moved.wait(pe, it, "tT")
                ps = take(it, "gr")
                for t in range(T):
                    nc.tensor.matmul(ps[:, t * GR:t * GR + H0], tT[:, t * P:(t + 1) * P], wgr[:, 0:H0],
                                     start=True, stop=True)
                    last = nc.tensor.matmul(ps[:, t * GR + H0:(t + 1) * GR], xnT[:, t * P:(t + 1) * P], wgr[:, H0:GR],
                                            start=True, stop=True)
                ring.steps.done(last, "gr")
                for p in range(PAIRS0):
                    product(it, ("q", p), wq[:, p * P:(p + 1) * P], tT[:, :])
                    product(it, ("k", p), wk[:, p * P:(p + 1) * P], tT[:, :])
                for t in range(T):
                    product(it, ("v", t), tT[:, t * P:(t + 1) * P], wv[:, :])
                copied.wait(pe, it, ("v", T - 1))
                causal(it, "a", H0,
                       lambda h, i: qz[:, h, i * P:(i + 1) * P],
                       lambda h, nk: kT[:, h // 2, 0:nk],
                       lambda h, j: v[:, j, h * E0:(h + 1) * E0])
                moved.wait(pe, it, "comb")
                ps = take(it, "ct")
                for t in range(T):
                    last = nc.tensor.transpose(ps[0:EXPERTS, t * P:(t + 1) * P], comb[:, t, :], ident[:, :])
                ring.steps.done(last, "ct")
                copied.wait(pe, it, "ct")
                for c in range(CH0 + 1):
                    m = chunk(c)
                    product(it, ("h1", c), w1[:, c * P:c * P + m], xnT[:, :], m)
                    product(it, ("h3", c), w3[:, c * P:c * P + m], xnT[:, :], m)
                    if c < CH0:
                        product(it, ("cb", c), sel[:, c, :], combT[:, :])
                ps = take(it, "y")
                copied.wait(pe, it, ("ot", PAIRS0 - 1))
                gated.wait(pe, it, CH0)
                for t in range(T):
                    yt = ps[:, t * D:(t + 1) * D]
                    for p in range(PAIRS0):
                        nc.tensor.matmul(yt, oT[:, p, t * P:(t + 1) * P], wo[:, p, :], start=(p == 0), stop=False)
                    for c in range(CH0 + 1):
                        m = chunk(c)
                        last = nc.tensor.matmul(yt, hT[0:m, c, t * P:(t + 1) * P], w2[0:m, c, :],
                                                start=False, stop=(c == CH0))
                ring.steps.done(last, "y")
                normed.wait(pe, it, "x1n")
                turn4(it, "x1t", lambda t: x1n[:, t, :])
                copied.wait(pe, it, "x1T")
                product(it, "q1", wq1[:, :], x1T[:, :])
                product(it, "k1", wk1[:, :], x1T[:, :])
                ps = take(it, "v1")
                for t in range(T):
                    last = nc.tensor.matmul(ps[:, t * D:(t + 1) * D], x1T[:, t * P:(t + 1) * P], wv1[:, :],
                                            start=True, stop=True)
                ring.steps.done(last, "v1")
                copied.wait(pe, it, "v1")
                causal(it, "b", H1,
                       lambda h, i: qz1[:, h % HG, i * P:(i + 1) * P],
                       lambda h, nk: kT1[:, 0:nk],
                       lambda h, j: v1z[:, j, h, :])
                copied.wait(pe, it, "ot1")
                ps = take(it, "y1")
                for t in range(T):
                    last = nc.tensor.matmul(ps[:, t * D:(t + 1) * D], oT1[:, t * P:(t + 1) * P], wo1[:, :],
                                            start=True, stop=True)
                ring.steps.done(last, "y1")

        @block.scalar
        def _(act):
            rooted.prime(act, 2)
            for s in (copied, spread, exped, turned_s, silued):
                s.prime(act)
            act.wait_ge(const_loaded, ALL_LOADED)
            act.wait_ge(const_made, ALL_MADE)
            chain, first = Chain(act, rlink, 3), Chain(act, first_rlink, 2, once=True)

            def full(it, key):
                return psum[ring.full(act, it, key)]

            def rsqrt(chain, it, key, out, tmp, src, scale, eps):
                chain.link(it, nc.scalar.activation(tmp, src, ACT.Ln, bias=eps[:, 0:1], scale=scale))
                rooted.done(nc.scalar.activation(out, tmp, ACT.Exp, scale=-0.5), key)

            def copy(it, key, dst, src=None, scale=1.0):
                ps = full(it, key)
                copied.done(nc.scalar.activation(dst, ps[:, :] if src is None else src(ps), ACT.Copy, scale=scale),
                            key if key not in names else names[key])

            names = {"xt": "xnT", "x1t": "x1T"}

            def next_rstd(chain, it):
                measured.wait(act, it, "var")
                rsqrt(chain, it, "rstd", rstd[:, :], lnv[:, :], mv[:, :, 1], 1.0, eps5)

            def next_rrms(chain, it):
                measured.wait(act, it, "ms")
                rsqrt(chain, it, "rrms", rrms[:, :], lnm[:, :], ms[:, :], 1.0 / D, epst)

            def spread_head(it, h):
                spread.done(nc.scalar.activation(qz1[:, h % HG, :], qT1[:, :], ACT.Copy, scale=headmask[:, h:h + 1]), h)

            def causal(it, tag, heads):
                us = units_of(heads)
                for n in range(len(us) + PV_LAG + 2):
                    if n < len(us):
                        nk = (us[n][1] + 1) * P
                        maxed.wait(act, it, (tag, n))
                        exped.done(nc.scalar.activation(prob[:, n % PROBS, 0:nk], full(it, (tag + "s", n))[:, 0:nk], ACT.Exp,
                                                        bias=negmax[:, n % SUMS:n % SUMS + 1],
                                                        accum_out=sums[:, n % SUMS:n % SUMS + 1]), (tag, n))
                    if tag == "b" and n == NEXT_AT + 3:
                        next_rstd(chain, it)
                    if tag == "b" and n == NEXT_AT + 9:
                        next_rrms(chain, it)
                    m = n - TURN_LAG
                    if m in range(len(us)) and m % 2 == 1:
                        nk = (us[m][1] + 1) * P
                        turned_s.done(nc.scalar.copy(probT[:, m % PROBTS, 0:nk],
                                                     full(it, (tag + "pt", m))[:, 0:nk]), (tag, m))
                    if tag == "b" and n % T == 1 and n // T + 3 in range(HG, heads):
                        spread_head(it, n // T + 3)
                    m = n - PV_LAG - 1
                    if tag == "a" and m >= 0 and m % (2 * T) == 2 * T - 1 and m < len(us):
                        p = m // (2 * T)
                        outs.wait(act, it, ("a", p))
                        copied.done(nc.scalar.copy(oT[:, p, :], psum[out_bank("a", p)][:, :]), ("ot", p))

            nc.scalar.preload_act_table_set(LN_EXP)
            next_rstd(first, -1)
            next_rrms(first, -1)
            first.end()
            with act.Fori(0, B) as it:
                copy(it, "xt", xnT[:, :])
                ps = full(it, "gr")
                copied.done(nc.scalar.activation(egr[:, :, :], ps[:, 0:T * GR].rearrange("p (t c) -> p t c", t=T),
                                                 ACT.Exp, scale=-1.0), "gr")
                for p in range(PAIRS0):
                    ps = full(it, ("q", p))
                    nc.scalar.activation(qz[0:E0, 2 * p, :], ps[0:E0, :], ACT.Copy, scale=float(E0) ** -0.5)
                    copied.done(nc.scalar.activation(qz[E0:P, 2 * p + 1, :], ps[E0:P, :], ACT.Copy,
                                                     scale=float(E0) ** -0.5), ("q", p))
                    copy(it, ("k", p), kT[:, p, :])
                for t in range(T):
                    copy(it, ("v", t), v[:, t, :])
                causal(it, "a", H0)
                copy(it, "ct", combT[:, :], lambda ps: ps[0:EXPERTS, :])
                for c in range(CH0 + 1):
                    m = chunk(c)
                    if c >= 2:
                        gated.wait(act, it, c - 2)
                    silued.done(nc.scalar.activation(act1[0:m, c % 2, :], full(it, ("h1", c))[0:m, :], ACT.Silu), c)
                nc.scalar.preload_act_table_set(LN_EXP)
                measured.wait(act, it, "var1")
                rsqrt(chain, it, "rstd1", rstd[:, :], lnv[:, :], mv[:, :, 1], 1.0, eps5)
                copy(it, "x1t", x1T[:, :])
                copy(it, "q1", qT1[:, :], scale=float(E1) ** -0.5)
                copied.wait(act, it, "q1")
                copy(it, "k1", kT1[:, :])
                ps = full(it, "v1")[:, :].rearrange("p (t g r e) -> p t g r e", t=T, g=HG, r=HG)
                for r in range(HG):
                    last = nc.scalar.copy(v1z[:, :, :, :].rearrange("p t (g r) c -> p t g r c", r=HG)
                                          [:, :, :, r, r * E1:(r + 1) * E1], ps[:, :, :, r, :])
                copied.done(last, "v1")
                for h in range(HG):
                    spread_head(it, h)
                causal(it, "b", H1)
                outs.wait(act, it, ("b", 0))
                copied.done(nc.scalar.copy(oT1[:, :], psum[out_bank("b", 0)][:, :]), "ot1")
                chain.end()

        @block.vector
        def _(dve):
            measured.prime(dve, 2)
            normed.prime(dve, 2)
            for s in (maxed, turned_v, inverted, scaled_v, moved, gated):
                s.prime(dve)
            dve.wait_ge(const_loaded, ALL_LOADED)
            dve.wait_ge(const_made, ALL_MADE)
            chain, first = Chain(dve, link, LINKS0), Chain(dve, first_link, 1, once=True)
            V = nc.vector

            def full(it, key):
                return psum[ring.full(dve, it, key)]

            def moments(chain, it, src, key):
                for t in range(T):
                    last = V.bn_stats(stats[:, t, :], src[:, t, :])
                chain.link(it, last)
                settle(dve, passed)
                for t in range(T):
                    last = V.bn_aggr(mv[:, t, :], stats[:, t, :])
                measured.done(last, key)

            def normalize(it, dst, src, key, root, norm):
                measured.wait(dve, it, key)
                rooted.wait(dve, it, root)
                for t in range(T):
                    last = V.tensor_scalar(dst[:, t, :], src[:, t, :], mv[:, t, 0:1], rstd[:, t:t + 1],
                                           ALU.subtract, ALU.mult)
                normed.done(last, norm)
                normed.wait(dve, it, norm)

            def rank(it, values, gt, eq, tie, out, n):
                other = values.unsqueeze(2).to_broadcast([P, T, n, n])
                own = values.unsqueeze(3).to_broadcast([P, T, n, n])
                V.tensor_tensor(gt[:, :, :, :], other, own, ALU.is_gt)
                yield
                chain.link(it, V.tensor_tensor(eq[:, :, :, :], other, own, ALU.is_equal))
                yield
                chain.link(it, V.tensor_tensor(eq[:, :, :, :], eq[:, :, :, :],
                                               tie[:, :, :].unsqueeze(1).to_broadcast([P, T, n, n]), ALU.mult))
                yield
                chain.link(it, V.tensor_tensor(gt[:, :, :, :], gt[:, :, :, :], eq[:, :, :, :], ALU.add))
                yield
                chain.link(it, V.tensor_reduce(out[:, :, :], gt[:, :, :, :], AX.X, ALU.add))

            def gates(it):
                copied.wait(dve, it, "gr")
                chain.link(it, V.tensor_scalar(sig[:, :, :], egr[:, :, :], 1.0, None, ALU.add))
                moved.done(V.reciprocal(sig[:, :, :], sig[:, :, :]), "sig")

            def route(it):
                score = sig[:, :, H0:GR]
                chain.link(it, V.tensor_tensor(biased[:, :, :], score,
                                               gbias[:, :].unsqueeze(1).to_broadcast([P, T, EXPERTS]), ALU.add))
                chain.link(it, V.tensor_reduce(gmax[:, :, :], biased[:, :, :].rearrange("p t (g e) -> p t g e", g=GROUPS),
                                               AX.X, ALU.max))
                yield
                yield from rank(it, gmax[:, :, :], gt4, eq4, tie4, rank4, GROUPS)
                chain.link(it, V.tensor_scalar(keep[:, :, :], rank4[:, :, :], float(TOPG), None, ALU.is_lt))
                chain.link(it, V.tensor_scalar(pen[:, :, :], keep[:, :, :], -NEG, NEG, ALU.mult, ALU.add))
                yield
                groups = [P, T * GROUPS, EXPERTS // GROUPS]
                wide = lambda a: a[:, :, :].rearrange("p t g -> p (t g)").unsqueeze(2).to_broadcast(groups)
                by_group = lambda a: a[:, :, :].rearrange("p t (g e) -> p (t g) e", g=GROUPS)
                chain.link(it, V.tensor_tensor(by_group(kept), by_group(biased), wide(keep), ALU.mult))
                chain.link(it, V.tensor_tensor(by_group(kept), by_group(kept), wide(pen), ALU.add))
                yield
                yield from rank(it, kept[:, :, :], gt16, eq16, tie16, rank16, EXPERTS)
                chain.link(it, V.tensor_scalar(rank16[:, :, :], rank16[:, :, :], float(TOPK), None, ALU.is_lt))
                moved.done(V.tensor_tensor(comb[:, :, :], rank16[:, :, :], score, ALU.mult), "comb")

            def causal(it, tag, heads, other_work):
                us = units_of(heads)
                for n in range(len(us) + PV_LAG):
                    if n < len(us):
                        nk = (us[n][1] + 1) * P
                        maxed.done(V.tensor_reduce(negmax[:, n % SUMS:n % SUMS + 1], full(it, (tag + "s", n))[:, 0:nk],
                                                   AX.X, ALU.max, negate=True), (tag, n))
                    m = n - 2
                    if m in range(len(us)):
                        exped.wait(dve, it, (tag, m))
                        r = rsum[:, m % SUMS:m % SUMS + 1]
                        inverted.done(V.reciprocal(r, sums[:, m % SUMS:m % SUMS + 1]), (tag, m))
                        if by_vector(m):
                            h, i = us[m]
                            p = prob[:, m % PROBS, 0:(i + 1) * P]
                            inverted.wait(dve, it, (tag, m))
                            if tag == "a":
                                ins = V.tensor_scalar(p, p, r, sig[:, i, h:h + 1], ALU.mult, ALU.mult)
                            else:
                                ins = V.tensor_scalar(p, p, r, None, ALU.mult)
                            scaled_v.done(ins, (tag, m))
                    m = n - TURN_LAG
                    if m in range(len(us)) and m % 2 == 0:
                        nk = (us[m][1] + 1) * P
                        turned_v.done(V.tensor_copy(probT[:, m % PROBTS, 0:nk],
                                                    full(it, (tag + "pt", m))[:, 0:nk]), (tag, m))
                    if tag == "b" or n % 2:
                        next(other_work, None)
                for _ in other_work:
                    pass

            def normalize_next(chain, it):
                dve.wait_ge(x_loaded, (it + 2) * 16)
                moments(chain, it, x, "var")
                yield
                for _ in range(5):
                    yield
                if chain is not first:
                    ring.steps.wait(dve, it, "tt")
                normalize(it, xn, x, "var", "rstd", "xn")
                yield
                for t in range(T):
                    last = V.tensor_tensor_reduce(square[:, t, :], xn[:, t, :], xn[:, t, :], 1.0, 0.0, ALU.mult, ALU.add,
                                                  ms[:, t:t + 1])
                measured.done(last, "ms")
                for _ in range(5):
                    yield
                rooted.wait(dve, it, "rrms")
                for t in range(T):
                    last = V.tensor_scalar(tn[:, t, :], xn[:, t, :], rrms[:, t:t + 1], None, ALU.mult)
                normed.done(last, "tn")

            for _ in normalize_next(first, -1):
                pass
            first.end()
            with dve.Fori(0, B) as it:
                moved.done(V.tensor_scalar(tT[:, :], full(it, "tt")[:, :], rmsw[:, 0:1], None, ALU.mult), "tT")
                gates(it)
                moved.wait(dve, it, "sig")
                causal(it, "a", H0, route(it))
                for c in range(CH0 + 1):
                    m = chunk(c)
                    silued.wait(dve, it, c)
                    ps = full(it, ("h3", c))
                    if c < CH0:
                        chain.link(it, V.tensor_tensor(prod[:, c % 2, :], ps[:, :], act1[:, c % 2, :], ALU.mult))
                        gated.done(V.tensor_tensor(hT[:, c, :], full(it, ("cb", c))[:, :], prod[:, c % 2, :], ALU.mult), c)
                    else:
                        gated.done(V.tensor_tensor(hT[0:m, c, :], ps[0:m, :], act1[0:m, c % 2, :], ALU.mult), c)
                moved.done(V.tensor_tensor(x1[:, :, :], full(it, "y")[:, :].rearrange("p (t d) -> p t d", t=T), x[:, :, :],
                                           ALU.add), "x1")
                moved.wait(dve, it, "x1")
                moments(chain, it, x1, "var1")
                normalize(it, x1n, x1, "var1", "rstd1", "x1n")
                copied.wait(dve, it, "x1T")
                V.tensor_copy(state[0:D // 2, bass.ds(it, 1), 0:N].rearrange("p s n -> p (s n)"), x1T[0:D // 2, :])
                V.tensor_copy(state[D // 2:D, bass.ds(it, 1), 1:N + 1].rearrange("p s n -> p (s n)"), x1T[D // 2:D, :])
                causal(it, "b", H1, later(NEXT_AT, normalize_next(chain, it)))
                ps = full(it, "y1")
                dve.wait_ge(stored, it * 16 + 16)
                moved.done(V.tensor_tensor(sumout[:, :, :], ps[:, :].rearrange("p (t d) -> p t d", t=T), x1[:, :, :],
                                           ALU.add), "sum")
                chain.end()


def pass1(nc, io, sh, ctx):
    buf = Buffers(nc, ctx)
    transformer(nc, io, sh, buf, ctx, BODY)
    transformer(nc, io, sh, buf, ctx, OF_LAST)


WK = WIN + P


class Buffers:

    def __init__(self, nc, ctx):
        def sb(name, shape, dt=F32):
            return ctx.enter_context(nc.sbuf_tensor(name, shape, dt))

        self.wqkv, self.wol = sb("wqkv", [P, 3 * INNER]), sb("wol", [P, PAIRSL, D])
        self.w1l, self.w2l = sb("w1l", [P, 2 * DI]), sb("w2l", [P, 3, D])
        self.b1l = sb("b1l", [P, 2, 3])
        self.lng, self.lnb, self.b2l = sb("lng", [P, 1]), sb("lnb", [P, 1]), sb("b2l", [P, 1])
        self.qks = sb("qks", [P, 2, EL])
        self.rot = sb("rot", [P, 4, T, EL])
        self.rots = sb("rots", [P, 4, T, EL])

        self.xw = sb("xw", [P, N + 1])
        self.xm = sb("xm", [P, N + 1])
        self.sq = sb("sq", [P, 2, BANK])
        self.ss, self.ssc = sb("ss", [P, 2 * HL]), sb("ssc", [P, 2, 2 * HL])
        self.lns, self.rn = sb("lns", [P, 2 * HL]), sb("rn", [P, 2, 2 * HL])
        self.cosd, self.sind = sb("cosd", [P, 2, 4, BANK]), sb("sind", [P, 2, 4, BANK])
        self.qk = sb("qk", [P, 4, BANK])
        self.qzl = sb("qzl", [P, 2, HL, P])
        self.kTl = sb("kTl", [P, PAIRSL, N])
        self.vl = sb("vl", [P, T, INNER])
        self.negmaxl = sb("negmaxl", [P, 2, HL])
        self.probl = sb("probl", [P, 2, HL, WK])
        self.pT = sb("pT", [P, HL, P])
        self.pP = sb("pP", [P, HL, WIN])
        self.suml, self.rs = sb("suml", [P, 2, HL]), sb("rs", [P, 2, HL])
        self.oTl = sb("oTl", [P, PAIRSL, N])
        self.stats, self.mv = sb("statsl", [P, T, 6]), sb("mvl", [P, T, 2])
        self.lnv, self.rstd = sb("lnvl", [P, T]), sb("rstdl", [P, T])
        self.x2, self.x2T = sb("x2", [P, T, D]), sb("x2T", [P, N])
        self.gel, self.hf = sb("gel", [P, 2, N]), sb("hf", [P, 3, N])
        self.qkv_loaded, self.o_loaded, self.ffn_loaded, self.rot_loaded, self.made = (
            ctx.enter_context(nc.semaphore(n)) for n in ("qkv_loaded", "o_loaded", "ffn_loaded", "rot_loaded", "made"))


def transformer(nc, io, sh, buf, ctx, order):
    last_part = order is OF_LAST
    ident, identb, maskw, state, psum = sh.ident, sh.identb, sh.maskw, sh.state, sh.psum

    wqkv, wol, w1l, w2l, b1l, lng, lnb, b2l = buf.wqkv, buf.wol, buf.w1l, buf.w2l, buf.b1l, buf.lng, buf.lnb, buf.b2l
    qks, rot, rots, xw, xm, sq, ss, ssc = buf.qks, buf.rot, buf.rots, buf.xw, buf.xm, buf.sq, buf.ss, buf.ssc
    lns, rn, cosd, sind, qk, qzl, kTl, vl = buf.lns, buf.rn, buf.cosd, buf.sind, buf.qk, buf.qzl, buf.kTl, buf.vl
    negmaxl, probl, pT, pP, suml, rs, oTl, stats = buf.negmaxl, buf.probl, buf.pT, buf.pP, buf.suml, buf.rs, buf.oTl, buf.stats
    mv, lnv, rstd, x2, x2T, gel, hf, qkv_loaded = buf.mv, buf.lnv, buf.rstd, buf.x2, buf.x2T, buf.gel, buf.hf, buf.qkv_loaded
    o_loaded, ffn_loaded, rot_loaded, made = buf.o_loaded, buf.ffn_loaded, buf.rot_loaded, buf.made

    def sem(name):
        return ctx.enter_context(nc.semaphore(name + ("_tail" if last_part else "")))

    def steps(name, step_of):
        found = lambda keys: [x for x in map(step_of, keys) if x is not None]
        keys = found(order)
        return Steps(sem(name), keys, set(found(BODY)) - set(keys))

    def place(*kinds, only=lambda where: True):
        return lambda key: key[1:] if key[0] in kinds and only(key[1:]) else None

    def last_of(kind, step):
        return lambda key: step if key[0] == kind else None

    pieces = [(t, j) for t in range(T) for j in range(4)]
    fetched = steps("fetched", lambda key: "xw" if key == ("v", T - 1, 1) else None)
    scaled = sem("scaled")
    summed_rot = steps("summed_rot", place("qk"))
    rotated = Steps(sem("rotated"), [] if last_part else pieces, pieces if last_part else ())
    weighed = steps("weighed", place("s"))
    parts = steps("parts", place("qk"))
    summed = steps("summed", place("qk"))
    clamped = steps("clamped", lambda key: key[1] if key[0] == "v" and key[2] == 0 else None)
    maxed = steps("maxedl", place("s"))
    turned_v = steps("turned_vl", place("pt", only=lambda where: where[1] % 2 == 0))
    inverted = steps("invertedl", place("s"))
    mid = steps("mid", last_of("y", "xm"))
    ffn = Steps(sem("ffn"), ["var", "x2", "x2T"])
    hidden = steps("hidden", lambda key: key[1] if key[0] == "up" else None)
    left = steps("left", last_of("y2", "state"))
    squared = steps("squared", place("qk"))
    vcopied = steps("vcopied", place("v"))
    rooted = steps("rootedl", lambda key: "ffn" if key[0] == "xt" else key[1] if key[0] == "v" and key[2] == 1 else None)
    tcopied = steps("tcopied", place("t"))
    exped = steps("expedl", place("s"))
    turned_s = steps("turned_sl", lambda key: (key[1], "pp") if key[0] == "pp" else
                     key[1:] if key[0] == "pt" and key[2] % 2 else None)
    ocopied = steps("ocopied", place("o"))
    gelued = steps("gelued", lambda key: key[1] if key[0] == "gate" else None)
    link, rlink, passed = sem("linkl"), sem("rlinkl"), sem("passedl")

    def readers(key):
        kind, at = key[0], key[1:]
        if kind == "qk":
            return [(squared, at)]
        if kind == "v":
            return [(vcopied, at)]
        if kind == "t":
            return [(tcopied, at)]
        if kind == "s":
            return [(exped, at)]
        if kind == "pt":
            return [(turned_s if at[1] % 2 else turned_v, at)]
        if kind == "pp":
            return [(turned_s, (at[0], "pp"))]
        if kind == "o":
            return [(ocopied, at)]
        if kind == "y":
            return [(mid, "xm")]
        if kind == "xt":
            return [(ffn, "x2")]
        if kind == "xn":
            return [(ffn, "x2T")]
        if kind == "gate":
            return [(gelued, at[0])]
        if kind == "up":
            return [(hidden, at[0])]
        return [(left, "state")]

    ring = Ring(sem("filledl"), [(key, readers(key)) for key in order])

    def wait_made(steps, eng, it, key, before):
        (steps.wait_before if before else steps.wait)(eng, it, key)

    rest_at = lambda l, s: bass.ds((s + B - 1) % B + 1 - (l * B + s + TRIPS - 1) // TRIPS, 1)
    rest_loads = lambda l, s: (l * B + s + B - 1) // B + 1

    def keys0(t):
        return (t * P - WIN, 0) if t else (0, WIN)

    with nc.Block() as block:
        @block.sync
        def _(sp):
            def load_output(layer):
                sp.dma_start(wol[:, :, :], io["wol"][layer].rearrange("l (c p) d -> p (l c) d", p=P)).then_inc(o_loaded, 16)

            def load_ffn(layer):
                sp.dma_start(w1l[:, :], io["w1l"][layer].rearrange("l p n -> p (l n)")).then_inc(ffn_loaded, 16)
                for dst, name in ((lng, "lng"), (lnb, "lnb"), (b2l, "b2l")):
                    sp.dma_start(dst[:, :], io[name][layer].rearrange("l p -> p l")).then_inc(ffn_loaded, 16)
                at = 0
                for c, m in enumerate(CW):
                    sp.dma_start(w2l[0:m, c, :], io["w2l"][layer][:, at:at + m, :].rearrange("l p d -> p (l d)")
                                 ).then_inc(ffn_loaded, 16)
                    for a in range(2):
                        sp.dma_start(b1l[0:m, a, c:c + 1], io["b1l"][layer][:, a * DI + at:a * DI + at + m]
                                     .rearrange("l p -> p l")).then_inc(ffn_loaded, 16)
                    at += m

            if last_part:
                return
            sp.dma_start(rot[:, :, :, :], io["rot"]).then_inc(rot_loaded, 16)
            load_output(slice(0, 1))
            load_ffn(slice(0, 1))
            with sp.Fori(0, DEPTH) as l:
                it = l * B
                one = bass.ds(l, 1)
                ring.steps.wait_before(sp, it, ("v", T - 1, 1))
                settle(sp, passed)
                sp.dma_start(wqkv[:, :], io["wqkv"][one].rearrange("l p n -> p (l n)")).then_inc(qkv_loaded, 16)
                sp.wait_ge(scaled, l * 4 + 4)
                settle(sp, passed)
                sp.dma_start(qks[:, 0, :], io["qs"][one].to_broadcast([P, EL])).then_inc(qkv_loaded, 16)
                sp.dma_start(qks[:, 1, :], io["ks"][one].to_broadcast([P, EL])).then_inc(qkv_loaded, 16)
                ring.steps.wait(sp, it, ("y",))
                settle(sp, passed)
                load_output(one)
                left.wait(sp, it, "state")
                settle(sp, passed)
                load_ffn(one)

        FFN_LOADS = 4 + 3 * 3

        @block.gpsimd
        def _(pool):
            for s in (summed_rot, rotated, weighed):
                s.prime(pool)
            pool.sem_inc(scaled, 4)
            def work(it, s, key):
                kind, at = key[0], key[1:]
                if kind == "qk":
                    t, j = at
                    parts.wait(pool, it, at)
                    summed_rot.done(nc.gpsimd.tensor_tensor(cosd[:, t % 2, j, :], cosd[:, t % 2, j, :],
                                                            sind[:, t % 2, j, :], ALU.add), at)
                elif kind == "v" and at[1] == 1:
                    t = at[0]
                    rooted.wait(pool, it, t)
                    for j in range(4):
                        ring.steps.wait(pool, it, ("t", (t - 1) % T, j))
                        summed_rot.wait(pool, it, (t, j))
                        rotated.done(nc.gpsimd.tensor_tensor(
                            qk[:, j, :].rearrange("p (h c) -> p h c", c=EL),
                            cosd[:, t % 2, j, :].rearrange("p (h c) -> p h c", c=EL),
                            rn[:, t % 2, 8 * j:8 * j + 8].unsqueeze(2).to_broadcast([P, 8, EL]), ALU.mult), (t, j))
                    if t == T - 1:
                        left.wait_before(pool, it, "state")
                        ring.steps.wait(pool, it, key)
                        settle(pool, passed)
                        fetched.done(nc.gpsimd.tensor_copy(
                            xw[:, :], state[:, bass.ds((s + 1) % B, 1), :].rearrange("p s n -> p (s n)")), "xw")
                elif kind == "s":
                    t, g = at
                    a, b = SCORE_HEADS[g]
                    _, c0 = keys0(t)
                    inverted.wait(pool, it, at)
                    p = probl[:, t % 2, a:b, c0:WK]
                    weighed.done(nc.gpsimd.tensor_tensor(
                        p, p, rs[:, t % 2, a:b].unsqueeze(2).to_broadcast([P, b - a, WK - c0]), ALU.mult), at)

            if last_part:
                for key in order:
                    work(0, 0, key)
                return
            for dst in (qzl[:, :, :, :], xm[:, :], qk[:, :, :], kTl[:, :, :], probl[:, :, :, :], vl[:, :, :], oTl[:, :, :]):
                nc.gpsimd.memset(dst, 0.0).then_inc(made, 1)
            nc.gpsimd.tensor_copy(xw[:, :], state[:, 0, :]).then_inc(fetched.sem, 1)
            pool.wait_ge(rot_loaded, 16)
            with pool.Fori(0, DEPTH) as l:
                pool.wait_ge(qkv_loaded, l * 48 + 48)
                parts.wait_before(pool, l * B, pieces[-1])
                for a in range(2):
                    scale = qks[:, a, :].rearrange("p (two c) -> p two c", two=2)
                    for b, own in ((2 * a, scale), (2 * a + 1, scale[:, ::-1, :])):
                        nc.gpsimd.tensor_tensor(
                            rots[:, b, :, :].rearrange("p t (two c) -> p t two c", two=2),
                            rot[:, b, :, :].rearrange("p t (two c) -> p t two c", two=2),
                            own.unsqueeze(1).to_broadcast([P, T, 2, EL // 2]), ALU.mult).then_inc(scaled, 1)
                with pool.Fori(0, B) as s:
                    it = l * B + s
                    for key in order:
                        work(it, s, key)

        @block.tensor
        def _(pe):
            ring.steps.prime(pe)
            pe.wait_ge(made, 7)

            def fill(it, l, s, key):
                ps = psum[ring.take(pe, it, key)]
                kind, at = key[0], key[1:]
                t = at[0] if at else 0
                if kind in ("qk", "v"):
                    col = (4 if kind == "v" else 0) * BANK + at[1] * BANK
                    last = nc.tensor.matmul(ps[:, :], xw[:, t * P:(t + 1) * P], wqkv[:, col:col + BANK],
                                            start=True, stop=True)
                elif kind == "t":
                    wait_made(rotated, pe, it, at, t == T - 1)
                    for c in range(4):
                        last = nc.tensor.transpose(ps[:, c * P:(c + 1) * P], qk[:, at[1], c * P:(c + 1) * P], ident[:, :])
                elif kind == "s":
                    if at[1] == 0:
                        tcopied.wait(pe, it, (t, 3))
                    heads = range(*SCORE_HEADS[at[1]])
                    k0, c0 = keys0(t)
                    blocks = ps[:, 0:len(heads) * WK].rearrange("p (h k) -> p h k", k=WK)
                    nc.tensor.matmul(blocks[:, :, c0:WK], identb[:, :],
                                     maskw[:, c0:WK].unsqueeze(1).to_broadcast([P, len(heads), WK - c0]),
                                     start=True, stop=False, skip_group_check=True)
                    for n, h in enumerate(heads):
                        last = nc.tensor.matmul(blocks[:, n, c0:WK], qzl[:, t % 2, h, :],
                                                kTl[:, h // 2, k0:(t + 1) * P],
                                                start=False, stop=(n == len(heads) - 1), skip_group_check=True)
                elif kind == "pt":
                    wait_made(weighed, pe, it, (t, next(g for g, (a, b) in enumerate(SCORE_HEADS) if b >= 4 * at[1] + 4)), t == 2)
                    for c in range(4):
                        last = nc.tensor.transpose(ps[:, c * P:(c + 1) * P], probl[:, t % 2, 4 * at[1] + c, WIN:WK], ident[:, :])
                elif kind == "pp":
                    settle(pe, passed)
                    for h in range(HL):
                        last = nc.tensor.transpose(ps[0:WIN, h * WIN:(h + 1) * WIN], probl[0:WIN, t % 2, h, 0:WIN],
                                                   ident[0:WIN, 0:WIN])
                elif kind == "o":
                    if at[1] == 0:
                        turned_v.wait(pe, it, (t, 2))
                        turned_s.wait(pe, it, (t, "pp" if t else 3))
                        wait_made(vcopied, pe, it, (t, 1), t >= 2)
                    for n, h in enumerate(range(8 * at[1], 8 * at[1] + 8)):
                        half, col = slice(64 * (h % 2), 64 * (h % 2) + 64), n // 2 * P
                        last = nc.tensor.matmul(ps[half, col:col + P], vl[:, t, h * EL:(h + 1) * EL], pT[:, h, :],
                                                start=(n < 2), stop=(t == 0), skip_group_check=True)
                    for n, h in enumerate(range(8 * at[1], 8 * at[1] + 8) if t else ()):
                        half, col = slice(64 * (h % 2), 64 * (h % 2) + 64), n // 2 * P
                        last = nc.tensor.matmul(ps[half, col:col + WIN], vl[P - WIN:P, t - 1, h * EL:(h + 1) * EL],
                                                pP[P - WIN:P, h, :], start=False, stop=True, skip_group_check=True,
                                                tile_position=(P - WIN, 64 * (h % 2)))
                elif kind == "y":
                    pe.wait_ge(o_loaded, rest_loads(l, s) * 16)
                    ocopied.wait(pe, it, (T - 1, 1))
                    for c in range(PAIRSL):
                        last = nc.tensor.matmul(ps[:, :], wol[:, c, :], oTl[:, c, :],
                                                start=(c == 0), stop=(c == PAIRSL - 1))
                elif kind == "xt":
                    pe.wait_ge(ffn_loaded, rest_loads(l, s) * (16 * FFN_LOADS))
                    mid.wait(pe, it, "xm")
                    for c in range(T):
                        last = nc.tensor.transpose(ps[:, c * P:(c + 1) * P], xm[:, c * P:(c + 1) * P], ident[:, :])
                elif kind == "xn":
                    ffn.wait(pe, it, "x2")
                    for c in range(T):
                        last = nc.tensor.transpose(ps[:, c * P:(c + 1) * P], x2[:, c, :], ident[:, :])
                elif kind in ("gate", "up"):
                    if key == ("gate", 0):
                        ffn.wait(pe, it, "x2T")
                    col = (DI if kind == "gate" else 0) + sum(CW[:t])
                    last = nc.tensor.matmul(ps[0:CW[t], :], w1l[:, col:col + CW[t]], x2T[:, :], start=True, stop=True)
                else:
                    hidden.wait(pe, it, 2)
                    for c, m in enumerate(CW):
                        last = nc.tensor.matmul(ps[:, :], w2l[0:m, c, :], hf[0:m, c, :], start=(c == 0), stop=(c == 2))
                ring.steps.done(last, key)

            if last_part:
                for key in order:
                    fill(0, DEPTH, 0, key)
                return
            with pe.Fori(0, DEPTH) as l:
                with pe.Fori(0, B) as s:
                    it = l * B + s
                    pe.wait_ge(qkv_loaded, l * 48 + 48)
                    fetched.wait_before(pe, it, "xw")
                    for key in order:
                        fill(it, l, s, key)

        @block.scalar
        def _(act):
            for s in (squared, vcopied, rooted, tcopied, exped, turned_s, ocopied, gelued):
                s.prime(act)
            act.wait_ge(made, 7)
            chain = Chain(act, rlink, 1 if last_part else T + 1)
            nc.scalar.preload_act_table_set(LN_EXP)

            def read(it, l, s, key):
                kind, at = key[0], key[1:]
                t = at[0] if at else 0
                if kind in ("up", "y2", "y", "xn") or (kind == "pt" and at[1] % 2 == 0):
                    return
                ps = psum[ring.full(act, it, key)]
                if kind == "qk":
                    parts.wait(act, it, at)
                    n = 4 * t + at[1]
                    if n >= 2:
                        summed.wait(act, it, pieces[n - 2])
                    else:
                        summed.wait_before(act, it, pieces[n - 2])
                    squared.done(nc.scalar.activation(sq[:, n % 2, :], ps[:, :], ACT.Square), at)
                elif kind == "v":
                    vcopied.done(nc.scalar.copy(vl[:, t, BANK * at[1]:BANK * (at[1] + 1)], ps[:, :]), at)
                    if at[1] == 1:
                        clamped.wait(act, it, t)
                        chain.link(it, nc.scalar.activation(lns[:, :], ssc[:, t % 2, :], ACT.Ln))
                        rooted.done(nc.scalar.activation(rn[:, t % 2, :], lns[:, :], ACT.Exp, scale=-0.5,
                                                         bias=sh.lnt[:, 0:1]), t)
                elif kind == "t":
                    src = ps[:, :].rearrange("p (c n) -> p c n", n=P)
                    if at[1] < 2:
                        dst = qzl[:, t % 2, 8 * at[1]:8 * at[1] + 8, :].rearrange("p (c two) n -> p c two n", two=2)
                        nc.scalar.copy(dst[0:EL, :, 0, :], src[0:EL, :, :])
                        last = nc.scalar.copy(dst[EL:P, :, 1, :], src[EL:P, :, :])
                    else:
                        last = nc.scalar.copy(kTl[:, 4 * at[1] - 8:4 * at[1] - 4, t * P:(t + 1) * P], src)
                    tcopied.done(last, at)
                elif kind == "s":
                    maxed.wait(act, it, at)
                    _, c0 = keys0(t)
                    for n, h in enumerate(range(*SCORE_HEADS[at[1]])):
                        last = nc.scalar.activation(probl[:, t % 2, h, c0:WK], ps[:, n * WK + c0:(n + 1) * WK], ACT.Exp,
                                                    bias=negmaxl[:, t % 2, h:h + 1], accum_out=suml[:, t % 2, h:h + 1])
                    exped.done(last, at)
                elif kind == "pt":
                    turned_s.done(nc.scalar.copy(pT[:, 4 * at[1]:4 * at[1] + 4, :], ps[:, :].rearrange("p (h n) -> p h n", n=P)), at)
                elif kind == "pp":
                    turned_s.done(nc.scalar.copy(pP[P - WIN:P, :, :], ps[0:WIN, :].rearrange("p (h n) -> p h n", n=WIN)), (t, "pp"))
                elif kind == "o":
                    ocopied.done(nc.scalar.copy(oTl[:, 4 * at[1]:4 * at[1] + 4, t * P:(t + 1) * P],
                                                ps[:, :].rearrange("p (c n) -> p c n", n=P)), at)
                elif kind == "xt":
                    ffn.wait(act, it, "var")
                    chain.link(it, nc.scalar.activation(lnv[:, :], mv[:, :, 1], ACT.Ln, bias=sh.eps5[:, 0:1]))
                    rooted.done(nc.scalar.activation(rstd[:, :], lnv[:, :], ACT.Exp, scale=-0.5), "ffn")
                elif kind == "gate":
                    if t == 0:
                        act.wait_ge(ffn_loaded, rest_loads(l, s) * (16 * FFN_LOADS))
                    if t == 2:
                        hidden.wait(act, it, 0)
                    m = CW[t]
                    gelued.done(nc.scalar.activation(gel[0:m, t % 2, :], ps[0:m, :], ACT.Gelu, bias=b1l[0:m, 1, t:t + 1]), t)
                    if t == 2:
                        nc.scalar.preload_act_table_set(LN_EXP)

            if last_part:
                for key in order:
                    read(0, DEPTH, 0, key)
                chain.end()
                return
            with act.Fori(0, DEPTH) as l:
                with act.Fori(0, B) as s:
                    it = l * B + s
                    for key in order:
                        read(it, l, s, key)
                    chain.end()

        @block.vector
        def _(dve):
            for s in (parts, summed, clamped, maxed, turned_v, inverted, mid, ffn, hidden, left):
                s.prime(dve)
            dve.wait_ge(made, 7)
            V = nc.vector
            chain = Chain(dve, link, LINKS1)
            HALF = D // 2

            def unshift(ins_of, it_rows=((0, HALF, 0), (HALF, D, 1))):
                for a, b, d in it_rows:
                    last = ins_of(a, b, d)
                return last

            def sum_squares(it, piece):
                squared.wait(dve, it, piece)
                j = piece[1]
                summed.done(V.tensor_reduce(ss[:, 8 * j:8 * j + 8], sq[:, j % 2, :].rearrange("p (h c) -> p h c", c=EL),
                                            AX.X, ALU.add), piece)

            def invert(it, t, g):
                a, b = SCORE_HEADS[g]
                exped.wait(dve, it, (t, g))
                inverted.done(V.reciprocal(rs[:, t % 2, a:b], suml[:, t % 2, a:b]), (t, g))

            def read(it, l, s, key):
                kind, at = key[0], key[1:]
                t = at[0] if at else 0
                if kind == "v" and at[1] == 0:
                    sum_squares(it, (t, 3))
                    summed.wait(dve, it, (t, 3))
                    clamped.done(V.tensor_scalar(ssc[:, t % 2, :], ss[:, :], 1e-24, TINY, ALU.max, ALU.mult), t)
                if kind in ("v", "t", "pp", "o", "gate") or (kind == "pt" and at[1] % 2):
                    return
                ps = psum[ring.full(dve, it, key)]
                if kind == "qk":
                    j = at[1]
                    if t >= 2:
                        rotated.wait(dve, it, (t - 2, j))
                    else:
                        rotated.wait_before(dve, it, (t + 2, j))
                    table = 2 * (j // 2)
                    heads = ps[:, :].rearrange("p (h two c) -> p h two c", two=2, c=EL // 2)
                    by_head = lambda a: a.rearrange("p (h c) -> p h c", c=EL)
                    wide = lambda a: a.unsqueeze(1).to_broadcast([P, 8, EL])
                    V.tensor_tensor(by_head(cosd[:, t % 2, j, :]), by_head(ps[:, :]), wide(rots[:, table, t, :]), ALU.mult)
                    halves = lambda a: a.rearrange("p h (two c) -> p h two c", two=2)
                    parts.done(V.tensor_tensor(halves(by_head(sind[:, t % 2, j, :])), heads[:, :, ::-1, :],
                                               halves(wide(rots[:, table + 1, t, :])), ALU.mult), at)
                    if j:
                        sum_squares(it, (t, j - 1))
                elif kind == "s":
                    _, c0 = keys0(t)
                    a, b = SCORE_HEADS[at[1]]
                    nh = b - a
                    blocks = ps[:, 0:nh * WK].rearrange("p (h k) -> p h k", k=WK)
                    maxed.done(V.tensor_reduce(negmaxl[:, t % 2, a:b], blocks[:, :, c0:WK], AX.X, ALU.max, negate=True), at)
                    if at[1]:
                        invert(it, t, at[1] - 1)
                    if at[1] == len(SCORE_HEADS) - 1:
                        invert(it, t, at[1])
                elif kind == "pt":
                    turned_v.done(V.tensor_copy(pT[:, 4 * at[1]:4 * at[1] + 4, :], ps[:, :].rearrange("p (h n) -> p h n", n=P)), at)
                elif kind == "y":
                    mid.done(unshift(lambda a, b, d: V.tensor_tensor(
                        xm[a:b, d:N + d], ps[a:b, :], state[a:b, rest_at(l, s), d:N + d].rearrange("p s n -> p (s n)"),
                        ALU.add)), "xm")
                elif kind == "xt":
                    for c in range(T):
                        last = V.bn_stats(stats[:, c, :], ps[:, c * P:(c + 1) * P])
                    chain.link(it, last)
                    settle(dve, passed)
                    for c in range(T):
                        last = V.bn_aggr(mv[:, c, :], stats[:, c, :])
                    ffn.done(last, "var")
                    ffn.wait(dve, it, "var")
                    rooted.wait(dve, it, "ffn")
                    for c in range(T):
                        last = V.tensor_scalar(x2[:, c, :], ps[:, c * P:(c + 1) * P], mv[:, c, 0:1], rstd[:, c:c + 1],
                                               ALU.subtract, ALU.mult)
                    ffn.done(last, "x2")
                elif kind == "xn":
                    dve.wait_ge(ffn_loaded, rest_loads(l, s) * (16 * FFN_LOADS))
                    ffn.done(V.tensor_scalar(x2T[:, :], ps[:, :], lng[:, 0:1], lnb[:, 0:1], ALU.mult, ALU.add), "x2T")
                elif kind == "up":
                    m = CW[t]
                    gelued.wait(dve, it, t)
                    hidden.done(V.scalar_tensor_tensor(out=hf[0:m, t, :], in0=ps[0:m, :], scalar=b1l[0:m, 0, t:t + 1],
                                                       in1=gel[0:m, t % 2, :], op0=ALU.add, op1=ALU.mult), t)
                else:
                    last = unshift(lambda a, b, d: V.scalar_tensor_tensor(
                        out=state[a:b, rest_at(l, s), d:N + d].rearrange("p s n -> p (s n)"), in0=ps[a:b, :],
                        scalar=b2l[a:b, 0:1], in1=xm[a:b, d:N + d], op0=ALU.add, op1=ALU.add))
                    left.done(last, "state")

            if last_part:
                for key in order:
                    read(0, DEPTH, 0, key)
                chain.end()
                return
            with dve.Fori(0, DEPTH) as l:
                with dve.Fori(0, B) as s:
                    it = l * B + s
                    dve.wait_ge(scaled, l * 4 + 8)
                    for key in order:
                        read(it, l, s, key)
                    chain.end()


def pass2(nc, io, sh, ctx):
    ident, state, psum = sh.ident, sh.state, sh.psum

    def sb(name, shape, dt=F32):
        return ctx.enter_context(nc.sbuf_tensor(name, shape, dt))

    def sem(name):
        return ctx.enter_context(nc.semaphore(name))

    xf, sums, out = sb("xf", [P, N]), sb("sums_in", [P, T, D]), sb("outs", [P, T, D])
    straight, turned, added, loaded, stored, passed = (sem(n) for n in ("straight", "turned", "added", "loaded",
                                                                         "stored2", "passed2"))
    tokens = "s (t p) d -> p (s t) d"
    with nc.Block() as block:
        @block.sync
        def _(sp):
            sp.sem_inc(stored, 16)
            with sp.Fori(0, B) as s:
                sp.wait_ge(added, s + 1)
                settle(sp, passed)
                sp.dma_start(sums[:, :, :], io["sums"][bass.ds(s, 1)].rearrange(tokens, p=P)).then_inc(loaded, 16)
                sp.wait_ge(added, s + 2)
                settle(sp, passed)
                sp.dma_start(io["out"][bass.ds(s, 1)].rearrange(tokens, p=P), out[:, :, :]).then_inc(stored, 16)
            sp.wait_ge(stored, 16 * B + 16)

        @block.scalar
        def _(act):
            with act.Fori(0, B) as s:
                act.wait_ge(turned, s + 1)
                one = bass.ds(s, 1)
                nc.scalar.copy(xf[0:D // 2, :], state[0:D // 2, one, 0:N].rearrange("p s n -> p (s n)"))
                nc.scalar.copy(xf[D // 2:D, :], state[D // 2:D, one, 1:N + 1].rearrange("p s n -> p (s n)")
                               ).then_inc(straight, 1)

        @block.tensor
        def _(pe):
            pe.sem_inc(turned, 1)
            with pe.Fori(0, B) as s:
                pe.wait_ge(straight, s + 1)
                pe.wait_ge(added, s + 1)
                for t in range(T):
                    last = nc.tensor.transpose(psum[0][:, t * P:(t + 1) * P], xf[:, t * P:(t + 1) * P], ident[:, :])
                last.then_inc(turned, 1)

        @block.vector
        def _(dve):
            dve.sem_inc(added, 1)
            with dve.Fori(0, B) as s:
                dve.wait_ge(turned, s + 2)
                dve.wait_ge(loaded, s * 16 + 16)
                dve.wait_ge(stored, s * 16 + 16)
                nc.vector.tensor_tensor(out[:, :, :], psum[0][:, :].rearrange("p (t d) -> p t d", t=T), sums[:, :, :],
                                        ALU.add).then_inc(added, 1)


LINKS0 = 26
LINKS1 = 1


def build(nc, io):
    with ExitStack() as ctx:
        sh = Shared(nc, ctx)
        with ExitStack() as inner:
            pass0(nc, io, sh, inner)
        with ExitStack() as inner:
            pass1(nc, io, sh, inner)
        with ExitStack() as inner:
            pass2(nc, io, sh, inner)


def rotary():
    f = np.float32
    half = np.arange(0, EL, 2, dtype=f)
    inv_freq = (f(1.0) / f(10000.0) ** (half / f(EL))).astype(f)
    tok = np.arange(N, dtype=f)
    freqs = tok[:, None] * inv_freq[None, :]
    freqs = np.concatenate([freqs, freqs], -1).astype(np.float64)
    base = ((half + f(0.4 * EL)) / f(1.4 * EL)).astype(np.float64)
    power = (tok - N // 2) / (WIN // 2)
    scale = base[None, :] ** power[:, None].astype(np.float64)
    scale = np.concatenate([scale, scale], -1)
    cos, sin = np.cos(freqs), np.sin(freqs)
    sin[:, :EL // 2] *= -1
    tables = np.stack([QK_SCALE * cos * scale, QK_SCALE * sin * scale, cos / scale, sin / scale])
    return np.ascontiguousarray(tables.reshape(4, T, P, EL).transpose(2, 0, 1, 3).astype(f))


def masks():
    q, k = np.arange(P)[:, None], np.arange(P)[None, :]
    causal = np.where(k <= q, 0.0, NEG)
    r = np.arange(WIN + P)[None, :] - WIN
    window = np.where((r <= q) & (q <= r + WIN), 0.0, NEG)
    return causal.astype(np.float32), window.astype(np.float32)


def kernel(**inputs):
    from concourse import bacc
    from concourse.bass_utils import run_bass_kernel_spmd

    a = {k: np.asarray(v) for k, v in inputs.items()}
    f = np.float32
    causal, window = masks()
    pick = np.zeros((EXPERTS, CH0, P), f)
    for e in range(EXPERTS):
        pick[e, e // 2, (e % 2) * INTER:(e % 2 + 1) * INTER] = 1.0
    earlier = lambda n: np.tril(np.ones((n, n), f), -1)

    flat = lambda w: w.transpose(1, 0, 2).reshape(D, H0 * E0)
    up = lambda w, shared: np.concatenate([w.reshape(EXPERTS * INTER, D), shared], 0).T
    arrays = {
        "ident": np.eye(P, dtype=f), "maskc": causal, "maskw": window, "sel": pick,
        "tie16": earlier(EXPERTS), "tie4": earlier(GROUPS), "rot": rotary(),
        "x": a["L0_attn_tokens"],
        "wq0": flat(a["L0_attn_wq"]), "wk0": flat(a["L0_attn_wk"]), "wv0": flat(a["L0_attn_wv"]),
        "wo0": a["L0_attn_wo"].reshape(PAIRS0, P, D).transpose(1, 0, 2),
        "wgates": a["L0_attn_w_gates"], "wroute": a["L0_ffn_gate_w"].T,
        "rmsw": a["L0_attn_rms_w"].reshape(D, 1), "gbias": a["L0_ffn_gate_bias"],
        "w1": up(a["L0_ffn_w1"], a["L0_ffn_ws1"]), "w3": up(a["L0_ffn_w3"], a["L0_ffn_ws3"]),
        "w2": a["L0_ffn_w2"].transpose(0, 2, 1).reshape(CH0, P, D).transpose(1, 0, 2), "ws2": a["L0_ffn_ws2"].T,
        "wq1": a["L1_attn_Wq"].T, "wk1": a["L1_attn_Wk"].T, "headmask": np.repeat(np.eye(H1, dtype=f), E1, axis=0),
        "wv1": a["L1_attn_Wv"].T, "wo1": a["L1_attn_Wo"].T,
        "wqkv": a["L1_ffn_Wqkv"], "qs": a["L1_ffn_q_scale"], "ks": a["L1_ffn_k_scale"], "wol": a["L1_ffn_Wo"],
        "lng": a["L1_ffn_ln_g"], "lnb": a["L1_ffn_ln_b"], "w1l": a["L1_ffn_W1"], "b1l": a["L1_ffn_b1"],
        "w2l": a["L1_ffn_W2"], "b2l": a["L1_ffn_b2"],
    }
    arrays = {f"in_{k}": np.ascontiguousarray(v) for k, v in arrays.items()}
    nc = bacc.Bacc("TRN2", target_bir_lowering=False, num_devices=1)
    io = {k[3:]: nc.dram_tensor(k, v.shape, mybir.dt.from_np(v.dtype), kind="ExternalInput").ap()
          for k, v in arrays.items()}
    io["out"] = nc.dram_tensor("out", (B, N, D), F32, kind="ExternalOutput").ap()
    io["sums"] = nc.dram_tensor("sums", (B, N, D), F32, kind="Internal").ap()
    build(nc, io)
    r = run_bass_kernel_spmd(nc, [arrays], core_ids=[0])
    return r.results[0]["out"]
```
